# Optimizing a Trainium2 kernel written in Bass

```python
import numpy as np
import jax
import jax.numpy as jnp

def _softmax(x, axis=-1):
    return jax.nn.softmax(x, axis=axis)

def _gelu(x):
    return jax.nn.gelu(x, approximate=True)

def _silu(x):
    return jax.nn.silu(x)

def _sigmoid(x):
    return jax.nn.sigmoid(x)

def _layernorm(x, axis=-1, eps=1e-05):
    m = jnp.mean(x, axis=axis, keepdims=True)
    v = jnp.var(x, axis=axis, keepdims=True)
    return (x - m) / jnp.sqrt(v + eps)

def _scatter_add(tgt, idx, src, axis=0):
    return tgt.at[idx].add(src)

def _segment_sum(src, seg, n):
    return jax.ops.segment_sum(src, seg, n)
kernel_name = 'mk_adj_resnorm_d4_adj_r2_2f38fe'

def setup_inputs(seed: int=0):
    np.random.seed(seed)
    _w = jnp.asarray

    def _rec_inputs():
        import jax
        import jax.numpy as jnp
        _gk = jax.random.key(seed)
        x = -0.0005207 + 1.001 * jax.random.normal(jax.random.fold_in(_gk, 1), (4096, 128), jnp.float32)
        _w = (1.0 + jnp.arange(4096, dtype=jnp.float32)) ** (-0.5)
        _w = _w / _w.mean()
        _pij = jnp.clip(0.00195312 * _w[:, None] * _w[None, :], 0.0, 1.0)
        _a = jax.random.uniform(jax.random.fold_in(_gk, 2), (4096, 4096)) < _pij
        _a = jnp.logical_or(_a, jnp.eye(4096, dtype=bool))
        _af = _a.astype(jnp.float32)
        _af = _af * jax.random.uniform(jax.random.fold_in(_gk, 3), (4096, 4096), jnp.float32, 0.05, 1)
        adj = _af
        return (x, adj)
    x, adj = _rec_inputs()

    def _L0_gnn_setup():
        import jax, jax.numpy as jnp
        import numpy as np
        N, DIM = (8192, 128)

        def _gru_cell(x, h, W_ih, W_hh, b_ih, b_hh):
            gi = x @ W_ih.T + b_ih
            gh = h @ W_hh.T + b_hh
            i_r, i_z, i_n = jnp.split(gi, 3, axis=-1)
            h_r, h_z, h_n = jnp.split(gh, 3, axis=-1)
            r = jax.nn.sigmoid(i_r + h_r)
            z = jax.nn.sigmoid(i_z + h_z)
            n = jnp.tanh(i_n + r * h_n)
            return (1.0 - z) * n + z * h
        key = jax.random.key(seed)
        ks = jax.random.split(key, 8)
        states = jax.random.normal(ks[0], (N, DIM), dtype=jnp.float32)
        adj = jax.random.uniform(ks[1], (N, N), dtype=jnp.float32)
        s = 1.0 / np.sqrt(DIM)
        W_msg = jax.random.uniform(ks[2], (DIM, DIM), minval=-s, maxval=s, dtype=jnp.float32)
        b_msg = jax.random.uniform(ks[3], (DIM,), minval=-s, maxval=s, dtype=jnp.float32)
        W_ih = jax.random.uniform(ks[4], (3 * DIM, DIM), minval=-s, maxval=s, dtype=jnp.float32)
        W_hh = jax.random.uniform(ks[5], (3 * DIM, DIM), minval=-s, maxval=s, dtype=jnp.float32)
        b_ih = jax.random.uniform(ks[6], (3 * DIM,), minval=-s, maxval=s, dtype=jnp.float32)
        b_hh = jax.random.uniform(ks[7], (3 * DIM,), minval=-s, maxval=s, dtype=jnp.float32)
        return {'states': states, 'adj': adj, 'W_msg': W_msg, 'b_msg': b_msg, 'W_ih': W_ih, 'W_hh': W_hh, 'b_ih': b_ih, 'b_hh': b_hh}
    _L0_gnn_all = _L0_gnn_setup()
    _L0_gnn_in = {k: v for k, v in _L0_gnn_all.items() if k in ('W_msg', 'b_msg', 'W_ih', 'W_hh', 'b_ih', 'b_hh')}
    del _L0_gnn_all

    def _L1_gnn_setup():
        import jax, jax.numpy as jnp
        import numpy as np
        N = 4096
        D_IN = 128
        D_OUT = 128
        key = jax.random.key(seed)
        k1, k2, k3 = jax.random.split(key, 3)
        node_features = jax.random.normal(k1, (N, D_IN), dtype=jnp.float32)
        adj_matrix = jax.random.uniform(k2, (N, N), dtype=jnp.float32)
        limit = float(np.sqrt(6.0 / (D_IN + D_OUT)))
        weight = jax.random.uniform(k3, (D_IN, D_OUT), dtype=jnp.float32, minval=-limit, maxval=limit)
        bias = jnp.zeros((D_OUT,), dtype=jnp.float32)
        return {'node_features': node_features, 'adj_matrix': adj_matrix, 'weight': weight, 'bias': bias}
    _L1_gnn_all = _L1_gnn_setup()
    _L1_gnn_in = {k: v for k, v in _L1_gnn_all.items() if k in ('weight', 'bias')}
    del _L1_gnn_all

    def _L2_gnn_setup():
        import jax, jax.numpy as jnp
        import numpy as np
        N, IN, H, C = (2048, 128, 4, 32)
        HC = H * C
        EDGE_P = 0.008

        def _linear_params(key, fan_in, fan_out, bias=True):
            k1, k2 = jax.random.split(key)
            lim = 1.0 / np.sqrt(fan_in)
            W = jax.random.uniform(k1, (fan_in, fan_out), jnp.float32, -lim, lim)
            if not bias:
                return W
            b = jax.random.uniform(k2, (fan_out,), jnp.float32, -lim, lim)
            return (W, b)

        def _transformer_conv(x, adj, Wq, bq, Wk, bk, Wv, bv, Ws, bs, Wb):
            n = x.shape[0]
            q = (x @ Wq + bq).reshape(n, H, C)
            k = (x @ Wk + bk).reshape(n, H, C)
            v = (x @ Wv + bv).reshape(n, H, C)
            attn = jnp.einsum('nhc,mhc->hnm', q, k) / np.float32(np.sqrt(C))
            mask = adj == 0.0
            neg = jnp.where(mask[None], -jnp.inf, attn)
            m = jnp.max(neg, axis=-1, keepdims=True)
            all_inf = jnp.isneginf(m)
            e = jnp.where(mask[None], 0.0, jnp.exp(neg - jnp.where(all_inf, 0.0, m)))
            denom = jnp.sum(e, axis=-1, keepdims=True)
            alpha = e / jnp.where(denom == 0.0, 1.0, denom)
            out = jnp.einsum('hnm,mhc->hnc', alpha, v)
            out = jnp.transpose(out, (1, 2, 0)).reshape(n, C * H)
            x_r = x @ Ws + bs
            beta = jax.nn.sigmoid(jnp.concatenate([out, x_r, out - x_r], axis=-1) @ Wb)
            return beta * x_r + (1.0 - beta) * out
        key = jax.random.key(seed)
        ks = jax.random.split(key, 7)
        x = jax.random.normal(ks[0], (N, IN), jnp.float32)
        adj = (jax.random.uniform(ks[1], (N, N)) < EDGE_P).astype(jnp.float32)
        Wq, bq = _linear_params(ks[2], IN, HC)
        Wk, bk = _linear_params(ks[3], IN, HC)
        Wv, bv = _linear_params(ks[4], IN, HC)
        Ws, bs = _linear_params(ks[5], IN, HC)
        Wb = _linear_params(ks[6], 3 * HC, 1, bias=False)
        return dict(x=x, adj=adj, Wq=Wq, bq=bq, Wk=Wk, bk=bk, Wv=Wv, bv=bv, Ws=Ws, bs=bs, Wb=Wb)
    _L2_gnn_all = _L2_gnn_setup()
    _L2_gnn_in = {k: v for k, v in _L2_gnn_all.items() if k in ('Wq', 'bq', 'Wk', 'bk', 'Wv', 'bv', 'Ws', 'bs', 'Wb')}
    del _L2_gnn_all

    def _L3_gnn_setup():
        import jax, jax.numpy as jnp
        import numpy as np
        MIN_NORM = 1e-15
        BALL_EPS = 0.004
        C_IN = 1.0
        C_OUT = 1.0

        def _norm(x):
            return jnp.clip(jnp.linalg.norm(x, axis=-1, keepdims=True), MIN_NORM, None)

        def artanh(x):
            return jnp.arctanh(jnp.clip(x, -1.0 + 1e-07, 1.0 - 1e-07))

        def proj(x, c):
            norm = _norm(x)
            maxnorm = (1.0 - BALL_EPS) / jnp.sqrt(c)
            return jnp.where(norm > maxnorm, x / norm * maxnorm, x)

        def expmap0(u, c):
            sc = jnp.sqrt(c)
            un = _norm(u)
            return jnp.tanh(sc * un) * u / (sc * un)

        def logmap0(p, c):
            sc = jnp.sqrt(c)
            pn = _norm(p)
            return artanh(sc * pn) * p / (sc * pn)

        def mobius_add(x, y, c):
            x2 = jnp.sum(x * x, -1, keepdims=True)
            y2 = jnp.sum(y * y, -1, keepdims=True)
            xy = jnp.sum(x * y, -1, keepdims=True)
            num = (1 + 2 * c * xy + c * y2) * x + (1 - c * x2) * y
            denom = 1 + 2 * c * xy + c * c * x2 * y2
            return num / jnp.clip(denom, MIN_NORM, None)

        def mobius_matvec(m, x, c):
            sc = jnp.sqrt(c)
            xn = _norm(x)
            mx = x @ m.T
            mxn = _norm(mx)
            res = jnp.tanh(mxn / xn * artanh(sc * xn)) * mx / (mxn * sc)
            zero_rows = jnp.all(mx == 0, axis=-1, keepdims=True)
            return jnp.where(zero_rows, jnp.zeros_like(res), res)
        key = jax.random.key(seed)
        k1, k2, k3, k4 = jax.random.split(key, 4)
        N, din, dout = (8192, 128, 128)
        x = jax.random.normal(k1, (N, din), dtype=jnp.float32) * 0.01
        adj = jax.random.uniform(k2, (N, N), dtype=jnp.float32)
        adj = adj / jnp.sum(adj, axis=-1, keepdims=True)
        bound = math_bound = float(np.sqrt(2.0) * np.sqrt(6.0 / (din + dout)))
        weight = jax.random.uniform(k3, (dout, din), dtype=jnp.float32, minval=-bound, maxval=bound)
        bias = jax.random.normal(k4, (dout,), dtype=jnp.float32) * 0.01
        return {'x': x, 'adj': adj, 'weight': weight, 'bias': bias}
    _L3_gnn_all = _L3_gnn_setup()
    _L3_gnn_in = {k: v for k, v in _L3_gnn_all.items() if k in ('weight', 'bias')}
    del _L3_gnn_all
    return {'x': x, 'adj': adj, 'L0_gnn_W_msg': _L0_gnn_in['W_msg'], 'L0_gnn_b_msg': _L0_gnn_in['b_msg'], 'L0_gnn_W_ih': _L0_gnn_in['W_ih'], 'L0_gnn_W_hh': _L0_gnn_in['W_hh'], 'L0_gnn_b_ih': _L0_gnn_in['b_ih'], 'L0_gnn_b_hh': _L0_gnn_in['b_hh'], 'L1_gnn_weight': _L1_gnn_in['weight'], 'L1_gnn_bias': _L1_gnn_in['bias'], 'L2_gnn_Wq': _L2_gnn_in['Wq'], 'L2_gnn_bq': _L2_gnn_in['bq'], 'L2_gnn_Wk': _L2_gnn_in['Wk'], 'L2_gnn_bk': _L2_gnn_in['bk'], 'L2_gnn_Wv': _L2_gnn_in['Wv'], 'L2_gnn_bv': _L2_gnn_in['bv'], 'L2_gnn_Ws': _L2_gnn_in['Ws'], 'L2_gnn_bs': _L2_gnn_in['bs'], 'L2_gnn_Wb': _L2_gnn_in['Wb'], 'L3_gnn_weight': _L3_gnn_in['weight'], 'L3_gnn_bias': _L3_gnn_in['bias']}

def reference(x, adj, L0_gnn_W_msg, L0_gnn_b_msg, L0_gnn_W_ih, L0_gnn_W_hh, L0_gnn_b_ih, L0_gnn_b_hh, L1_gnn_weight, L1_gnn_bias, L2_gnn_Wq, L2_gnn_bq, L2_gnn_Wk, L2_gnn_bk, L2_gnn_Wv, L2_gnn_bv, L2_gnn_Ws, L2_gnn_bs, L2_gnn_Wb, L3_gnn_weight, L3_gnn_bias):
    import jax
    import jax.numpy as jnp

    def _L0_gnn_ref(states, adj, W_msg, b_msg, W_ih, W_hh, b_ih, b_hh):
        import jax, jax.numpy as jnp
        import numpy as np
        N, DIM = (8192, 128)

        def _gru_cell(x, h, W_ih, W_hh, b_ih, b_hh):
            gi = x @ W_ih.T + b_ih
            gh = h @ W_hh.T + b_hh
            i_r, i_z, i_n = jnp.split(gi, 3, axis=-1)
            h_r, h_z, h_n = jnp.split(gh, 3, axis=-1)
            r = jax.nn.sigmoid(i_r + h_r)
            z = jax.nn.sigmoid(i_z + h_z)
            n = jnp.tanh(i_n + r * h_n)
            return (1.0 - z) * n + z * h
        agg = adj @ states
        msg = jax.nn.relu(agg @ W_msg.T + b_msg)
        return _gru_cell(msg, states, W_ih, W_hh, b_ih, b_hh)

    def _L1_gnn_ref(node_features, adj_matrix, weight, bias):
        import jax, jax.numpy as jnp
        import numpy as np
        N = 4096
        D_IN = 128
        D_OUT = 128
        n = adj_matrix.shape[0]
        a_hat = adj_matrix + jnp.eye(n, dtype=adj_matrix.dtype)
        d_hat = jnp.sum(a_hat, axis=1)
        d_inv_sqrt = jnp.where(d_hat > 0, jax.lax.rsqrt(d_hat), 0.0)
        adj_normalized = d_inv_sqrt[:, None] * a_hat * d_inv_sqrt[None, :]
        support = node_features @ weight
        out = adj_normalized @ support + bias
        return out

    def _L2_gnn_ref(x, adj, Wq, bq, Wk, bk, Wv, bv, Ws, bs, Wb):
        import jax, jax.numpy as jnp
        import numpy as np
        N, IN, H, C = (2048, 128, 4, 32)
        HC = H * C
        EDGE_P = 0.008

        def _linear_params(key, fan_in, fan_out, bias=True):
            k1, k2 = jax.random.split(key)
            lim = 1.0 / np.sqrt(fan_in)
            W = jax.random.uniform(k1, (fan_in, fan_out), jnp.float32, -lim, lim)
            if not bias:
                return W
            b = jax.random.uniform(k2, (fan_out,), jnp.float32, -lim, lim)
            return (W, b)

        def _transformer_conv(x, adj, Wq, bq, Wk, bk, Wv, bv, Ws, bs, Wb):
            n = x.shape[0]
            q = (x @ Wq + bq).reshape(n, H, C)
            k = (x @ Wk + bk).reshape(n, H, C)
            v = (x @ Wv + bv).reshape(n, H, C)
            attn = jnp.einsum('nhc,mhc->hnm', q, k) / np.float32(np.sqrt(C))
            mask = adj == 0.0
            neg = jnp.where(mask[None], -jnp.inf, attn)
            m = jnp.max(neg, axis=-1, keepdims=True)
            all_inf = jnp.isneginf(m)
            e = jnp.where(mask[None], 0.0, jnp.exp(neg - jnp.where(all_inf, 0.0, m)))
            denom = jnp.sum(e, axis=-1, keepdims=True)
            alpha = e / jnp.where(denom == 0.0, 1.0, denom)
            out = jnp.einsum('hnm,mhc->hnc', alpha, v)
            out = jnp.transpose(out, (1, 2, 0)).reshape(n, C * H)
            x_r = x @ Ws + bs
            beta = jax.nn.sigmoid(jnp.concatenate([out, x_r, out - x_r], axis=-1) @ Wb)
            return beta * x_r + (1.0 - beta) * out
        return _transformer_conv(x, adj, Wq, bq, Wk, bk, Wv, bv, Ws, bs, Wb)

    def _L3_gnn_ref(x, adj, weight, bias):
        import jax, jax.numpy as jnp
        import numpy as np
        MIN_NORM = 1e-15
        BALL_EPS = 0.004
        C_IN = 1.0
        C_OUT = 1.0

        def _norm(x):
            return jnp.clip(jnp.linalg.norm(x, axis=-1, keepdims=True), MIN_NORM, None)

        def artanh(x):
            return jnp.arctanh(jnp.clip(x, -1.0 + 1e-07, 1.0 - 1e-07))

        def proj(x, c):
            norm = _norm(x)
            maxnorm = (1.0 - BALL_EPS) / jnp.sqrt(c)
            return jnp.where(norm > maxnorm, x / norm * maxnorm, x)

        def expmap0(u, c):
            sc = jnp.sqrt(c)
            un = _norm(u)
            return jnp.tanh(sc * un) * u / (sc * un)

        def logmap0(p, c):
            sc = jnp.sqrt(c)
            pn = _norm(p)
            return artanh(sc * pn) * p / (sc * pn)

        def mobius_add(x, y, c):
            x2 = jnp.sum(x * x, -1, keepdims=True)
            y2 = jnp.sum(y * y, -1, keepdims=True)
            xy = jnp.sum(x * y, -1, keepdims=True)
            num = (1 + 2 * c * xy + c * y2) * x + (1 - c * x2) * y
            denom = 1 + 2 * c * xy + c * c * x2 * y2
            return num / jnp.clip(denom, MIN_NORM, None)

        def mobius_matvec(m, x, c):
            sc = jnp.sqrt(c)
            xn = _norm(x)
            mx = x @ m.T
            mxn = _norm(mx)
            res = jnp.tanh(mxn / xn * artanh(sc * xn)) * mx / (mxn * sc)
            zero_rows = jnp.all(mx == 0, axis=-1, keepdims=True)
            return jnp.where(zero_rows, jnp.zeros_like(res), res)
        mv = mobius_matvec(weight, x, C_IN)
        res = proj(mv, C_IN)
        hyp_bias = proj(expmap0(bias[None, :], C_IN), C_IN)
        h = proj(mobius_add(res, hyp_bias, C_IN), C_IN)
        xt = logmap0(h, C_IN)
        support_t = adj @ xt
        h = proj(expmap0(support_t, C_IN), C_IN)
        xt = jax.nn.relu(logmap0(h, C_IN))
        h = proj(expmap0(xt, C_OUT), C_OUT)
        return h
    x = _layernorm(x + _L0_gnn_ref(x, adj, L0_gnn_W_msg, L0_gnn_b_msg, L0_gnn_W_ih, L0_gnn_W_hh, L0_gnn_b_ih, L0_gnn_b_hh), axis=-1)
    x = _layernorm(x + _L1_gnn_ref(x, adj, L1_gnn_weight, L1_gnn_bias), axis=-1)
    x = _layernorm(x + _L2_gnn_ref(x, adj, L2_gnn_Wq, L2_gnn_bq, L2_gnn_Wk, L2_gnn_bk, L2_gnn_Wv, L2_gnn_bv, L2_gnn_Ws, L2_gnn_bs, L2_gnn_Wb), axis=-1)
    x = _layernorm(x + _L3_gnn_ref(x, adj, L3_gnn_weight, L3_gnn_bias), axis=-1)
    return x

_drawn_inputs = setup_inputs


def setup_inputs(seed=0):
    import zlib

    import numpy as np

    out = dict(_drawn_inputs(seed))
    spreads = {'L1_gnn_bias': (0.0, 0.1)}
    factors = {'L0_gnn_b_msg': 7.326,
     'L0_gnn_b_hh': 4.343,
     'L2_gnn_bq': 8.0,
     'L2_gnn_bk': 8.0,
     'L3_gnn_bias': 8.0}
    for name, (base, spread) in spreads.items():
        noise = np.random.default_rng([zlib.crc32(name.encode()), seed]).standard_normal(out[name].shape)
        drawn = base * np.exp(spread * noise) if base else spread * noise
        out[name] = jnp.asarray(drawn.astype(out[name].dtype))
    for name, factor in factors.items():
        out[name] = (out[name] * factor).astype(out[name].dtype)
    return out
```

```python
from contextlib import ExitStack

import concourse.bass as bass
from concourse import mybir

F32 = mybir.dt.float32
F32R = mybir.dt.float32r
BF16 = mybir.dt.bfloat16
ALU = mybir.AluOpType
ACT = mybir.ActivationFunctionType
AX = mybir.AxisListType

P = 128
N = 4096
CONSTS = 6
WEIGHTS = 19
TILES = N // P
CHUNK = 512
CHUNKS = N // CHUNK
TPC = CHUNK // P
SLOTS = 8
JPS = TILES // SLOTS
H, C = 4, 32
BLOCK = 1024
BLOCKS = N // BLOCK
COLS = TPC * BLOCKS
UPB = BLOCK // P
SCORE_SCALE = 1.0 / float(C) ** 0.5
MASKED = -1.0e30
LOWEST = -1.0e20
LN_EPS = 1e-5
MIN_NORM = 1e-15
MAX_NORM = 1.0 - 0.004
ARTANH_MAX = 1.0 - 1e-7
VECTOR_UNITS = (1, 4, 6)
OUT_AT = 5
X3_AT = (5, 3)
MX_AT = (6, 3)


def is_zero(c):
    return isinstance(c, int) and c == 0


class Steps:

    def __init__(self, *names):
        self.names = names

    def __call__(self, c, name):
        return c * len(self.names) + self.names.index(name) + 1


class TurnBanks:

    BANKS = (4, 5, 6)

    def __init__(self):
        self.uses = []
        for n in range(COLS):
            for u in range(UPB):
                self.uses.append(("unit", n, u))
                if u == OUT_AT and n % BLOCKS == 0:
                    self.uses.append(("out", n))
                if (n, u) == X3_AT:
                    self.uses.append(("x3",))
                if (n, u) == MX_AT:
                    self.uses.append(("mx",))
        while len(self.uses) % len(self.BANKS):
            self.uses.append(None)

    def bank(self, use):
        return self.BANKS[self.uses.index(use) % len(self.BANKS)]

    def before(self, use, first):
        i = self.uses.index(use) - len(self.BANKS)
        while i >= 0:
            if self.uses[i] and not (first and self.uses[i] in (("out", 0), ("x3",), ("mx",))):
                return self.uses[i], 0
            i -= len(self.BANKS)
        if first:
            return None, 0
        i += len(self.uses)
        while not self.uses[i]:
            i -= len(self.BANKS)
        return self.uses[i], 1


TURN_BANKS = TurnBanks()
UNITS = [(n, u) for n in range(COLS) for u in range(UPB)]
BY_VECTOR = [n * UPB + u for n, u in UNITS if u in VECTOR_UNITS]
BY_SCALAR = [n * UPB + u for n, u in UNITS if u not in VECTOR_UNITS]


def build_program(nc, adj_cols, adj, x_tiles, x_t, w_msg, b_msg, w_ih, w_hh, b_ih, b_hh, w_gcn, b_gcn,
                  w_q, b_q, w_k, b_k, w_vs, b_vs, w_beta, w_hyp, b_hyp, out):
    x1_dram = nc.dram_tensor("x1_dram", [P, TILES * P], F32)
    x2_dram = nc.dram_tensor("x2_dram", [P, TILES * P], F32)
    root_dram = nc.dram_tensor("root_dram", [P, TILES * P], F32)
    x3_dram = nc.dram_tensor("x3_dram", [P, TILES * P], F32)
    q4_dram = nc.dram_tensor("q4_dram", [CHUNKS, 4, H, C, CHUNK], F32)
    k4_dram = nc.dram_tensor("k4_dram", [CHUNKS, 4, H, C, CHUNK], F32)

    with ExitStack() as ctx:
        def sb(name, shape, dt=F32):
            return ctx.enter_context(nc.sbuf_tensor(name, shape, dt))

        def sem(name):
            return ctx.enter_context(nc.semaphore(name))

        k4 = sb("k4", [P, H, N], F32R)
        parts = sb("parts", [P, 2, CHUNK], F32R)
        stat_x = sb("stat_x", [P, TILES, P])
        stat_s = sb("stat_s", [P, TILES, P])
        arena = sb("arena", [P, 25600])
        ident = sb("ident", [P, P])
        wgcn = sb("wgcn", [P, P])
        wq = sb("wq", [P, P])
        wk = sb("wk", [P, P])
        wvs = sb("wvs", [P, 2 * P])
        whyp = sb("whyp", [P, P])
        bgcn = sb("bgcn", [P, P])
        bvs = sb("bvs", [P, 2 * P])
        wbo = sb("wbo", [P, P])
        wbr = sb("wbr", [P, P])
        hbias = sb("hbias", [P, P])
        small = sb("small", [P, 340])
        taken = [0]

        def cut(n):
            taken[0] += n
            return small[:, taken[0] - n:taken[0]]

        bmsg, bih, bhh, bq, bk = cut(1), cut(3), cut(3), cut(1), cut(1)
        brz = cut(2)
        ones = cut(1)
        minus_half, half, minus_one = cut(4), cut(4), cut(4)
        dinv = cut(TILES)
        deg = cut(4)
        deg_on = cut(4)
        bn6 = cut(24)
        mean_var = cut(8).rearrange("p (t k) -> p t k", k=2)
        rstd = cut(4)
        hb = cut(4)
        blockmax = cut(32).rearrange("p (b k) -> p b k", b=2)
        shift = cut(32).rearrange("p (b k) -> p b k", b=2)
        blocksum = cut(32).rearrange("p (b k) -> p b k", b=2)
        rowmax, rowsum, noedge, rrow = cut(4), cut(4), cut(4), cut(4)
        mix = cut(16)
        mix2 = cut(16)
        zz, ez, beta = cut(4), cut(4), cut(4)
        xx, mm, mh, hh = cut(4), cut(4), cut(4), cut(4)
        s1, s2, s3, s4, s5, s6, s7 = [cut(4) for _ in range(7)]
        t1, t2, t3 = [cut(4) for _ in range(3)]

        RING = SLOTS * JPS * CHUNK
        ring = arena[:, 0:RING].rearrange("p (s j i) -> p s j i", s=SLOTS, j=JPS)
        stages = [arena[:, RING + i * CHUNK:RING + (i + 1) * CHUNK] for i in range(18)]
        agg_t, msg_t, xt_in, r_t, z_t, n_t, hn_t, y_t, x_new, x_new_t = stages[:10]
        colsum = arena[:, RING + 10 * CHUNK:RING + 12 * CHUNK]
        wih = arena[:, RING + 12 * CHUNK:RING + 12 * CHUNK + 384]
        whh = arena[:, RING + 13 * CHUNK:RING + 13 * CHUNK + 384]
        wmsg = arena[:, RING + 14 * CHUNK:RING + 14 * CHUNK + 128]
        res_in, root_out, y_n = stages[15:18]
        wb3, bias_sq = root_out[:, 0:P], root_out[:, P:2 * P]
        cols = arena[:, 0:4 * H * BLOCK].rearrange("p (s h n) -> p s h n", s=4, h=H)
        at = 4 * H * BLOCK
        turned = arena[:, at:at + 4 * CHUNK].rearrange("p (s n) -> p s n", s=4)
        at += 4 * CHUNK
        adj_in = arena[:, at:at + 2 * BLOCK].rearrange("p (s n) -> p s n", s=2)
        at += 2 * BLOCK
        maskbias = arena[:, at:at + BLOCK].bitcast(BF16).rearrange("p (s n) -> p s n", s=2)
        at += BLOCK
        o_t, wide, o_n, root_g, x2_g, y_g, x3_g, mx_g = [arena[:, at + i * CHUNK:at + (i + 1) * CHUNK]
                                                        for i in range(8)]
        x3_t = wide
        bank = ctx.enter_context(nc.psum_tensor("bank", [P, 8, CHUNK], F32))

        def tiles(ap):
            return ap.rearrange("p (t f) -> p t f", f=P)

        def per_tile(row, n=TPC):
            return row.unsqueeze(1).to_broadcast([P, n, P])

        x_in = sem("x_in")
        weights_in = sem("weights_in")
        consts_set = sem("consts_set")
        bias_dve = sem("bias_dve")
        bias_act = sem("bias_act")
        bias_pool = sem("bias_pool")
        ring_landed = [sem(f"ring_landed{s}") for s in range(SLOTS)]
        ring_multiplied = sem("ring_multiplied")
        ring_summed = sem("ring_summed")
        half_summed = sem("half_summed")
        gru_pe, gru_act, gru_dve, gru_pool = [sem(f"gru_{e}") for e in ("pe", "act", "dve", "pool")]
        gru_xt_in, gru_x1_out = sem("gru_xt_in"), sem("gru_x1_out")
        GP = Steps("degree", "msg", "r", "z", "n_in", "n_hid", "y_turned", "x1_turned", "support")
        GA = Steps("agg", "msg", "r", "z", "n", "x1_t")
        GV = Steps("degree", "deg_on", "hn", "rhn", "npre", "diff", "zdiff", "nz", "y", "bn6", "bn", "x1", "dinv", "scaled")
        GG = Steps("deg_max", "deg_pow", "eps", "rstd")
        gcn_pe, gcn_act, gcn_dve, gcn_pool = [sem(f"gcn_{e}") for e in ("pe", "act", "dve", "pool")]
        gcn_x1_in, gcn_x2_out, gcn_root_out = sem("gcn_x1_in"), sem("gcn_x2_out"), sem("gcn_root_out")
        gcn_k_out, gcn_q_out, gcn_k4_in = sem("gcn_k_out"), sem("gcn_q_out"), sem("gcn_k4_in")
        CP = Steps("turned", "x2_turned", "k", "q", "vs")
        CA = Steps("agg", "x2_t", "k_hi", "q_hi")
        CV = Steps("self", "dinv", "y", "bn6", "bn", "x2", "k_lo", "q_lo", "v", "root")
        CG = Steps("x1_bias", "eps", "rstd")
        adj_landed = [sem(f"adj_landed{s}") for s in range(2)]
        q4_landed = [sem(f"q4_landed{s}") for s in range(2)]
        bias_ready = sem("bias_ready")
        scores_ready = sem("scores_ready")
        masked_ready = sem("masked_ready")
        shift_ready = sem("shift_ready")
        exp_ready = sem("exp_ready")
        unit_turned = sem("unit_turned")
        unit_copied_act = sem("unit_copied_act")
        unit_copied_dve = sem("unit_copied_dve")
        unit_used = sem("unit_used")
        tile_pe, tile_act, tile_dve = sem("tile_pe"), sem("tile_act"), sem("tile_dve")
        TP = Steps("turned")
        TA = Steps("weights", "copied")
        TV = Steps("rowmax", "below", "wsum", "rowsum", "noedge", "guard", "recip", "mix", "wide", "out")
        att_pe, att_act, att_dve, att_pool = [sem(f"att_{e}") for e in ("pe", "act", "dve", "pool")]
        att_in, att_x3_out = sem("att_in"), sem("att_x3_out")
        AP_ = Steps("x3_turned", "mx")
        AA = Steps("ez", "x3_t", "mx", "ln_a", "ln_b", "tanh", "ln_c", "ln_d")
        AV = Steps("zz", "one_ez", "beta", "y", "bn6", "bn", "x3", "xx", "mm", "mh", "scaled_bias", "h", "hh", "xt")
        AG = Steps("zo", "zr", "z", "diff", "sum", "eps", "rstd", "x3sq", "mxsq", "mxhb",
                   "xn", "xn_max", "mn", "mn_max", "xn_min", "a", "a_half", "xn_inv", "arg", "arg2",
                   "g_min", "mn_inv", "g", "g2", "x2", "xy", "xy2", "x2y2", "den", "den_max", "den_inv",
                   "a_num", "a_g", "A", "b_num", "B", "hsq", "hn", "hn_max", "pn", "fa", "fa_half",
                   "hn_inv", "fac")
        hyp_pe, hyp_act, hyp_dve, hyp_pool = [sem(f"hyp_{e}") for e in ("pe", "act", "dve", "pool")]
        hyp_in, hyp_out, hyp_sub = sem("hyp_in"), sem("hyp_out"), sem("hyp_sub")
        HP = Steps("turned")
        HA = Steps("agg", "uu", "tanh", "ln_a", "ln_b", "w", "ww", "tanh2")
        HV = Steps("y", "bn6", "bn", "out")
        HG = Steps("un", "un_max", "p", "un_inv", "fac", "wn", "wn_max", "p2", "wn_inv", "f2", "fh", "eps", "rstd")

        block = ctx.enter_context(nc.Block())

        @block.sync
        def _(sp):
            def load_ring(layer, c, first):
                for s in range(SLOTS):
                    turn = layer * CHUNKS + c
                    if not first:
                        sp.wait_ge(ring_multiplied, (turn - 1) * SLOTS + s + 1)
                        if layer == 0 or is_zero(c):
                            sp.wait_ge(ring_summed, (turn - 1) * SLOTS + s + 1)
                    sp.dma_start(ring[:, s, :, :].rearrange("p j i -> p (j i)"),
                                 adj_cols[bass.ds(c, 1), s, :, :].rearrange("c p n -> (c p) n")
                                 ).then_inc(ring_landed[s], 16)

            sp.dma_start(stat_x[:, :, :].rearrange("p t f -> p (t f)"), x_tiles).then_inc(x_in, 16)
            load_ring(0, 0, True)
            with sp.Fori(1, CHUNKS) as c:
                load_ring(0, c, False)
            load_ring(1, 0, False)
            with sp.Fori(1, CHUNKS) as c:
                load_ring(1, c, False)

            def load_mask(c, m, fresh):
                t, b = m // BLOCKS, m % BLOCKS
                if not (fresh and m < 2):
                    sp.wait_ge(bias_ready, c * COLS + m - 1)
                sp.dma_start(adj_in[:, m % 2, :],
                             adj[bass.ds((c * TPC + t) * P, P), b * BLOCK:(b + 1) * BLOCK]
                             ).then_inc(adj_landed[m % 2], 16)

            def load_queries(c, t, fresh):
                if not (fresh and t < 2):
                    sp.wait_ge(scores_ready, (c * TPC + t - 1) * BLOCKS * H)
                for g in range(4):
                    sp.dma_start(parts[g * C:(g + 1) * C, t % 2, :].bitcast(F32).rearrange("p (h n) -> p h n", h=H),
                                 q4_dram[bass.ds(c, 1), g, :, :, t * P:(t + 1) * P].rearrange("o h c n -> (o c) h n")
                                 ).then_inc(q4_landed[t % 2], 16)

            def attention_loads(c, first):
                for m in range(COLS):
                    if m % BLOCKS == 0:
                        load_queries(c, m // BLOCKS, first)
                    load_mask(c, m, first)
                    if m == 5 and not first:
                        load_residuals(c - 1)
                    if m == 11 and not first:
                        store_x3(c - 1)

            def load_residuals(c):
                if not is_zero(c):
                    sp.wait_ge(att_dve, AV(c - 1, "xt"))
                    sp.wait_ge(att_x3_out, 16 * c)
                sp.dma_start(x2_g, x2_dram[:, bass.ds(c * CHUNK, CHUNK)]).then_inc(att_in, 16)
                sp.dma_start(root_g, root_dram[:, bass.ds(c * CHUNK, CHUNK)]).then_inc(att_in, 16)

            def store_x3(c):
                sp.wait_ge(att_dve, AV(c, "x3"))
                sp.dma_start(x3_dram[:, bass.ds(c * CHUNK, CHUNK)], x3_g).then_inc(att_x3_out, 16)

            sp.wait_ge(ring_multiplied, 2 * CHUNKS * SLOTS)
            sp.wait_ge(gcn_dve, CV(CHUNKS - 1, "root"))
            sp.wait_ge(gcn_q_out, 64 * CHUNKS)
            sp.wait_ge(gcn_k4_in, 64 * CHUNKS)
            sp.wait_ge(gcn_root_out, 16 * CHUNKS)
            sp.wait_ge(gcn_x2_out, 16 * CHUNKS)
            attention_loads(0, True)
            load_residuals(0)
            for m in range(COLS):
                if m % BLOCKS == 0:
                    load_queries(1, m // BLOCKS, False)
                load_mask(1, m, False)
                if m == 11:
                    store_x3(0)
            with sp.Fori(2, CHUNKS) as c:
                attention_loads(c, False)
            load_residuals(CHUNKS - 1)
            sp.wait_ge(unit_turned, CHUNKS * COLS * UPB)
            load_ring(2, 0, True)
            store_x3(CHUNKS - 1)
            with sp.Fori(1, CHUNKS) as c:
                load_ring(2, c, False)
            sp.wait_ge(hyp_out, 16 * CHUNKS)

        @block.tensor
        def _(pe):
            def turn4(dst_bank, src):
                for t in range(4):
                    last = pe.transpose(bank[:, dst_bank, t * P:(t + 1) * P], src[:, t * P:(t + 1) * P], ident[:, :])
                return last

            def product(layer, c, hooks):
                stat = stat_x if layer == 0 else stat_s
                for s in range(SLOTS):
                    pe.wait_ge(ring_landed[s], 16 * (layer * CHUNKS + c + 1))
                    for j in range(JPS):
                        jt = s * JPS + j
                        mm_ = pe.matmul(bank[:, 0, :], stat[:, jt, :], ring[:, s, j, :], start=(jt == 0),
                                        stop=(jt == TILES - 1))
                    mm_.then_inc(ring_multiplied, 1)
                    for hook in hooks.get(s, ()):
                        hook()

            def degree(c):
                pe.wait_ge(ring_summed, (c + 1) * SLOTS)
                for t in range(TPC):
                    for half_ in range(2):
                        last = pe.matmul(bank[:, 1, t:t + 1], colsum[:, half_ * CHUNK + t * P:half_ * CHUNK + (t + 1) * P],
                                         ones, start=(half_ == 0), stop=(half_ == 1))
                last.then_inc(gru_pe, 1)

            def message(c):
                pe.wait_ge(gru_act, GA(c, "agg"))
                pe.matmul(bank[:, 2, :], wmsg, agg_t, start=True, stop=True).then_inc(gru_pe, 1)

            def gates(c):
                pe.wait_ge(gru_act, GA(c, "msg"))
                pe.wait_ge(gru_xt_in, 16 * (c + 1))
                for g in range(2):
                    pe.matmul(bank[:, 3 + g, :], wih[:, g * P:(g + 1) * P], msg_t, start=True, stop=False)
                    pe.matmul(bank[:, 3 + g, :], whh[:, g * P:(g + 1) * P], xt_in, start=False,
                              stop=True).then_inc(gru_pe, 1)
                pe.matmul(bank[:, 5, :], wih[:, 2 * P:3 * P], msg_t, start=True, stop=True).then_inc(gru_pe, 1)
                pe.matmul(bank[:, 6, :], whh[:, 2 * P:3 * P], xt_in, start=True, stop=True).then_inc(gru_pe, 1)

            def turn_y(c):
                pe.wait_ge(gru_dve, GV(c, "y"))
                turn4(7, y_t).then_inc(gru_pe, 1)

            def turn_x1(c):
                pe.wait_ge(gru_dve, GV(c, "x1"))
                turn4(7, x_new).then_inc(gru_pe, 1)

            def support(c):
                pe.wait_ge(gru_act, GA(c, "x1_t"))
                pe.wait_ge(gru_dve, GV(c, "degree"))
                for t in range(TPC):
                    last = pe.matmul(bank[:, 1, t * P:(t + 1) * P], x_new_t[:, t * P:(t + 1) * P], wgcn[:, :],
                                     start=True, stop=True)
                last.then_inc(gru_pe, 1)

            def gru_hooks(c):
                return {0: [lambda: degree(c), lambda: message(c)], 1: [lambda: gates(c)], 4: [lambda: turn_y(c)],
                        5: [lambda: turn_x1(c)], 6: [lambda: support(c)]}

            def turn_agg(c):
                pe.wait_ge(gcn_act, CA(c, "agg"))
                turn4(1, agg_t).then_inc(gcn_pe, 1)

            def turn_x2(c):
                pe.wait_ge(gcn_dve, CV(c, "x2"))
                turn4(1, x_new).then_inc(gcn_pe, 1)

            def project(c):
                pe.wait_ge(gcn_act, CA(c, "x2_t"))
                pe.matmul(bank[:, 3, :], wk[:, :], x_new_t, start=True, stop=True).then_inc(gcn_pe, 1)
                pe.matmul(bank[:, 4, :], wq[:, :], x_new_t, start=True, stop=True).then_inc(gcn_pe, 1)
                for t in range(TPC):
                    last = pe.matmul(bank[:, 5 + t // 2, (t % 2) * 256:(t % 2) * 256 + 256],
                                     x_new_t[:, t * P:(t + 1) * P], wvs[:, :], start=True, stop=True)
                last.then_inc(gcn_pe, 1)

            def gcn_hooks(c):
                return {0: [lambda: turn_agg(c)], 3: [lambda: turn_x2(c)], 4: [lambda: project(c)]}

            def run(hooks):
                for s in sorted(hooks):
                    for hook in hooks[s]:
                        hook()

            pe.wait_ge(x_in, 16)
            product(0, 0, {})
            pe.wait_ge(weights_in, 16 * WEIGHTS)
            pe.wait_ge(consts_set, CONSTS)
            with pe.Fori(1, CHUNKS) as c:
                pe.wait_ge(gru_act, GA(c - 1, "agg"))
                product(0, c, gru_hooks(c - 1))
            pe.wait_ge(gru_act, GA(CHUNKS - 1, "agg"))
            pe.wait_ge(gru_dve, GV(CHUNKS - 2, "scaled"))
            hooks = gru_hooks(CHUNKS - 1)
            hooks[6] = hooks[6] + [lambda: pe.wait_ge(gru_dve, GV(CHUNKS - 1, "scaled"))]
            product(1, 0, hooks)
            with pe.Fori(1, CHUNKS) as c:
                pe.wait_ge(gcn_act, CA(c - 1, "agg"))
                product(1, c, gcn_hooks(c - 1))
            run(gcn_hooks(CHUNKS - 1))

            def scores(c, m, h, fresh):
                t, b = m // BLOCKS, m % BLOCKS
                if b == 0 and h == 0:
                    pe.wait_ge(q4_landed[t % 2], 64 * (2 * c + t // 2 + 1))
                if not (fresh and m == 0 and h < 2):
                    pe.wait_ge(masked_ready, (c * COLS + m) * H + h - 1)
                u = 2 * (h % 2)
                for i in range(BLOCK // CHUNK):
                    at_ = b * BLOCK + i * CHUNK
                    last = pe.matmul(bank[:, u + i, :], parts[:, t % 2, h * P:(h + 1) * P],
                                     k4[:, h, at_:at_ + CHUNK], start=True, stop=True)
                last.then_inc(scores_ready, 1)

            def turn_bank(c, first, use):
                prev, chunks = TURN_BANKS.before(use, first)
                if prev is None:
                    return
                if prev[0] == "unit":
                    k = prev[1] * UPB + prev[2]
                    if prev[2] in VECTOR_UNITS:
                        pe.wait_ge(unit_copied_dve, (c - chunks) * len(BY_VECTOR) + BY_VECTOR.index(k) + 1)
                    else:
                        pe.wait_ge(unit_copied_act, (c - chunks) * len(BY_SCALAR) + BY_SCALAR.index(k) + 1)
                elif prev[0] == "out":
                    pe.wait_ge(tile_dve, TV((c - chunks) * TPC + prev[1] // BLOCKS - 1, "wide"))
                else:
                    pe.wait_ge(att_act, AA(c - chunks - 1, {"x3": "x3_t", "mx": "mx"}[prev[0]]))

            def turn_unit(c, n, u, first):
                if u == 0:
                    pe.wait_ge(exp_ready, (c * COLS + n) * H + H)
                turn_bank(c, first, ("unit", n, u))
                b_ = TURN_BANKS.bank(("unit", n, u))
                for h in range(H):
                    last = pe.transpose(bank[:, b_, h * P:(h + 1) * P], cols[:, n % 4, h, u * P:(u + 1) * P],
                                        ident[:, :])
                last.then_inc(unit_turned, 1)

            def attend(c, k, first):
                n, u = k // UPB, k % UPB
                t, b = n // BLOCKS, n % BLOCKS
                if b == 0 and u == 0 and not (first and t == 0):
                    pe.wait_ge(tile_act, TA(c * TPC + t - 1, "copied"))
                if u in VECTOR_UNITS:
                    pe.wait_ge(unit_copied_dve, c * len(BY_VECTOR) + BY_VECTOR.index(k) + 1)
                else:
                    pe.wait_ge(unit_copied_act, c * len(BY_SCALAR) + BY_SCALAR.index(k) + 1)
                for h in range(H):
                    last = pe.matmul(bank[h * C:(h + 1) * C, 7, b * P:(b + 1) * P],
                                     stat_x[:, b * UPB + u, h * C:(h + 1) * C], turned[:, k % 4, h * P:(h + 1) * P],
                                     start=(u == 0), stop=(u == UPB - 1))
                last.then_inc(unit_used, 1)

            def turn_out(c, t, body_c, first, use):
                pe.wait_ge(tile_act, TA(c * TPC + t, "copied"))
                turn_bank(body_c, first, use)
                turn4(TURN_BANKS.bank(use), o_t).then_inc(tile_pe, 1)

            def turn_x3(c, dst, body_c=None):
                pe.wait_ge(att_dve, AV(c, "x3"))
                if body_c is not None:
                    turn_bank(body_c, False, ("x3",))
                turn4(dst, x3_g).then_inc(att_pe, 1)

            def mobius_product(c, dst, body_c=None):
                pe.wait_ge(att_act, AA(c, "x3_t"))
                if body_c is not None:
                    turn_bank(body_c, False, ("mx",))
                for t in range(TPC):
                    last = pe.matmul(bank[:, dst, t * P:(t + 1) * P], x3_t[:, t * P:(t + 1) * P], whyp[:, :],
                                     start=True, stop=True)
                last.then_inc(att_pe, 1)

            def attention(c, first, last_chunk):
                for n in range(COLS):
                    for u in range(UPB):
                        if u % 2 == 0:
                            ahead = n + 2
                            if ahead < COLS:
                                scores(c, ahead, u // 2, False)
                            elif not last_chunk:
                                scores(c + 1, ahead - COLS, u // 2, False)
                        turn_unit(c, n, u, first)
                        k = n * UPB + u
                        if k >= 2:
                            attend(c, k - 2, first)
                        if u == OUT_AT and n % BLOCKS == 0:
                            if n > 0:
                                turn_out(c, n // BLOCKS - 1, c, first, ("out", n))
                            elif not first:
                                turn_out(c - 1, TPC - 1, c, first, ("out", 0))
                        if (n, u) == X3_AT and not first:
                            turn_x3(c - 1, TURN_BANKS.bank(("x3",)), c)
                        if (n, u) == MX_AT and not first:
                            mobius_product(c - 1, TURN_BANKS.bank(("mx",)), c)
                attend(c, COLS * UPB - 2, first)
                attend(c, COLS * UPB - 1, first)

            pe.wait_ge(gcn_k4_in, 64 * CHUNKS)
            pe.wait_ge(gcn_dve, CV(CHUNKS - 1, "root"))
            for m in range(2):
                for h in range(H):
                    scores(0, m, h, True)
            attention(0, True, False)
            with pe.Fori(1, CHUNKS - 1) as c:
                attention(c, False, False)
            attention(CHUNKS - 1, False, True)

            def turn_u(c):
                pe.wait_ge(hyp_act, HA(c, "agg"))
                turn4(1, agg_t).then_inc(hyp_pe, 1)

            last = CHUNKS - 1

            pe.wait_ge(att_dve, AV(last - 1, "xt"))

            def final_out():
                pe.wait_ge(tile_act, TA(last * TPC + TPC - 1, "copied"))
                turn4(1, o_t).then_inc(tile_pe, 1)

            product(2, 0, {0: [final_out], 2: [lambda: turn_x3(last, 2)], 3: [lambda: mobius_product(last, 3)],
                           6: [lambda: pe.wait_ge(att_dve, AV(last, "xt"))]})
            with pe.Fori(1, CHUNKS) as c:
                pe.wait_ge(hyp_act, HA(c - 1, "agg"))
                product(2, c, {0: [lambda: turn_u(c - 1)]})
            turn_u(last)

        @block.scalar
        def _(act):
            for ap, src in ((wmsg, w_msg), (wih, w_ih), (whh, w_hh), (bmsg, b_msg), (bih, b_ih), (bhh, b_hh),
                            (bq, b_q), (bk, b_k), (wgcn[:, :], w_gcn), (wq[:, :], w_q), (wk[:, :], w_k),
                            (wvs[:, :], w_vs), (whyp[:, :], w_hyp)):
                act.dma_start(ap, src).then_inc(weights_in, 16)
            for ap, src in ((bgcn[:, :], b_gcn), (bvs[:, :], b_vs), (hbias[:, :], b_hyp), (wbo[:, :], w_beta[0:P]),
                            (wbr[:, :], w_beta[P:2 * P]), (wb3, w_beta[2 * P:3 * P])):
                act.dma_start(ap, src.partition_broadcast(P)).then_inc(weights_in, 16)
            act.wait_ge(weights_in, 16 * WEIGHTS)
            act.activation(bias_sq, hbias[:, :], ACT.Square, accum_out=hb[:, 0:1]).then_inc(bias_act, 1)
            act.wait_ge(bias_pool, 2)
            act.activation(hb[:, 2:3], hb[:, 1:2], ACT.Tanh).then_inc(bias_act, 1)
            act.wait_ge(bias_dve, 6)
            act.activation(bias_sq, hbias[:, :], ACT.Square, accum_out=hb[:, 3:4]).then_inc(bias_act, 1)

            def gru(c, first):
                if not first:
                    act.wait_ge(gru_dve, GV(c - 1, "y"))
                    act.wait_ge(gru_x1_out, 16 * c)
                act.dma_start(xt_in, x_t[:, bass.ds(c * CHUNK, CHUNK)]).then_inc(gru_xt_in, 16)
                act.wait_ge(ring_multiplied, (c + 1) * SLOTS)
                act.activation(agg_t, bank[:, 0, :], ACT.Copy).then_inc(gru_act, 1)
                act.wait_ge(gru_pe, GP(c, "msg"))
                act.activation(msg_t, bank[:, 2, :], ACT.Relu, bias=bmsg).then_inc(gru_act, 1)
                act.wait_ge(gru_pe, GP(c, "r"))
                act.activation(r_t, bank[:, 3, :], ACT.Tanh, bias=brz[:, 0:1], scale=0.5).then_inc(gru_act, 1)
                act.wait_ge(gru_pe, GP(c, "z"))
                act.activation(z_t, bank[:, 4, :], ACT.Tanh, bias=brz[:, 1:2], scale=0.5).then_inc(gru_act, 1)
                act.wait_ge(gru_dve, GV(c, "npre"))
                act.activation(n_t, hn_t, ACT.Tanh, bias=bih[:, 2:3]).then_inc(gru_act, 1)
                act.wait_ge(gru_dve, GV(c, "x1"))
                act.dma_start(x1_dram[:, bass.ds(c * CHUNK, CHUNK)], x_new).then_inc(gru_x1_out, 16)
                act.wait_ge(gru_pe, GP(c, "x1_turned"))
                act.activation(x_new_t, bank[:, 7, :], ACT.Copy).then_inc(gru_act, 1)

            gru(0, True)
            with act.Fori(1, CHUNKS) as c:
                gru(c, False)

            def gcn(c, first):
                if not first:
                    act.wait_ge(gcn_dve, CV(c - 1, "y"))
                else:
                    act.wait_ge(gru_x1_out, 16 * CHUNKS)
                act.dma_start(res_in, x1_dram[:, bass.ds(c * CHUNK, CHUNK)]).then_inc(gcn_x1_in, 16)
                act.wait_ge(ring_multiplied, (CHUNKS + c + 1) * SLOTS)
                act.activation(agg_t, bank[:, 0, :], ACT.Copy).then_inc(gcn_act, 1)
                act.wait_ge(gcn_dve, CV(c, "x2"))
                act.dma_start(x2_dram[:, bass.ds(c * CHUNK, CHUNK)], x_new).then_inc(gcn_x2_out, 16)
                act.wait_ge(gcn_pe, CP(c, "x2_turned"))
                act.activation(x_new_t, bank[:, 1, :], ACT.Copy).then_inc(gcn_act, 1)
                act.wait_ge(gcn_pe, CP(c, "k"))
                if not first:
                    act.wait_ge(gcn_q_out, 64 * c)
                act.activation(parts[:, 0, :], bank[:, 3, :], ACT.Identity, bias=bk).then_inc(gcn_act, 1)
                act.wait_ge(gcn_act, CA(c, "k_hi"))
                act.wait_ge(gcn_dve, CV(c, "k_lo"))
                for g in range(4):
                    act.dma_start(k4_dram[bass.ds(c, 1), g, :, :, :].rearrange("o h c n -> (o h c) n"),
                                  parts[:, g % 2, :].bitcast(F32)).then_inc(gcn_k_out, 16)
                act.wait_ge(gcn_pe, CP(c, "q"))
                act.wait_ge(gcn_k_out, 64 * (c + 1))
                act.activation(parts[:, 0, :], bank[:, 4, :], ACT.Identity, bias=bq).then_inc(gcn_act, 1)
                act.wait_ge(gcn_act, CA(c, "q_hi"))
                act.wait_ge(gcn_dve, CV(c, "q_lo"))
                for g in range(4):
                    act.dma_start(q4_dram[bass.ds(c, 1), g, :, :, :].rearrange("o h c n -> (o h c) n"),
                                  parts[:, g // 2, :].bitcast(F32)).then_inc(gcn_q_out, 16)
                act.wait_ge(gcn_dve, CV(c, "root"))
                act.dma_start(root_dram[:, bass.ds(c * CHUNK, CHUNK)], root_out).then_inc(gcn_root_out, 16)

            gcn(0, True)
            with act.Fori(1, CHUNKS) as c:
                gcn(c, False)

            def exponent(c, m, h):
                t, b = m // BLOCKS, m % BLOCKS
                if h == 0:
                    act.wait_ge(shift_ready, c * COLS + m + 1)
                piece = cols[:, m % 4, h, :]
                i = b * H + h
                act.activation(piece, piece, ACT.Exp, bias=shift[:, t % 2, i:i + 1], scale=SCORE_SCALE,
                               accum_out=blocksum[:, t % 2, i:i + 1]).then_inc(exp_ready, 1)

            def copy_unit(c, n, u, first):
                k = n * UPB + u
                act.wait_ge(unit_turned, c * COLS * UPB + k + 1)
                if not (first and k < 4):
                    act.wait_ge(unit_used, c * COLS * UPB + k - 3)
                act.activation(turned[:, k % 4, :], bank[:, TURN_BANKS.bank(("unit", n, u)), :],
                               ACT.Copy).then_inc(unit_copied_act, 1)

            def block_weights(c, t):
                g = c * TPC + t
                act.wait_ge(tile_dve, TV(g, "below"))
                act.activation(mix, mix, ACT.Exp, scale=SCORE_SCALE).then_inc(tile_act, 1)

            def copy_out(c, t):
                g = c * TPC + t
                act.wait_ge(unit_used, (g + 1) * BLOCKS * UPB)
                if not is_zero(g):
                    act.wait_ge(tile_pe, TP(g - 1, "turned"))
                act.activation(o_t, bank[:, 7, :], ACT.Copy).then_inc(tile_act, 1)

            def post_steps(c, x3_bank, mx_bank, wide_free):
                def beta_exp():
                    act.wait_ge(att_dve, AV(c, "zz"))
                    act.activation(ez, zz, ACT.Exp, scale=-1.0).then_inc(att_act, 1)

                def copy_x3():
                    act.wait_ge(att_pe, AP_(c, "x3_turned"))
                    act.wait_ge(tile_dve, TV(wide_free, "out"))
                    act.activation(x3_t, bank[:, x3_bank, :], ACT.Copy).then_inc(att_act, 1)

                def copy_mx():
                    act.wait_ge(att_pe, AP_(c, "mx"))
                    act.activation(mx_g, bank[:, mx_bank, :], ACT.Copy).then_inc(att_act, 1)

                def logs(name):
                    act.wait_ge(att_pool, AG(c, name))
                    act.activation(t1, s3, ACT.Ln, bias=1.0, scale=1.0).then_inc(att_act, 1)
                    act.activation(t2, s3, ACT.Ln, bias=1.0, scale=-1.0).then_inc(att_act, 1)

                def arg_tanh():
                    act.wait_ge(att_pool, AG(c, "arg2"))
                    act.activation(s4, s4, ACT.Tanh).then_inc(att_act, 1)

                return {(3, 3): beta_exp, (5, 4): copy_x3, (6, 4): copy_mx, (9, 3): lambda: logs("xn_min"),
                        (10, 3): arg_tanh, (13, 7): lambda: logs("pn")}

            def attention(c, first, last_chunk):
                post = {} if first else post_steps(c - 1, TURN_BANKS.bank(("x3",)), TURN_BANKS.bank(("mx",)), c * TPC)
                for n in range(COLS):
                    for u in range(UPB):
                        if n % BLOCKS == 0 and u == 0:
                            if n > 0:
                                block_weights(c, n // BLOCKS - 1)
                            elif not first:
                                block_weights(c - 1, TPC - 1)
                        if n % BLOCKS == 0 and u == 2:
                            if n > 0:
                                copy_out(c, n // BLOCKS - 1)
                            elif not first:
                                copy_out(c - 1, TPC - 1)
                        if u not in VECTOR_UNITS:
                            copy_unit(c, n, u, first)
                        if u % 2 == 1:
                            ahead = n + 1
                            if ahead < COLS:
                                exponent(c, ahead, u // 2)
                            elif not last_chunk:
                                exponent(c + 1, ahead - COLS, u // 2)
                        if (n, u) in post:
                            post[(n, u)]()

            for h in range(H):
                exponent(0, 0, h)
            attention(0, True, False)
            with act.Fori(1, CHUNKS - 1) as c:
                attention(c, False, False)
            attention(CHUNKS - 1, False, True)
            block_weights(CHUNKS - 1, TPC - 1)
            copy_out(CHUNKS - 1, TPC - 1)
            final = post_steps(CHUNKS - 1, 2, 3, TILES - 1)
            for place in sorted(final):
                final[place]()
            act.wait_ge(att_dve, AV(CHUNKS - 1, "xt"))

            def hyperbolic(c, first):
                if first:
                    act.wait_ge(att_x3_out, 16 * CHUNKS)
                else:
                    act.wait_ge(hyp_dve, HV(c - 1, "y"))
                act.dma_start(res_in, x3_dram[:, bass.ds(c * CHUNK, CHUNK)]).then_inc(hyp_in, 16)
                act.wait_ge(ring_multiplied, (2 * CHUNKS + c + 1) * SLOTS)
                act.activation(agg_t, bank[:, 0, :], ACT.Copy).then_inc(hyp_act, 1)
                act.wait_ge(hyp_pe, HP(c, "turned"))
                for t in range(TPC):
                    last = act.activation(y_t[:, t * P:(t + 1) * P], bank[:, 1, t * P:(t + 1) * P], ACT.Square,
                                          accum_out=s1[:, t:t + 1])
                last.then_inc(hyp_act, 1)
                act.wait_ge(hyp_pool, HG(c, "un_max"))
                act.activation(t1, s2, ACT.Tanh).then_inc(hyp_act, 1)
                act.wait_ge(hyp_pool, HG(c, "p"))
                act.activation(t2, s3, ACT.Ln, bias=1.0, scale=1.0).then_inc(hyp_act, 1)
                act.activation(t3, s3, ACT.Ln, bias=1.0, scale=-1.0).then_inc(hyp_act, 1)
                act.wait_ge(hyp_pool, HG(c, "fac"))
                for t in range(TPC):
                    last = act.activation(msg_t[:, t * P:(t + 1) * P], bank[:, 1, t * P:(t + 1) * P], ACT.Relu,
                                          scale=s5[:, t:t + 1])
                last.then_inc(hyp_act, 1)
                act.wait_ge(hyp_act, HA(c, "w"))
                for t in range(TPC):
                    last = act.activation(y_t[:, t * P:(t + 1) * P], msg_t[:, t * P:(t + 1) * P], ACT.Square,
                                          accum_out=s6[:, t:t + 1])
                last.then_inc(hyp_act, 1)
                act.wait_ge(hyp_pool, HG(c, "wn_max"))
                act.activation(t1, s7, ACT.Tanh).then_inc(hyp_act, 1)
                act.wait_ge(hyp_dve, HV(c, "out"))
                act.dma_start(out[:, bass.ds(c * CHUNK, CHUNK)], x_new).then_inc(hyp_out, 16)

            hyperbolic(0, True)
            with act.Fori(1, CHUNKS) as c:
                hyperbolic(c, False)

        @block.vector
        def _(dve):
            def norm_stats(src, sem_, st, c):
                for t in range(TPC):
                    last = dve.bn_stats(bn6[:, 6 * t:6 * t + 6], src[:, t * P:(t + 1) * P])
                last.then_inc(sem_, 1)
                dve.wait_ge(sem_, st(c, "bn6"))
                dve.nop(nofuse=True)
                for t in range(TPC):
                    last = dve.bn_aggr(mean_var[:, t, :], bn6[:, 6 * t:6 * t + 6])
                last.then_inc(sem_, 1)

            def normalise(dst, src):
                for t in range(TPC):
                    last = dve.tensor_scalar(dst[:, t * P:(t + 1) * P], src[:, t * P:(t + 1) * P],
                                             mean_var[:, t, 0:1], rstd[:, t:t + 1], ALU.subtract, ALU.mult)
                return last

            dve.wait_ge(weights_in, 16 * WEIGHTS)
            dve.tensor_tensor(wbo[:, :], wbo[:, :], wb3, ALU.add).then_inc(bias_dve, 1)
            dve.tensor_tensor(wbr[:, :], wbr[:, :], wb3, ALU.subtract).then_inc(bias_dve, 1)
            dve.tensor_tensor(brz, bih[:, 0:2], bhh[:, 0:2], ALU.add).then_inc(bias_dve, 1)
            dve.wait_ge(bias_dve, 3)
            dve.tensor_scalar(brz, brz, 0.5, None, ALU.mult).then_inc(bias_dve, 1)
            dve.wait_ge(bias_pool, 3)
            dve.wait_ge(bias_act, 2)
            dve.tensor_scalar(hb[:, 2:3], hb[:, 2:3], MAX_NORM, hb[:, 0:1], ALU.min, ALU.mult).then_inc(bias_dve, 1)
            dve.wait_ge(bias_dve, 5)
            dve.tensor_scalar(hbias[:, :], hbias[:, :], hb[:, 2:3], None, ALU.mult).then_inc(bias_dve, 1)

            def sum_slot(c, s, fresh):
                dve.wait_ge(ring_landed[s], 16 * (c + 1))
                lo = ring[:, s, 0:2, :].rearrange("p j i -> p (j i)")
                hi = ring[:, s, 2:4, :].rearrange("p j i -> p (j i)")
                if s == 0:
                    if not fresh:
                        dve.wait_ge(gru_pe, GP(c - 1, "degree"))
                    dve.tensor_tensor(colsum, lo, hi, ALU.add).then_inc(ring_summed, 1)
                else:
                    dve.wait_ge(ring_summed, c * SLOTS + s)
                    dve.tensor_tensor(colsum, colsum, lo, ALU.add).then_inc(half_summed, 1)
                    dve.wait_ge(half_summed, c * (SLOTS - 1) + s)
                    dve.tensor_tensor(colsum, colsum, hi, ALU.add).then_inc(ring_summed, 1)

            def gru_steps(c):
                def degree():
                    dve.wait_ge(gru_pe, GP(c, "degree"))
                    dve.tensor_scalar(deg, bank[:, 1, 0:4], 1.0, None, ALU.add).then_inc(gru_dve, 1)
                    dve.wait_ge(gru_dve, GV(c, "degree"))
                    dve.tensor_scalar(deg_on, deg, 0.0, None, ALU.is_gt).then_inc(gru_dve, 1)

                def gate():
                    dve.wait_ge(gru_pe, GP(c, "n_hid"))
                    dve.tensor_scalar(hn_t, bank[:, 6, :], bhh[:, 2:3], 0.5, ALU.add, ALU.mult).then_inc(gru_dve, 1)
                    dve.wait_ge(gru_dve, GV(c, "hn"))
                    dve.wait_ge(gru_act, GA(c, "r"))
                    dve.scalar_tensor_tensor(hn_t, r_t, 1.0, hn_t, ALU.add, ALU.mult).then_inc(gru_dve, 1)
                    dve.wait_ge(gru_dve, GV(c, "rhn"))
                    dve.tensor_tensor(hn_t, bank[:, 5, :], hn_t, ALU.add).then_inc(gru_dve, 1)

                def blend():
                    dve.wait_ge(gru_act, GA(c, "n"))
                    dve.tensor_tensor(y_t, xt_in, n_t, ALU.subtract).then_inc(gru_dve, 1)
                    dve.wait_ge(gru_dve, GV(c, "diff"))
                    dve.scalar_tensor_tensor(y_t, z_t, 1.0, y_t, ALU.add, ALU.mult).then_inc(gru_dve, 1)
                    dve.wait_ge(gru_dve, GV(c, "zdiff"))
                    dve.scalar_tensor_tensor(y_t, y_t, 0.5, n_t, ALU.mult, ALU.add).then_inc(gru_dve, 1)
                    dve.wait_ge(gru_dve, GV(c, "nz"))
                    dve.tensor_tensor(y_t, y_t, xt_in, ALU.add).then_inc(gru_dve, 1)

                def stats():
                    dve.wait_ge(gru_pe, GP(c, "y_turned"))
                    norm_stats(bank[:, 7, :], gru_dve, GV, c)

                def norm():
                    dve.wait_ge(gru_pool, GG(c, "rstd"))
                    normalise(x_new, bank[:, 7, :]).then_inc(gru_dve, 1)

                def scale():
                    dve.wait_ge(gru_pool, GG(c, "deg_pow"))
                    dcol = dinv[:, bass.ds(c * TPC, TPC)]
                    dve.tensor_tensor(dcol, deg, deg_on, ALU.mult).then_inc(gru_dve, 1)
                    dve.wait_ge(gru_dve, GV(c, "dinv"))
                    dve.wait_ge(gru_pe, GP(c, "support"))
                    dve.tensor_tensor(stat_s[:, bass.ds(c * TPC, TPC), :], tiles(bank[:, 1, :]),
                                      dcol.unsqueeze(2).to_broadcast([P, TPC, P]), ALU.mult).then_inc(gru_dve, 1)

                return {0: [degree], 2: [gate], 3: [blend], 4: [stats], 5: [norm], 6: [scale]}

            def sums(c, fresh, steps):
                for s in range(SLOTS):
                    sum_slot(c, s, fresh)
                    for step in steps.get(s, ()):
                        step()

            sums(0, True, {})
            with dve.Fori(1, CHUNKS) as c:
                sums(c, False, gru_steps(c - 1))
            last_steps = gru_steps(CHUNKS - 1)
            for s in sorted(last_steps):
                for step in last_steps[s]:
                    step()

            def gcn(c):
                dve.wait_ge(gcn_pe, CP(c, "turned"))
                dve.tensor_tensor(tiles(y_n), tiles(bank[:, 1, :]), stat_s[:, bass.ds(c * TPC, TPC), :],
                                  ALU.add).then_inc(gcn_dve, 1)
                dve.tensor_copy(deg, dinv[:, bass.ds(c * TPC, TPC)]).then_inc(gcn_dve, 1)
                dve.wait_ge(gcn_dve, CV(c, "dinv"))
                dve.wait_ge(gcn_pool, CG(c, "x1_bias"))
                for t in range(TPC):
                    s_ = slice(t * P, (t + 1) * P)
                    last = dve.scalar_tensor_tensor(y_n[:, s_], y_n[:, s_], deg[:, t:t + 1], res_in[:, s_],
                                                    ALU.mult, ALU.add)
                last.then_inc(gcn_dve, 1)
                dve.wait_ge(gcn_dve, CV(c, "y"))
                norm_stats(y_n, gcn_dve, CV, c)
                dve.wait_ge(gcn_pool, CG(c, "rstd"))
                if not is_zero(c):
                    dve.wait_ge(gcn_x2_out, 16 * c)
                normalise(x_new, y_n).then_inc(gcn_dve, 1)
                dve.wait_ge(gcn_act, CA(c, "k_hi"))
                dve.scalar_tensor_tensor(parts[:, 1, :], bank[:, 3, :], bk, parts[:, 0, :].bitcast(F32), ALU.add,
                                         ALU.subtract).then_inc(gcn_dve, 1)
                dve.wait_ge(gcn_act, CA(c, "q_hi"))
                dve.scalar_tensor_tensor(parts[:, 1, :], bank[:, 4, :], bq, parts[:, 0, :].bitcast(F32), ALU.add,
                                         ALU.subtract).then_inc(gcn_dve, 1)
                dve.wait_ge(gcn_pe, CP(c, "vs"))
                both = bank[:, 5:7, :].rearrange("p b (t k f) -> p (b t) k f", t=2, k=2)
                for k, dst in ((0, stat_x[:, bass.ds(c * TPC, TPC), :]), (1, tiles(root_out))):
                    if k == 1 and not is_zero(c):
                        dve.wait_ge(gcn_root_out, 16 * c)
                    dve.tensor_tensor(dst, both[:, :, k, :], per_tile(bvs[:, k * P:(k + 1) * P]),
                                      ALU.add).then_inc(gcn_dve, 1)

            gcn(0)
            with dve.Fori(1, CHUNKS) as c:
                gcn(c)

            def mask(c, m, h, first):
                t, b = m // BLOCKS, m % BLOCKS
                if h == 0:
                    dve.wait_ge(bias_ready, c * COLS + m + 1)
                    if not (first and m < 4):
                        dve.wait_ge(unit_turned, (c * COLS + m - 3) * UPB)
                dve.wait_ge(scores_ready, (c * COLS + m) * H + h + 1)
                dve.nop(nofuse=True)
                i = b * H + h
                dve.tensor_tensor_reduce(out=cols[:, m % 4, h, :],
                                         in0=bank[:, 2 * (h % 2):2 * (h % 2) + 2, :].rearrange("p b n -> p (b n)"),
                                         in1=maskbias[:, m % 2, :], scale=1.0, scalar=LOWEST, op0=ALU.add,
                                         op1=ALU.max, accum_out=blockmax[:, t % 2, i:i + 1]).then_inc(masked_ready, 1)
                if h == H - 1:
                    dve.wait_ge(masked_ready, (c * COLS + m) * H + H)
                    dve.tensor_scalar(shift[:, t % 2, b * H:(b + 1) * H], blockmax[:, t % 2, b * H:(b + 1) * H],
                                      -SCORE_SCALE, None, ALU.mult).then_inc(shift_ready, 1)

            def copy_unit(c, n, u, first):
                k = n * UPB + u
                dve.wait_ge(unit_turned, c * COLS * UPB + k + 1)
                if not (first and k < 4):
                    dve.wait_ge(unit_used, c * COLS * UPB + k - 3)
                dve.tensor_copy(turned[:, k % 4, :], bank[:, TURN_BANKS.bank(("unit", n, u)), :]).then_inc(unit_copied_dve, 1)

            def below_max(c, t):
                g = c * TPC + t
                bm = blockmax[:, t % 2, :].rearrange("p (b h) -> p b h", h=H)
                dve.wait_ge(masked_ready, (g + 1) * BLOCKS * H)
                dve.tensor_reduce(rowmax, bm.rearrange("p b h -> p h b"), AX.X, ALU.max).then_inc(tile_dve, 1)
                dve.wait_ge(tile_dve, TV(g, "rowmax"))
                dve.tensor_tensor(mix.rearrange("p (b h) -> p b h", h=H), bm,
                                  rowmax.unsqueeze(1).to_broadcast([P, BLOCKS, H]), ALU.subtract).then_inc(tile_dve, 1)

            def combine(c, t, b_):
                g = c * TPC + t
                dve.wait_ge(tile_act, TA(g, "weights"))
                dve.wait_ge(exp_ready, (g + 1) * BLOCKS * H)
                dve.tensor_tensor(mix2, mix, blocksum[:, t % 2, :], ALU.mult).then_inc(tile_dve, 1)
                dve.wait_ge(tile_dve, TV(g, "wsum"))
                dve.tensor_reduce(rowsum, mix2.rearrange("p (b h) -> p h b", h=H), AX.X, ALU.add).then_inc(tile_dve, 1)
                dve.wait_ge(tile_dve, TV(g, "rowsum"))
                dve.tensor_scalar(noedge, rowsum, 0.0, None, ALU.is_equal).then_inc(tile_dve, 1)
                dve.wait_ge(tile_dve, TV(g, "noedge"))
                dve.tensor_tensor(rowsum, rowsum, noedge, ALU.add).then_inc(tile_dve, 1)
                dve.wait_ge(tile_dve, TV(g, "guard"))
                dve.reciprocal(rrow, rowsum).then_inc(tile_dve, 1)
                dve.wait_ge(tile_dve, TV(g, "recip"))
                dve.tensor_tensor(mix.rearrange("p (b h) -> p b h", h=H), mix.rearrange("p (b h) -> p b h", h=H),
                                  rrow.unsqueeze(1).to_broadcast([P, BLOCKS, H]), ALU.mult).then_inc(tile_dve, 1)
                dve.wait_ge(tile_dve, TV(g, "mix"))
                dve.wait_ge(tile_pe, TP(g, "turned"))
                dve.tensor_tensor(wide.rearrange("p (k f) -> p k f", f=C), bank[:, b_, :].rearrange("p (k f) -> p k f", f=C),
                                  mix.unsqueeze(2).to_broadcast([P, BLOCKS * H, C]), ALU.mult).then_inc(tile_dve, 1)
                dve.wait_ge(tile_dve, TV(g, "wide"))
                dve.tensor_reduce(o_n[:, t * P:(t + 1) * P].rearrange("p (f h) -> p h f", h=H),
                                  wide.rearrange("p (b h f) -> p h f b", b=BLOCKS, h=H), AX.X,
                                  ALU.add).then_inc(tile_dve, 1)

            def post_steps(c, ahead=0):
                def beta_logit():
                    dve.wait_ge(att_pool, AG(c, "z"))
                    dve.tensor_reduce(zz, tiles(y_g), AX.X, ALU.add).then_inc(att_dve, 1)

                def mix_root():
                    dve.wait_ge(att_act, AA(c, "ez"))
                    dve.tensor_scalar(ez, ez, 1.0, None, ALU.add).then_inc(att_dve, 1)
                    dve.wait_ge(att_dve, AV(c, "one_ez"))
                    dve.reciprocal(beta, ez).then_inc(att_dve, 1)
                    dve.wait_ge(att_dve, AV(c, "beta"))
                    dve.wait_ge(att_pool, AG(c, "sum"))
                    for t in range(TPC):
                        s_ = slice(t * P, (t + 1) * P)
                        last = dve.scalar_tensor_tensor(y_g[:, s_], root_g[:, s_], beta[:, t:t + 1], x2_g[:, s_],
                                                        ALU.mult, ALU.add)
                    last.then_inc(att_dve, 1)
                    dve.wait_ge(att_dve, AV(c, "y"))
                    norm_stats(y_g, att_dve, AV, c)

                def norm():
                    dve.wait_ge(att_pool, AG(c, "rstd"))
                    normalise(x3_g, y_g).then_inc(att_dve, 1)

                def norm_x3():
                    dve.wait_ge(att_pool, AG(c, "x3sq"))
                    dve.tensor_reduce(xx, tiles(y_g), AX.X, ALU.add).then_inc(att_dve, 1)

                def norm_mx():
                    dve.wait_ge(att_pool, AG(c, "mxsq"))
                    dve.tensor_reduce(mm, tiles(y_g), AX.X, ALU.add).then_inc(att_dve, 1)
                    dve.wait_ge(att_pool, AG(c, "mxhb"))
                    dve.tensor_reduce(mh, tiles(root_g), AX.X, ALU.add).then_inc(att_dve, 1)

                def mobius_sum():
                    dve.wait_ge(att_pool, AG(c, "B"))
                    for t in range(TPC):
                        s_ = slice(t * P, (t + 1) * P)
                        last = dve.tensor_scalar(root_g[:, s_], hbias[:, :], s7[:, t:t + 1], None, ALU.mult)
                    last.then_inc(att_dve, 1)
                    dve.wait_ge(att_dve, AV(c, "scaled_bias"))
                    for t in range(TPC):
                        s_ = slice(t * P, (t + 1) * P)
                        last = dve.scalar_tensor_tensor(mx_g[:, s_], mx_g[:, s_], s6[:, t:t + 1], root_g[:, s_],
                                                        ALU.mult, ALU.add)
                    last.then_inc(att_dve, 1)

                def norm_h():
                    dve.wait_ge(att_pool, AG(c, "hsq"))
                    dve.tensor_reduce(hh, tiles(y_g), AX.X, ALU.add).then_inc(att_dve, 1)

                def log_map():
                    dve.wait_ge(att_pool, AG(c, "fac"))
                    dve.tensor_tensor(stat_s[:, bass.ds(c * TPC, TPC), :], tiles(mx_g),
                                      s1.unsqueeze(2).to_broadcast([P, TPC, P]), ALU.mult).then_inc(att_dve, 1)

                return {5: [beta_logit], 7: [mix_root], 9: [norm], 12: [norm_x3], 16: [norm_mx], 23: [mobius_sum],
                        25: [norm_h], 30: [log_map]}

            def attention(c, first, last_chunk):
                post = post_steps(c - 1) if not first else {}
                for n in range(COLS):
                    for u in range(UPB):
                        if u % 2 == 0:
                            ahead = n + 2
                            if ahead < COLS:
                                mask(c, ahead, u // 2, first)
                            elif not last_chunk:
                                mask(c + 1, ahead - COLS, u // 2, False)
                        if u in VECTOR_UNITS:
                            copy_unit(c, n, u, first)
                        if n % BLOCKS == 0 and u == 7:
                            if n > 0:
                                combine(c, n // BLOCKS - 1, TURN_BANKS.bank(("out", n)))
                            elif not first:
                                combine(c - 1, TPC - 1, TURN_BANKS.bank(("out", 0)))
                        if n % BLOCKS == BLOCKS - 1 and u == 7:
                            below_max(c, n // BLOCKS)
                        if u in (3, 7):
                            for step in post.get(2 * n + u // 4, ()):
                                step()

            dve.wait_ge(ring_multiplied, 2 * CHUNKS * SLOTS)
            dve.wait_ge(bias_dve, 6)
            for m in range(2):
                for h in range(H):
                    mask(0, m, h, True)
            attention(0, True, False)
            with dve.Fori(1, CHUNKS - 1) as c:
                attention(c, False, False)
            attention(CHUNKS - 1, False, True)
            combine(CHUNKS - 1, TPC - 1, 1)
            final = post_steps(CHUNKS - 1)
            for slot in sorted(final):
                for step in final[slot]:
                    step()

            def hyperbolic(c):
                dve.wait_ge(hyp_pool, HG(c, "fh"))
                dve.tensor_tensor(y_n, msg_t, res_in, ALU.add).then_inc(hyp_dve, 1)
                dve.wait_ge(hyp_dve, HV(c, "y"))
                norm_stats(y_n, hyp_dve, HV, c)
                dve.wait_ge(hyp_pool, HG(c, "rstd"))
                if not is_zero(c):
                    dve.wait_ge(hyp_out, 16 * c)
                normalise(x_new, y_n).then_inc(hyp_dve, 1)

            hyperbolic(0)
            with dve.Fori(1, CHUNKS) as c:
                hyperbolic(c)

        @block.gpsimd
        def _(pool):
            pool.memset(ones, 1.0).then_inc(consts_set, 1)
            pool.memset(minus_half, -0.5).then_inc(consts_set, 1)
            pool.memset(half, 0.5).then_inc(consts_set, 1)
            pool.memset(minus_one, -1.0).then_inc(consts_set, 1)
            pool.memset(ident[:, :], 0.0).then_inc(consts_set, 1)
            pool.wait_ge(consts_set, 5)
            pool.affine_select(out=ident[:, :], in_=ident[:, :], compare_op=ALU.not_equal, fill=1.0, base=0,
                               pattern=[[-1, P]], channel_multiplier=1).then_inc(consts_set, 1)
            pool.wait_ge(bias_act, 1)
            pool.tensor_tensor(hb[:, 1:2], hb[:, 0:1], half[:, 0:1], ALU.pow).then_inc(bias_pool, 1)
            pool.wait_ge(bias_pool, 1)
            pool.tensor_scalar(hb[:, 1:2], hb[:, 1:2], MIN_NORM, None, ALU.max).then_inc(bias_pool, 1)
            pool.wait_ge(bias_pool, 2)
            pool.tensor_tensor(hb[:, 0:1], hb[:, 1:2], minus_one[:, 0:1], ALU.pow).then_inc(bias_pool, 1)

            def stage(sem_, st):
                def step(c, name, ins):
                    ins.then_inc(sem_, 1)
                    pool.wait_ge(sem_, st(c, name))
                    pool.nop(nofuse=True)
                return step

            def rsqrt_var(c, step):
                pool.nop(nofuse=True)
                step(c, "eps", pool.tensor_scalar(rstd, mean_var[:, :, 1], LN_EPS, None, ALU.add))
                step(c, "rstd", pool.tensor_tensor(rstd, rstd, minus_half, ALU.pow))

            def gru(c):
                step = stage(gru_pool, GG)
                pool.wait_ge(gru_dve, GV(c, "deg_on"))
                pool.nop(nofuse=True)
                step(c, "deg_max", pool.tensor_scalar(deg, deg, 1e-30, None, ALU.max))
                step(c, "deg_pow", pool.tensor_tensor(deg, deg, minus_half, ALU.pow))
                pool.wait_ge(gru_dve, GV(c, "bn"))
                rsqrt_var(c, step)

            gru(0)
            with pool.Fori(1, CHUNKS) as c:
                gru(c)

            def gcn(c):
                step = stage(gcn_pool, CG)
                pool.wait_ge(gcn_x1_in, 16 * (c + 1))
                step(c, "x1_bias", pool.tensor_tensor(tiles(res_in), tiles(res_in), per_tile(bgcn[:, :]), ALU.add))
                pool.wait_ge(gcn_dve, CV(c, "bn"))
                rsqrt_var(c, step)
                pool.wait_ge(gcn_k_out, 64 * (c + 1))
                for g in range(4):
                    pool.dma_start(k4[g * C:(g + 1) * C, :, bass.ds(c * CHUNK, CHUNK)].bitcast(F32),
                                   k4_dram[bass.ds(c, 1), g, :, :, :].rearrange("o h c n -> (o c) h n")
                                   ).then_inc(gcn_k4_in, 16)

            gcn(0)
            with pool.Fori(1, CHUNKS) as c:
                gcn(c)

            def mask_bias(c, m, first):
                pool.wait_ge(adj_landed[m % 2], 16 * (c * COLS // 2 + m // 2 + 1))
                if not (first and m < 2):
                    pool.wait_ge(masked_ready, (c * COLS + m - 1) * H)
                pool.nop(nofuse=True)
                pool.tensor_scalar(maskbias[:, m % 2, :], adj_in[:, m % 2, :], 0.0, MASKED, ALU.is_equal,
                                   ALU.mult).then_inc(bias_ready, 1)

            def post_steps(c):
                step = stage(att_pool, AG)

                def tt(name, out_, a, b, op):
                    step(c, name, pool.tensor_tensor(out_, a, b, op))

                def ts(name, out_, a, x, op, y=None, op2=None):
                    if op2 is None:
                        step(c, name, pool.tensor_scalar(out_, a, x, None, op))
                    else:
                        step(c, name, pool.tensor_scalar(out_, a, x, y, op, op2))

                def beta_terms():
                    pool.wait_ge(tile_dve, TV(c * TPC + TPC - 1, "out"))
                    pool.wait_ge(att_in, 32 * (c + 1))
                    tt("zo", tiles(y_g), tiles(o_n), per_tile(wbo[:, :]), ALU.mult)
                    tt("zr", tiles(mx_g), tiles(root_g), per_tile(wbr[:, :]), ALU.mult)
                    tt("z", y_g, y_g, mx_g, ALU.add)
                    tt("diff", root_g, root_g, o_n, ALU.subtract)
                    tt("sum", x2_g, x2_g, o_n, ALU.add)

                def rs():
                    pool.wait_ge(att_dve, AV(c, "bn"))
                    rsqrt_var(c, step)

                def x3sq():
                    pool.wait_ge(att_dve, AV(c, "x3"))
                    tt("x3sq", y_g, x3_g, x3_g, ALU.mult)

                def mx_terms():
                    pool.wait_ge(att_act, AA(c, "mx"))
                    pool.wait_ge(att_dve, AV(c, "xx"))
                    tt("mxsq", y_g, mx_g, mx_g, ALU.mult)
                    tt("mxhb", tiles(root_g), tiles(mx_g), per_tile(hbias[:, :]), ALU.mult)

                def norms():
                    pool.wait_ge(att_dve, AV(c, "mh"))
                    tt("xn", s1, xx, half, ALU.pow)
                    ts("xn_max", s1, s1, MIN_NORM, ALU.max)
                    tt("mn", s2, mm, half, ALU.pow)
                    ts("mn_max", s2, s2, MIN_NORM, ALU.max)
                    ts("xn_min", s3, s1, ARTANH_MAX, ALU.min)

                def argument():
                    pool.wait_ge(att_act, AA(c, "ln_b"))
                    tt("a", t1, t1, t2, ALU.subtract)
                    ts("a_half", t1, t1, 0.5, ALU.mult)
                    tt("xn_inv", s4, s1, minus_one, ALU.pow)
                    tt("arg", s4, s4, s2, ALU.mult)
                    tt("arg2", s4, s4, t1, ALU.mult)

                def coefficients():
                    pool.wait_ge(att_act, AA(c, "tanh"))
                    pool.nop(nofuse=True)
                    ts("g_min", s4, s4, MAX_NORM, ALU.min)
                    tt("mn_inv", s5, s2, minus_one, ALU.pow)
                    tt("g", s4, s4, s5, ALU.mult)
                    tt("g2", s5, s4, s4, ALU.mult)
                    tt("x2", s5, s5, mm, ALU.mult)
                    tt("xy", s6, s4, mh, ALU.mult)
                    ts("xy2", s6, s6, 2.0, ALU.mult, 1.0, ALU.add)
                    ts("x2y2", s7, s5, hb[:, 3:4], ALU.mult)
                    tt("den", s7, s7, s6, ALU.add)
                    ts("den_max", s7, s7, MIN_NORM, ALU.max)
                    tt("den_inv", s3, s7, minus_one, ALU.pow)
                    ts("a_num", s6, s6, hb[:, 3:4], ALU.add)
                    tt("a_g", s6, s6, s4, ALU.mult)
                    tt("A", s6, s6, s3, ALU.mult)
                    ts("b_num", s7, s5, -1.0, ALU.mult, 1.0, ALU.add)
                    tt("B", s7, s7, s3, ALU.mult)

                def hsq():
                    pool.wait_ge(att_dve, AV(c, "h"))
                    tt("hsq", y_g, mx_g, mx_g, ALU.mult)

                def norms_h():
                    pool.wait_ge(att_dve, AV(c, "hh"))
                    tt("hn", s1, hh, half, ALU.pow)
                    ts("hn_max", s1, s1, MIN_NORM, ALU.max)
                    ts("pn", s3, s1, MAX_NORM, ALU.min)

                def factor():
                    pool.wait_ge(att_act, AA(c, "ln_d"))
                    tt("fa", t1, t1, t2, ALU.subtract)
                    ts("fa_half", t1, t1, 0.5, ALU.mult)
                    tt("hn_inv", s1, s1, minus_one, ALU.pow)
                    tt("fac", s1, s1, t1, ALU.mult)

                return {2: [beta_terms], 8: [rs], 10: [x3sq], 14: [mx_terms], 17: [norms], 19: [argument],
                        21: [coefficients], 24: [hsq], 26: [norms_h], 28: [factor]}

            pool.wait_ge(bias_dve, 6)
            pool.wait_ge(bias_act, 3)

            def attention(c, first, last_chunk):
                post = post_steps(c - 1) if not first else {}
                for n in range(COLS):
                    for half_ in range(2):
                        if half_ == 0:
                            ahead = n + 3
                            if ahead < COLS:
                                mask_bias(c, ahead, first)
                            elif not last_chunk:
                                mask_bias(c + 1, ahead - COLS, False)
                        for step in post.get(2 * n + half_, ()):
                            step()

            for m in range(3):
                mask_bias(0, m, True)
            attention(0, True, False)
            with pool.Fori(1, CHUNKS - 1) as c:
                attention(c, False, False)
            attention(CHUNKS - 1, False, True)
            final = post_steps(CHUNKS - 1)
            for slot in sorted(final):
                for step in final[slot]:
                    step()

            def hyperbolic(c):
                step = stage(hyp_pool, HG)
                pool.wait_ge(hyp_act, HA(c, "uu"))
                step(c, "un", pool.tensor_tensor(s2, s1, half, ALU.pow))
                step(c, "un_max", pool.tensor_scalar(s2, s2, MIN_NORM, None, ALU.max))
                pool.wait_ge(hyp_act, HA(c, "tanh"))
                pool.nop(nofuse=True)
                step(c, "p", pool.tensor_scalar(s3, t1, MAX_NORM, None, ALU.min))
                step(c, "un_inv", pool.tensor_tensor(s5, s2, minus_one, ALU.pow))
                pool.wait_ge(hyp_act, HA(c, "ln_b"))
                pool.tensor_tensor(t2, t2, t3, ALU.subtract).then_inc(hyp_sub, 1)
                pool.wait_ge(hyp_sub, 2 * c + 1)
                pool.nop(nofuse=True)
                pool.tensor_scalar(t2, t2, 0.5, None, ALU.mult).then_inc(hyp_sub, 1)
                pool.wait_ge(hyp_sub, 2 * c + 2)
                step(c, "fac", pool.tensor_tensor(s5, s5, t2, ALU.mult))
                pool.wait_ge(hyp_act, HA(c, "ww"))
                step(c, "wn", pool.tensor_tensor(s7, s6, half, ALU.pow))
                step(c, "wn_max", pool.tensor_scalar(s7, s7, MIN_NORM, None, ALU.max))
                pool.wait_ge(hyp_act, HA(c, "tanh2"))
                pool.nop(nofuse=True)
                step(c, "p2", pool.tensor_scalar(t1, t1, MAX_NORM, None, ALU.min))
                step(c, "wn_inv", pool.tensor_tensor(s7, s7, minus_one, ALU.pow))
                step(c, "f2", pool.tensor_tensor(s7, s7, t1, ALU.mult))
                pool.wait_ge(hyp_in, 16 * (c + 1))
                step(c, "fh", pool.tensor_tensor(tiles(msg_t), tiles(msg_t), s7.unsqueeze(2).to_broadcast([P, TPC, P]),
                                                 ALU.mult))
                pool.wait_ge(hyp_dve, HV(c, "bn"))
                rsqrt_var(c, step)

            hyperbolic(0)
            with pool.Fori(1, CHUNKS) as c:
                hyperbolic(c)


def kernel(x, adj, L0_gnn_W_msg, L0_gnn_b_msg, L0_gnn_W_ih, L0_gnn_W_hh, L0_gnn_b_ih, L0_gnn_b_hh,
           L1_gnn_weight, L1_gnn_bias, L2_gnn_Wq, L2_gnn_bq, L2_gnn_Wk, L2_gnn_bk, L2_gnn_Wv, L2_gnn_bv,
           L2_gnn_Ws, L2_gnn_bs, L2_gnn_Wb, L3_gnn_weight, L3_gnn_bias):
    import numpy as np
    import concourse.bacc as bacc
    from concourse.bass_utils import run_bass_kernel_spmd

    def a(v):
        return np.asarray(v)

    arrays = {
        "adj_cols": a(adj).reshape(CHUNKS, CHUNK, SLOTS, JPS, P).transpose(0, 2, 4, 3, 1).reshape(
            CHUNKS, SLOTS, P, JPS * CHUNK),
        "adj": a(adj),
        "x_tiles": a(x).reshape(TILES, P, P).transpose(1, 0, 2).reshape(P, TILES * P),
        "x_t": a(x).T,
        "w_msg": a(L0_gnn_W_msg).T, "b_msg": a(L0_gnn_b_msg).reshape(P, 1),
        "w_ih": a(L0_gnn_W_ih).T, "w_hh": a(L0_gnn_W_hh).T,
        "b_ih": a(L0_gnn_b_ih).reshape(3, P).T, "b_hh": a(L0_gnn_b_hh).reshape(3, P).T,
        "w_gcn": a(L1_gnn_weight), "b_gcn": a(L1_gnn_bias),
        "w_q": a(L2_gnn_Wq), "b_q": a(L2_gnn_bq).reshape(P, 1),
        "w_k": a(L2_gnn_Wk), "b_k": a(L2_gnn_bk).reshape(P, 1),
        "w_vs": np.concatenate([a(L2_gnn_Wv), a(L2_gnn_Ws)], axis=1),
        "b_vs": np.concatenate([a(L2_gnn_bv), a(L2_gnn_bs)]),
        "w_beta": a(L2_gnn_Wb).reshape(3 * P),
        "w_hyp": a(L3_gnn_weight).T, "b_hyp": a(L3_gnn_bias),
    }
    arrays = {name: np.ascontiguousarray(v) for name, v in arrays.items()}
    nc = bacc.Bacc("TRN2", target_bir_lowering=False, num_devices=1)
    args = {name: nc.dram_tensor(name, v.shape, F32, kind="ExternalInput").ap() for name, v in arrays.items()}
    out = nc.dram_tensor("out", (P, TILES * P), F32, kind="ExternalOutput").ap()
    build_program(nc, out=out, **args)
    result = run_bass_kernel_spmd(nc, [arrays], core_ids=[0])
    return result.results[0]["out"].reshape(P, TILES, P).transpose(1, 0, 2).reshape(N, P)
```

```python
from contextlib import ExitStack

import concourse.bass as bass
from concourse import mybir

F32 = mybir.dt.float32
F32R = mybir.dt.float32r
BF16 = mybir.dt.bfloat16
ALU = mybir.AluOpType
ACT = mybir.ActivationFunctionType
AX = mybir.AxisListType

P = 128
N = 4096
CONSTS = 6
WEIGHTS = 19
TILES = N // P
CHUNK = 512
CHUNKS = N // CHUNK
TPC = CHUNK // P
SLOTS = 8
JPS = TILES // SLOTS
H, C = 4, 32
BLOCK = 1024
BLOCKS = N // BLOCK
COLS = TPC * BLOCKS
UPB = BLOCK // P
SCORE_SCALE = 1.0 / float(C) ** 0.5
MASKED = -1.0e30
LOWEST = -1.0e20
LN_EPS = 1e-5
MIN_NORM = 1e-15
MAX_NORM = 1.0 - 0.004
ARTANH_MAX = 1.0 - 1e-7
VECTOR_UNITS = (0, 2, 4, 6)
SCORE_LEAD = 11
MASK_LEAD = 10
EXP_LEAD = 6
BIAS_LEAD = 6
USE_LAG = 3
OUT_AT = 5
X3_AT = (6, 5)
MX_AT = (7, 5)


def is_zero(c):
    return isinstance(c, int) and c == 0


def head_ahead(c, n, u, lead, last_chunk):
    i = n * H + u // 2 + lead
    if i < COLS * H:
        return c, i // H, i % H
    return None if last_chunk else (c + 1, i // H - COLS, i % H)


class Steps:

    def __init__(self, *names):
        self.names = names

    def __call__(self, c, name):
        return c * len(self.names) + self.names.index(name) + 1


class TurnBanks:

    BANKS = (4, 5, 6)

    def __init__(self):
        self.uses = []
        for n in range(COLS):
            for u in range(UPB):
                self.uses.append(("unit", n, u))
                if u == OUT_AT and n % BLOCKS == 0:
                    self.uses.append(("out", n))
                if (n, u) == X3_AT:
                    self.uses.append(("x3",))
                if (n, u) == MX_AT:
                    self.uses.append(("mx",))
        while len(self.uses) % len(self.BANKS):
            self.uses.append(None)

    def bank(self, use):
        return self.BANKS[self.uses.index(use) % len(self.BANKS)]

    def before(self, use, first):
        i = self.uses.index(use) - len(self.BANKS)
        while i >= 0:
            if self.uses[i] and not (first and self.uses[i] in (("out", 0), ("x3",), ("mx",))):
                return self.uses[i], 0
            i -= len(self.BANKS)
        if first:
            return None, 0
        i += len(self.uses)
        while not self.uses[i]:
            i -= len(self.BANKS)
        return self.uses[i], 1


TURN_BANKS = TurnBanks()
UNITS = [(n, u) for n in range(COLS) for u in range(UPB)]
BY_VECTOR = [n * UPB + u for n, u in UNITS if u in VECTOR_UNITS]
BY_SCALAR = [n * UPB + u for n, u in UNITS if u not in VECTOR_UNITS]


def build_program(nc, adj_cols, adj, x_tiles, x_t, w_msg, b_msg, w_ih, w_hh, b_ih, b_hh, w_gcn, b_gcn,
                  w_q, b_q, w_k, b_k, w_vs, b_vs, w_beta, w_hyp, b_hyp, out):
    x1_dram = nc.dram_tensor("x1_dram", [P, TILES * P], F32)
    x2_dram = nc.dram_tensor("x2_dram", [P, TILES * P], F32)
    root_dram = nc.dram_tensor("root_dram", [P, TILES * P], F32)
    x3_dram = nc.dram_tensor("x3_dram", [P, TILES * P], F32)
    q4_dram = nc.dram_tensor("q4_dram", [CHUNKS, 4, H, C, CHUNK], F32)
    k4_dram = nc.dram_tensor("k4_dram", [CHUNKS, 4, H, C, CHUNK], F32)

    with ExitStack() as ctx:
        def sb(name, shape, dt=F32):
            return ctx.enter_context(nc.sbuf_tensor(name, shape, dt))

        def sem(name):
            return ctx.enter_context(nc.semaphore(name))

        k4 = sb("k4", [P, H, N], F32R)
        parts = sb("parts", [P, 2, CHUNK], F32R)
        stat_x = sb("stat_x", [P, TILES, P])
        stat_s = sb("stat_s", [P, TILES, P])
        arena = sb("arena", [P, 25600])
        ident = sb("ident", [P, P])
        early = sb("early", [P, 8 * P])
        wgcn, wq, wk, bgcn = [early[:, i * P:(i + 1) * P] for i in range(4)]
        wvs, bvs = early[:, 4 * P:6 * P], early[:, 6 * P:8 * P]
        whyp = sb("whyp", [P, P])
        wbo = sb("wbo", [P, P])
        wbr = sb("wbr", [P, P])
        hbias = sb("hbias", [P, P])
        small = sb("small", [P, 340])
        taken = [0]

        def cut(n):
            taken[0] += n
            return small[:, taken[0] - n:taken[0]]

        bmsg, bih, bhh, bq, bk = cut(1), cut(3), cut(3), cut(1), cut(1)
        brz = cut(2)
        ones = cut(1)
        minus_half, half, minus_one = cut(4), cut(4), cut(4)
        dinv = cut(TILES)
        deg = cut(4)
        deg_on = cut(4)
        bn6 = cut(24)
        mean_var = cut(8).rearrange("p (t k) -> p t k", k=2)
        rstd = cut(4)
        hb = cut(4)
        blockmax = cut(32).rearrange("p (b k) -> p b k", b=2)
        shift = cut(32).rearrange("p (b k) -> p b k", b=2)
        blocksum = cut(32).rearrange("p (b k) -> p b k", b=2)
        rowmax, rowsum, noedge, rrow = cut(4), cut(4), cut(4), cut(4)
        mix = cut(16)
        mix2 = cut(16)
        zz, ez, beta = cut(4), cut(4), cut(4)
        xx, mm, mh, hh = cut(4), cut(4), cut(4), cut(4)
        s1, s2, s3, s4, s5, s6, s7 = [cut(4) for _ in range(7)]
        t1, t2, t3 = [cut(4) for _ in range(3)]

        RING = SLOTS * JPS * CHUNK
        ring = arena[:, 0:RING].rearrange("p (s j i) -> p s j i", s=SLOTS, j=JPS)
        stages = [arena[:, RING + i * CHUNK:RING + (i + 1) * CHUNK] for i in range(18)]
        agg_t, msg_t, xt_in, r_t, z_t, n_t, hn_t, y_t, x_new, x_new_t = stages[:10]
        colsum = arena[:, RING + 10 * CHUNK:RING + 12 * CHUNK]
        wih = arena[:, RING + 12 * CHUNK:RING + 12 * CHUNK + 384]
        whh = arena[:, RING + 13 * CHUNK:RING + 13 * CHUNK + 384]
        wmsg = arena[:, RING + 14 * CHUNK:RING + 14 * CHUNK + 128]
        res_in, root_out, y_n = stages[15:18]
        agg1_t, x2_new, x2_new_t = stages[10:13]
        k_parts, q_parts = [arena[:, RING + i * CHUNK:RING + (i + 2) * CHUNK].bitcast(F32R).rearrange(
            "p (k n) -> p k n", k=2) for i in (2, 13)]
        wb3, bias_sq = root_out[:, 0:P], root_out[:, P:2 * P]
        cols = arena[:, 0:4 * H * BLOCK].rearrange("p (s h n) -> p s h n", s=4, h=H)
        at = 4 * H * BLOCK
        turned = arena[:, at:at + 4 * CHUNK].rearrange("p (s n) -> p s n", s=4)
        at += 4 * CHUNK
        adj_in = arena[:, at:at + 2 * BLOCK].rearrange("p (s n) -> p s n", s=2)
        at += 2 * BLOCK
        maskbias = [half_[:, i * BLOCK:(i + 1) * BLOCK] for half_ in
                    (arena[:, at:at + BLOCK].bitcast(BF16), early[:, :].bitcast(BF16)) for i in range(2)]
        at += BLOCK
        o_t, wide, o_n, root_g, x2_g, y_g, x3_g, mx_g = [arena[:, at + i * CHUNK:at + (i + 1) * CHUNK]
                                                        for i in range(8)]
        x3_t = wide
        bank = ctx.enter_context(nc.psum_tensor("bank", [P, 8, CHUNK], F32))

        def tiles(ap):
            return ap.rearrange("p (t f) -> p t f", f=P)

        def per_tile(row, n=TPC):
            return row.unsqueeze(1).to_broadcast([P, n, P])

        x_in = sem("x_in")
        weights_in = sem("weights_in")
        consts_set = sem("consts_set")
        bias_dve = sem("bias_dve")
        bias_act = sem("bias_act")
        bias_pool = sem("bias_pool")
        ring_landed = [sem(f"ring_landed{s}") for s in range(SLOTS)]
        ring_multiplied = sem("ring_multiplied")
        ring_summed = sem("ring_summed")
        half_summed = sem("half_summed")
        gru_pe, gru_act, gru_dve, gru_pool = [sem(f"gru_{e}") for e in ("pe", "act", "dve", "pool")]
        gru_xt_in, gru_x1_out = sem("gru_xt_in"), sem("gru_x1_out")
        GP = Steps("degree", "msg", "r", "z", "n_in", "n_hid", "y_turned", "x1_turned", "support")
        GA = Steps("agg", "msg", "r", "z", "n", "x1_t")
        GV = Steps("degree", "deg_on", "hn", "rhn", "npre", "diff", "zdiff", "nz", "y", "bn6", "bn", "x1", "dinv", "scaled")
        GG = Steps("deg_max", "deg_pow", "eps", "rstd")
        gcn_pe, gcn_act, gcn_dve, gcn_pool = [sem(f"gcn_{e}") for e in ("pe", "act", "dve", "pool")]
        gcn_x1_in, gcn_x2_out, gcn_root_out = sem("gcn_x1_in"), sem("gcn_x2_out"), sem("gcn_root_out")
        gcn_k_out, gcn_q_out, gcn_k4_in = sem("gcn_k_out"), sem("gcn_q_out"), sem("gcn_k4_in")
        CP = Steps("turned", "x2_turned", "k", "q", "vs")
        CA = Steps("agg", "x2_t", "k_hi", "q_hi")
        CV = Steps("self", "dinv", "y", "bn6", "bn", "x2", "k_lo", "q_lo", "v", "root")
        CG = Steps("x1_bias", "eps", "rstd")
        adj_landed = [sem(f"adj_landed{s}") for s in range(2)]
        q4_landed = [sem(f"q4_landed{s}") for s in range(2)]
        bias_ready = sem("bias_ready")
        scores_ready = sem("scores_ready")
        masked_ready = sem("masked_ready")
        shift_ready = sem("shift_ready")
        exp_ready = sem("exp_ready")
        unit_turned = sem("unit_turned")
        unit_copied_act = sem("unit_copied_act")
        unit_copied_dve = sem("unit_copied_dve")
        unit_used = sem("unit_used")
        rows_pe, rows_act, rows_dve, rows_pool = [sem(f"rows_{e}") for e in ("pe", "act", "dve", "pool")]
        TP = Steps("turned")
        TA = Steps("weights", "copied")
        TV = Steps("rowmax", "below", "wide", "out")
        TG = Steps("wsum", "pair", "rowsum", "noedge", "guard", "recip", "mix")
        att_pe, att_act, att_dve, att_pool = [sem(f"att_{e}") for e in ("pe", "act", "dve", "pool")]
        att_in, att_x3_out = sem("att_in"), sem("att_x3_out")
        AP_ = Steps("x3_turned", "mx")
        AA = Steps("ez", "x3_t", "mx", "ln_a", "ln_b", "tanh", "ln_c", "ln_d")
        AV = Steps("zz", "one_ez", "beta", "bn6", "bn", "x3", "xx", "mm", "mh", "hh")
        AG = Steps("zo", "zr", "z", "diff", "sum", "root_b", "y", "eps", "rstd", "x3sq", "mxsq", "mxhb",
                   "xn", "xn_max", "mn", "mn_max", "xn_min", "a", "a_half", "xn_inv", "arg", "arg2",
                   "g_min", "mn_inv", "g", "g2", "x2", "xy", "xy2", "x2y2", "den", "den_max", "den_inv",
                   "a_num", "a_g", "A", "b_num", "B", "bias_b", "mx_a", "h", "hsq", "hn", "hn_max", "pn", "fa", "fa_half",
                   "hn_inv", "fac", "xt")
        hyp_pe, hyp_act, hyp_dve, hyp_pool = [sem(f"hyp_{e}") for e in ("pe", "act", "dve", "pool")]
        hyp_in, hyp_out, hyp_sub = sem("hyp_in"), sem("hyp_out"), sem("hyp_sub")
        HP = Steps("turned")
        HA = Steps("agg", "uu", "tanh", "ln_a", "ln_b", "w", "ww", "tanh2")
        HV = Steps("y", "bn6", "bn", "out")
        HG = Steps("un", "un_max", "p", "un_inv", "fac", "wn", "wn_max", "p2", "wn_inv", "f2", "fh", "eps", "rstd")

        block = ctx.enter_context(nc.Block())

        @block.sync
        def _(sp):
            def load_ring(layer, c, first):
                for s in range(SLOTS):
                    turn = layer * CHUNKS + c
                    if not first:
                        sp.wait_ge(ring_multiplied, (turn - 1) * SLOTS + s + 1)
                        if layer == 0 or is_zero(c):
                            sp.wait_ge(ring_summed, (turn - 1) * SLOTS + s + 1)
                    sp.dma_start(ring[:, s, :, :].rearrange("p j i -> p (j i)"),
                                 adj_cols[bass.ds(c, 1), s, :, :].rearrange("c p n -> (c p) n")
                                 ).then_inc(ring_landed[s], 16)

            sp.dma_start(stat_x[:, :, :].rearrange("p t f -> p (t f)"), x_tiles).then_inc(x_in, 16)
            load_ring(0, 0, True)
            with sp.Fori(1, CHUNKS) as c:
                load_ring(0, c, False)
            load_ring(1, 0, False)
            with sp.Fori(1, CHUNKS) as c:
                load_ring(1, c, False)

            def load_mask(c, m, fresh):
                t, b = m // BLOCKS, m % BLOCKS
                if not (fresh and m < 2):
                    sp.wait_ge(bias_ready, c * COLS + m - 1)
                sp.dma_start(adj_in[:, m % 2, :],
                             adj[bass.ds((c * TPC + t) * P, P), b * BLOCK:(b + 1) * BLOCK]
                             ).then_inc(adj_landed[m % 2], 16)

            def load_queries(c, t, fresh):
                if not (fresh and t < 2):
                    sp.wait_ge(scores_ready, (c * TPC + t - 1) * BLOCKS * H)
                for g in range(4):
                    sp.dma_start(parts[g * C:(g + 1) * C, t % 2, :].bitcast(F32).rearrange("p (h n) -> p h n", h=H),
                                 q4_dram[bass.ds(c, 1), g, :, :, t * P:(t + 1) * P].rearrange("o h c n -> (o c) h n")
                                 ).then_inc(q4_landed[t % 2], 16)

            def attention_loads(c, first):
                for m in range(COLS):
                    if m % BLOCKS == 0:
                        load_queries(c, m // BLOCKS, first)
                    load_mask(c, m, first)
                    if m == 8 and not first:
                        load_residuals(c - 1)
                    if m == 15 and not first:
                        store_x3(c - 1)

            def load_residuals(c):
                if not is_zero(c):
                    sp.wait_ge(att_pool, AG(c - 1, "xt"))
                    sp.wait_ge(att_x3_out, 16 * c)
                sp.dma_start(x2_g, x2_dram[:, bass.ds(c * CHUNK, CHUNK)]).then_inc(att_in, 16)
                sp.dma_start(root_g, root_dram[:, bass.ds(c * CHUNK, CHUNK)]).then_inc(att_in, 16)

            def store_x3(c):
                sp.wait_ge(att_dve, AV(c, "x3"))
                sp.dma_start(x3_dram[:, bass.ds(c * CHUNK, CHUNK)], x3_g).then_inc(att_x3_out, 16)

            sp.wait_ge(ring_multiplied, 2 * CHUNKS * SLOTS)
            sp.wait_ge(gcn_dve, CV(CHUNKS - 1, "root"))
            sp.wait_ge(gcn_q_out, 64 * CHUNKS)
            sp.wait_ge(gcn_k4_in, 64 * CHUNKS)
            sp.wait_ge(gcn_root_out, 16 * CHUNKS)
            sp.wait_ge(gcn_x2_out, 16 * CHUNKS)
            attention_loads(0, True)
            load_residuals(0)
            for m in range(COLS):
                if m % BLOCKS == 0:
                    load_queries(1, m // BLOCKS, False)
                load_mask(1, m, False)
                if m == 15:
                    store_x3(0)
            with sp.Fori(2, CHUNKS) as c:
                attention_loads(c, False)
            load_residuals(CHUNKS - 1)
            sp.wait_ge(unit_turned, CHUNKS * COLS * UPB)
            load_ring(2, 0, True)
            store_x3(CHUNKS - 1)
            with sp.Fori(1, CHUNKS) as c:
                load_ring(2, c, False)
            sp.wait_ge(hyp_out, 16 * CHUNKS)

        @block.tensor
        def _(pe):
            def turn4(dst_bank, src):
                for t in range(4):
                    last = pe.transpose(bank[:, dst_bank, t * P:(t + 1) * P], src[:, t * P:(t + 1) * P], ident[:, :])
                return last

            def product(layer, c, hooks):
                stat = stat_x if layer == 0 else stat_s
                for s in range(SLOTS):
                    pe.wait_ge(ring_landed[s], 16 * (layer * CHUNKS + c + 1))
                    for j in range(JPS):
                        jt = s * JPS + j
                        mm_ = pe.matmul(bank[:, 0, :], stat[:, jt, :], ring[:, s, j, :], start=(jt == 0),
                                        stop=(jt == TILES - 1))
                    mm_.then_inc(ring_multiplied, 1)
                    for hook in hooks.get(s, ()):
                        hook()

            def degree(c):
                pe.wait_ge(ring_summed, (c + 1) * SLOTS)
                for t in range(TPC):
                    for half_ in range(2):
                        last = pe.matmul(bank[:, 7, t:t + 1], colsum[:, half_ * CHUNK + t * P:half_ * CHUNK + (t + 1) * P],
                                         ones, start=(half_ == 0), stop=(half_ == 1))
                last.then_inc(gru_pe, 1)

            def message(c):
                pe.wait_ge(gru_act, GA(c, "agg"))
                pe.matmul(bank[:, 2, :], wmsg, agg_t, start=True, stop=True).then_inc(gru_pe, 1)

            def gates(c):
                pe.wait_ge(gru_act, GA(c, "msg"))
                pe.wait_ge(gru_xt_in, 16 * (c + 1))
                for g in range(2):
                    pe.matmul(bank[:, 3 + g, :], wih[:, g * P:(g + 1) * P], msg_t, start=True, stop=False)
                    pe.matmul(bank[:, 3 + g, :], whh[:, g * P:(g + 1) * P], xt_in, start=False,
                              stop=True).then_inc(gru_pe, 1)
                pe.matmul(bank[:, 5, :], wih[:, 2 * P:3 * P], msg_t, start=True, stop=True).then_inc(gru_pe, 1)
                pe.matmul(bank[:, 6, :], whh[:, 2 * P:3 * P], xt_in, start=True, stop=True).then_inc(gru_pe, 1)

            def turn_y(c):
                pe.wait_ge(gru_dve, GV(c, "y"))
                turn4(7, y_t).then_inc(gru_pe, 1)

            def turn_x1(c):
                pe.wait_ge(gru_dve, GV(c, "x1"))
                turn4(7, x_new).then_inc(gru_pe, 1)

            def support(c):
                pe.wait_ge(gru_act, GA(c, "x1_t"))
                for t in range(TPC):
                    last = pe.matmul(bank[:, 1, t * P:(t + 1) * P], x_new_t[:, t * P:(t + 1) * P], wgcn[:, :],
                                     start=True, stop=True)
                last.then_inc(gru_pe, 1)

            def gru_hooks(c, support_at=SLOTS - 1):
                return {0: [lambda: degree(c), lambda: message(c)], 1: [lambda: gates(c)], 4: [lambda: turn_y(c)],
                        6: [lambda: turn_x1(c)], support_at: [lambda: support(c)]}

            def turn_agg(c):
                pe.wait_ge(gcn_act, CA(c, "agg"))
                turn4(7, agg1_t).then_inc(gcn_pe, 1)

            def turn_x2(c):
                pe.wait_ge(gcn_dve, CV(c, "x2"))
                turn4(7, x2_new).then_inc(gcn_pe, 1)

            def project(c):
                pe.wait_ge(gcn_act, CA(c, "x2_t"))
                pe.matmul(bank[:, 4, :], wk, x2_new_t, start=True, stop=True).then_inc(gcn_pe, 1)
                pe.matmul(bank[:, 7, :], wq, x2_new_t, start=True, stop=True).then_inc(gcn_pe, 1)
                for t in range(TPC):
                    last = pe.matmul(bank[:, 5 + t // 2, (t % 2) * 256:(t % 2) * 256 + 256],
                                     x2_new_t[:, t * P:(t + 1) * P], wvs, start=True, stop=True)
                last.then_inc(gcn_pe, 1)

            def gcn_hooks(c):
                return {0: [lambda: turn_agg(c)], 4: [lambda: turn_x2(c)], 5: [lambda: project(c)],
                        SLOTS - 1: [lambda: pe.wait_ge(gcn_dve, CV(c, "q_lo"))]}

            def run(hooks):
                for s in sorted(hooks):
                    for hook in hooks[s]:
                        hook()

            pe.wait_ge(x_in, 16)
            product(0, 0, {})
            pe.wait_ge(weights_in, 16 * WEIGHTS)
            pe.wait_ge(consts_set, CONSTS)
            with pe.Fori(1, CHUNKS) as c:
                pe.wait_ge(gru_act, GA(c - 1, "agg"))
                product(0, c, gru_hooks(c - 1))
            pe.wait_ge(gru_act, GA(CHUNKS - 1, "agg"))
            pe.wait_ge(gru_dve, GV(CHUNKS - 2, "scaled"))
            hooks = gru_hooks(CHUNKS - 1)
            hooks[5] = hooks.pop(6)
            hooks[6] = hooks.pop(SLOTS - 1) + [lambda: pe.wait_ge(gru_dve, GV(CHUNKS - 1, "scaled"))]
            product(1, 0, hooks)
            with pe.Fori(1, CHUNKS) as c:
                pe.wait_ge(gcn_act, CA(c - 1, "agg"))
                product(1, c, gcn_hooks(c - 1))
            run(gcn_hooks(CHUNKS - 1))

            def scores(c, m, h, fresh):
                t, b = m // BLOCKS, m % BLOCKS
                if b == 0 and h == 0:
                    pe.wait_ge(q4_landed[t % 2], 64 * (2 * c + t // 2 + 1))
                if not (fresh and m == 0 and h < 2):
                    pe.wait_ge(masked_ready, (c * COLS + m) * H + h - 1)
                u = 2 * (h % 2)
                for i in range(BLOCK // CHUNK):
                    at_ = b * BLOCK + i * CHUNK
                    last = pe.matmul(bank[:, u + i, :], parts[:, t % 2, h * P:(h + 1) * P],
                                     k4[:, h, at_:at_ + CHUNK], start=True, stop=True)
                last.then_inc(scores_ready, 1)

            def turn_bank(c, first, use):
                prev, chunks = TURN_BANKS.before(use, first)
                if prev is None:
                    return
                if prev[0] == "unit":
                    k = prev[1] * UPB + prev[2]
                    if prev[2] in VECTOR_UNITS:
                        pe.wait_ge(unit_copied_dve, (c - chunks) * len(BY_VECTOR) + BY_VECTOR.index(k) + 1)
                    else:
                        pe.wait_ge(unit_copied_act, (c - chunks) * len(BY_SCALAR) + BY_SCALAR.index(k) + 1)
                elif prev[0] == "out":
                    pe.wait_ge(rows_dve, TV((c - chunks) * TPC + prev[1] // BLOCKS - 1, "wide"))
                else:
                    pe.wait_ge(att_act, AA(c - chunks - 1, {"x3": "x3_t", "mx": "mx"}[prev[0]]))

            def turn_unit(c, n, u, first):
                if u == 0:
                    pe.wait_ge(exp_ready, (c * COLS + n) * H + H)
                turn_bank(c, first, ("unit", n, u))
                b_ = TURN_BANKS.bank(("unit", n, u))
                for h in range(H):
                    last = pe.transpose(bank[:, b_, h * P:(h + 1) * P], cols[:, n % 4, h, u * P:(u + 1) * P],
                                        ident[:, :])
                last.then_inc(unit_turned, 1)

            def attend(c, k, first):
                n, u = k // UPB, k % UPB
                t, b = n // BLOCKS, n % BLOCKS
                if b == 0 and u == 0 and not (first and t == 0):
                    pe.wait_ge(rows_act, TA(c * TPC + t - 1, "copied"))
                if u in VECTOR_UNITS:
                    pe.wait_ge(unit_copied_dve, c * len(BY_VECTOR) + BY_VECTOR.index(k) + 1)
                else:
                    pe.wait_ge(unit_copied_act, c * len(BY_SCALAR) + BY_SCALAR.index(k) + 1)
                for h in range(H):
                    last = pe.matmul(bank[h * C:(h + 1) * C, 7, b * P:(b + 1) * P],
                                     stat_x[:, b * UPB + u, h * C:(h + 1) * C], turned[:, k % 4, h * P:(h + 1) * P],
                                     start=(u == 0), stop=(u == UPB - 1))
                last.then_inc(unit_used, 1)

            def turn_out(c, t, body_c, first, use):
                pe.wait_ge(rows_act, TA(c * TPC + t, "copied"))
                turn_bank(body_c, first, use)
                turn4(TURN_BANKS.bank(use), o_t).then_inc(rows_pe, 1)

            def turn_x3(c, dst, body_c=None):
                pe.wait_ge(att_dve, AV(c, "x3"))
                if body_c is not None:
                    turn_bank(body_c, False, ("x3",))
                turn4(dst, x3_g).then_inc(att_pe, 1)

            def mobius_product(c, dst, body_c=None):
                pe.wait_ge(att_act, AA(c, "x3_t"))
                if body_c is not None:
                    turn_bank(body_c, False, ("mx",))
                for t in range(TPC):
                    last = pe.matmul(bank[:, dst, t * P:(t + 1) * P], x3_t[:, t * P:(t + 1) * P], whyp[:, :],
                                     start=True, stop=True)
                last.then_inc(att_pe, 1)

            def attention(c, first, last_chunk):
                for n in range(COLS):
                    for u in range(UPB):
                        ahead = head_ahead(c, n, u, SCORE_LEAD, last_chunk)
                        if u % 2 == 0 and ahead:
                            scores(*ahead, False)
                        turn_unit(c, n, u, first)
                        k = n * UPB + u
                        if k >= USE_LAG:
                            attend(c, k - USE_LAG, first)
                        if u == OUT_AT and n % BLOCKS == 0:
                            if n > 0:
                                turn_out(c, n // BLOCKS - 1, c, first, ("out", n))
                            elif not first:
                                turn_out(c - 1, TPC - 1, c, first, ("out", 0))
                        if (n, u) == X3_AT and not first:
                            turn_x3(c - 1, TURN_BANKS.bank(("x3",)), c)
                        if (n, u) == MX_AT and not first:
                            mobius_product(c - 1, TURN_BANKS.bank(("mx",)), c)
                for k in range(COLS * UPB - USE_LAG, COLS * UPB):
                    attend(c, k, first)

            pe.wait_ge(gcn_k4_in, 64 * CHUNKS)
            pe.wait_ge(gcn_dve, CV(CHUNKS - 1, "root"))
            for i in range(SCORE_LEAD):
                scores(0, i // H, i % H, True)
            attention(0, True, False)
            with pe.Fori(1, CHUNKS - 1) as c:
                attention(c, False, False)
            attention(CHUNKS - 1, False, True)

            def turn_u(c):
                pe.wait_ge(hyp_act, HA(c, "agg"))
                turn4(1, agg_t).then_inc(hyp_pe, 1)

            last = CHUNKS - 1

            pe.wait_ge(att_pool, AG(last - 1, "xt"))

            def final_out():
                pe.wait_ge(rows_act, TA(last * TPC + TPC - 1, "copied"))
                turn4(1, o_t).then_inc(rows_pe, 1)

            product(2, 0, {0: [final_out], 2: [lambda: turn_x3(last, 2)], 3: [lambda: mobius_product(last, 3)],
                           6: [lambda: pe.wait_ge(att_pool, AG(last, "xt"))]})
            with pe.Fori(1, CHUNKS) as c:
                pe.wait_ge(hyp_act, HA(c - 1, "agg"))
                product(2, c, {0: [lambda: turn_u(c - 1)]})
            turn_u(last)

        @block.scalar
        def _(act):
            for ap, src in ((wmsg, w_msg), (wih, w_ih), (whh, w_hh), (bmsg, b_msg), (bih, b_ih), (bhh, b_hh),
                            (bq, b_q), (bk, b_k), (wgcn[:, :], w_gcn), (wq[:, :], w_q), (wk[:, :], w_k),
                            (wvs[:, :], w_vs), (whyp[:, :], w_hyp)):
                act.dma_start(ap, src).then_inc(weights_in, 16)
            for ap, src in ((bgcn[:, :], b_gcn), (bvs[:, :], b_vs), (hbias[:, :], b_hyp), (wbo[:, :], w_beta[0:P]),
                            (wbr[:, :], w_beta[P:2 * P]), (wb3, w_beta[2 * P:3 * P])):
                act.dma_start(ap, src.partition_broadcast(P)).then_inc(weights_in, 16)
            act.wait_ge(weights_in, 16 * WEIGHTS)
            act.activation(bias_sq, hbias[:, :], ACT.Square, accum_out=hb[:, 0:1]).then_inc(bias_act, 1)
            act.wait_ge(bias_pool, 2)
            act.activation(hb[:, 2:3], hb[:, 1:2], ACT.Tanh).then_inc(bias_act, 1)
            act.wait_ge(bias_dve, 6)
            act.activation(bias_sq, hbias[:, :], ACT.Square, accum_out=hb[:, 3:4]).then_inc(bias_act, 1)

            def gru(c, first):
                if not first:
                    act.wait_ge(gru_dve, GV(c - 1, "y"))
                    act.wait_ge(gru_x1_out, 16 * c)
                act.dma_start(xt_in, x_t[:, bass.ds(c * CHUNK, CHUNK)]).then_inc(gru_xt_in, 16)
                act.wait_ge(ring_multiplied, (c + 1) * SLOTS)
                act.activation(agg_t, bank[:, 0, :], ACT.Copy).then_inc(gru_act, 1)
                act.wait_ge(gru_pe, GP(c, "msg"))
                act.activation(msg_t, bank[:, 2, :], ACT.Relu, bias=bmsg).then_inc(gru_act, 1)
                act.wait_ge(gru_pe, GP(c, "r"))
                act.activation(r_t, bank[:, 3, :], ACT.Tanh, bias=brz[:, 0:1], scale=0.5).then_inc(gru_act, 1)
                act.wait_ge(gru_pe, GP(c, "z"))
                act.activation(z_t, bank[:, 4, :], ACT.Tanh, bias=brz[:, 1:2], scale=0.5).then_inc(gru_act, 1)
                act.wait_ge(gru_dve, GV(c, "npre"))
                act.activation(n_t, hn_t, ACT.Tanh, bias=bih[:, 2:3]).then_inc(gru_act, 1)
                act.wait_ge(gru_dve, GV(c, "x1"))
                act.dma_start(x1_dram[:, bass.ds(c * CHUNK, CHUNK)], x_new).then_inc(gru_x1_out, 16)
                act.wait_ge(gru_pe, GP(c, "x1_turned"))
                act.activation(x_new_t, bank[:, 7, :], ACT.Copy).then_inc(gru_act, 1)

            gru(0, True)
            with act.Fori(1, CHUNKS) as c:
                gru(c, False)

            def gcn(c, first):
                if not first:
                    act.wait_ge(gcn_dve, CV(c - 1, "y"))
                else:
                    act.wait_ge(gru_x1_out, 16 * CHUNKS)
                act.dma_start(res_in, x1_dram[:, bass.ds(c * CHUNK, CHUNK)]).then_inc(gcn_x1_in, 16)
                act.wait_ge(ring_multiplied, (CHUNKS + c + 1) * SLOTS)
                act.activation(agg1_t, bank[:, 0, :], ACT.Copy).then_inc(gcn_act, 1)
                if not first:
                    store_projections(c - 1)
                act.wait_ge(gcn_dve, CV(c, "x2"))
                act.dma_start(x2_dram[:, bass.ds(c * CHUNK, CHUNK)], x2_new).then_inc(gcn_x2_out, 16)
                act.wait_ge(gcn_pe, CP(c, "x2_turned"))
                act.activation(x2_new_t, bank[:, 7, :], ACT.Copy).then_inc(gcn_act, 1)
                act.wait_ge(gcn_pe, CP(c, "k"))
                if not first:
                    act.wait_ge(gcn_k_out, 64 * c)
                act.activation(k_parts[:, 0, :], bank[:, 4, :], ACT.Identity, bias=bk).then_inc(gcn_act, 1)
                act.wait_ge(gcn_pe, CP(c, "q"))
                if not first:
                    act.wait_ge(gcn_q_out, 64 * c)
                act.activation(q_parts[:, 0, :], bank[:, 7, :], ACT.Identity, bias=bq).then_inc(gcn_act, 1)

            def store_projections(c):
                act.wait_ge(gcn_act, CA(c, "k_hi"))
                act.wait_ge(gcn_dve, CV(c, "k_lo"))
                for g in range(4):
                    act.dma_start(k4_dram[bass.ds(c, 1), g, :, :, :].rearrange("o h c n -> (o h c) n"),
                                  k_parts[:, g % 2, :].bitcast(F32)).then_inc(gcn_k_out, 16)
                act.wait_ge(gcn_act, CA(c, "q_hi"))
                act.wait_ge(gcn_dve, CV(c, "q_lo"))
                for g in range(4):
                    act.dma_start(q4_dram[bass.ds(c, 1), g, :, :, :].rearrange("o h c n -> (o h c) n"),
                                  q_parts[:, g // 2, :].bitcast(F32)).then_inc(gcn_q_out, 16)
                act.wait_ge(gcn_dve, CV(c, "root"))
                act.dma_start(root_dram[:, bass.ds(c * CHUNK, CHUNK)], root_out).then_inc(gcn_root_out, 16)

            gcn(0, True)
            with act.Fori(1, CHUNKS) as c:
                gcn(c, False)
            store_projections(CHUNKS - 1)

            def exponent(c, m, h):
                t, b = m // BLOCKS, m % BLOCKS
                if h == 0:
                    act.wait_ge(shift_ready, c * COLS + m + 1)
                piece = cols[:, m % 4, h, :]
                i = b * H + h
                act.activation(piece, piece, ACT.Exp, bias=shift[:, t % 2, i:i + 1], scale=SCORE_SCALE,
                               accum_out=blocksum[:, t % 2, i:i + 1]).then_inc(exp_ready, 1)

            def copy_unit(c, n, u, first):
                k = n * UPB + u
                act.wait_ge(unit_turned, c * COLS * UPB + k + 1)
                if not (first and k < 4):
                    act.wait_ge(unit_used, c * COLS * UPB + k - 3)
                act.activation(turned[:, k % 4, :], bank[:, TURN_BANKS.bank(("unit", n, u)), :],
                               ACT.Copy).then_inc(unit_copied_act, 1)

            def block_weights(c, t):
                g = c * TPC + t
                act.wait_ge(rows_dve, TV(g, "below"))
                act.activation(mix, mix, ACT.Exp, scale=SCORE_SCALE).then_inc(rows_act, 1)

            def copy_out(c, t):
                g = c * TPC + t
                act.wait_ge(unit_used, (g + 1) * BLOCKS * UPB)
                if not is_zero(g):
                    act.wait_ge(rows_pe, TP(g - 1, "turned"))
                act.activation(o_t, bank[:, 7, :], ACT.Copy).then_inc(rows_act, 1)

            def post_steps(c, x3_bank, mx_bank, wide_free):
                def beta_exp():
                    act.wait_ge(att_dve, AV(c, "zz"))
                    act.activation(ez, zz, ACT.Exp, scale=-1.0).then_inc(att_act, 1)

                def copy_x3():
                    act.wait_ge(att_pe, AP_(c, "x3_turned"))
                    act.wait_ge(rows_dve, TV(wide_free, "out"))
                    act.activation(x3_t, bank[:, x3_bank, :], ACT.Copy).then_inc(att_act, 1)

                def copy_mx():
                    act.wait_ge(att_pe, AP_(c, "mx"))
                    act.activation(mx_g, bank[:, mx_bank, :], ACT.Copy).then_inc(att_act, 1)

                def logs(name):
                    act.wait_ge(att_pool, AG(c, name))
                    act.activation(t1, s3, ACT.Ln, bias=1.0, scale=1.0).then_inc(att_act, 1)
                    act.activation(t2, s3, ACT.Ln, bias=1.0, scale=-1.0).then_inc(att_act, 1)

                def arg_tanh():
                    act.wait_ge(att_pool, AG(c, "arg2"))
                    act.activation(s4, s4, ACT.Tanh).then_inc(att_act, 1)

                return {(3, 3): beta_exp, (6, 6): copy_x3, (7, 6): copy_mx, (9, 7): lambda: logs("xn_min"),
                        (10, 7): arg_tanh, (14, 7): lambda: logs("pn")}

            def attention(c, first, last_chunk):
                post = {} if first else post_steps(c - 1, TURN_BANKS.bank(("x3",)), TURN_BANKS.bank(("mx",)), c * TPC)
                for n in range(COLS):
                    for u in range(UPB):
                        if n % BLOCKS == BLOCKS - 1 and u == 4:
                            block_weights(c, n // BLOCKS)
                        if n % BLOCKS == 0 and u == 2:
                            if n > 0:
                                copy_out(c, n // BLOCKS - 1)
                            elif not first:
                                copy_out(c - 1, TPC - 1)
                        if u not in VECTOR_UNITS:
                            copy_unit(c, n, u, first)
                        ahead = head_ahead(c, n, u, EXP_LEAD, last_chunk)
                        if u % 2 == 1 and ahead:
                            exponent(*ahead)
                        if (n, u) in post:
                            post[(n, u)]()

            for i in range(EXP_LEAD):
                exponent(0, i // H, i % H)
            attention(0, True, False)
            with act.Fori(1, CHUNKS - 1) as c:
                attention(c, False, False)
            attention(CHUNKS - 1, False, True)
            copy_out(CHUNKS - 1, TPC - 1)
            final = post_steps(CHUNKS - 1, 2, 3, TILES - 1)
            for place in sorted(final):
                final[place]()
            act.wait_ge(att_pool, AG(CHUNKS - 1, "xt"))

            def hyperbolic(c, first):
                if first:
                    act.wait_ge(att_x3_out, 16 * CHUNKS)
                else:
                    act.wait_ge(hyp_dve, HV(c - 1, "y"))
                act.dma_start(res_in, x3_dram[:, bass.ds(c * CHUNK, CHUNK)]).then_inc(hyp_in, 16)
                act.wait_ge(ring_multiplied, (2 * CHUNKS + c + 1) * SLOTS)
                act.activation(agg_t, bank[:, 0, :], ACT.Copy).then_inc(hyp_act, 1)
                act.wait_ge(hyp_pe, HP(c, "turned"))
                for t in range(TPC):
                    last = act.activation(y_t[:, t * P:(t + 1) * P], bank[:, 1, t * P:(t + 1) * P], ACT.Square,
                                          accum_out=s1[:, t:t + 1])
                last.then_inc(hyp_act, 1)
                act.wait_ge(hyp_pool, HG(c, "un_max"))
                act.activation(t1, s2, ACT.Tanh).then_inc(hyp_act, 1)
                act.wait_ge(hyp_pool, HG(c, "p"))
                act.activation(t2, s3, ACT.Ln, bias=1.0, scale=1.0).then_inc(hyp_act, 1)
                act.activation(t3, s3, ACT.Ln, bias=1.0, scale=-1.0).then_inc(hyp_act, 1)
                act.wait_ge(hyp_pool, HG(c, "fac"))
                for t in range(TPC):
                    last = act.activation(msg_t[:, t * P:(t + 1) * P], bank[:, 1, t * P:(t + 1) * P], ACT.Relu,
                                          scale=s5[:, t:t + 1])
                last.then_inc(hyp_act, 1)
                act.wait_ge(hyp_act, HA(c, "w"))
                for t in range(TPC):
                    last = act.activation(y_t[:, t * P:(t + 1) * P], msg_t[:, t * P:(t + 1) * P], ACT.Square,
                                          accum_out=s6[:, t:t + 1])
                last.then_inc(hyp_act, 1)
                act.wait_ge(hyp_pool, HG(c, "wn_max"))
                act.activation(t1, s7, ACT.Tanh).then_inc(hyp_act, 1)
                act.wait_ge(hyp_dve, HV(c, "out"))
                act.dma_start(out[:, bass.ds(c * CHUNK, CHUNK)], x_new).then_inc(hyp_out, 16)

            hyperbolic(0, True)
            with act.Fori(1, CHUNKS) as c:
                hyperbolic(c, False)

        @block.vector
        def _(dve):
            def row_stats(src, sem_):
                for t in range(TPC):
                    last = dve.bn_stats(bn6[:, 6 * t:6 * t + 6], src[:, t * P:(t + 1) * P])
                last.then_inc(sem_, 1)

            def mean_and_var(sem_, st, c):
                dve.wait_ge(sem_, st(c, "bn6"))
                dve.nop(nofuse=True)
                for t in range(TPC):
                    last = dve.bn_aggr(mean_var[:, t, :], bn6[:, 6 * t:6 * t + 6])
                last.then_inc(sem_, 1)

            def norm_stats(src, sem_, st, c):
                row_stats(src, sem_)
                mean_and_var(sem_, st, c)

            def normalise(dst, src):
                for t in range(TPC):
                    last = dve.tensor_scalar(dst[:, t * P:(t + 1) * P], src[:, t * P:(t + 1) * P],
                                             mean_var[:, t, 0:1], rstd[:, t:t + 1], ALU.subtract, ALU.mult)
                return last

            dve.wait_ge(weights_in, 16 * WEIGHTS)
            dve.tensor_tensor(wbo[:, :], wbo[:, :], wb3, ALU.add).then_inc(bias_dve, 1)
            dve.tensor_tensor(wbr[:, :], wbr[:, :], wb3, ALU.subtract).then_inc(bias_dve, 1)
            dve.tensor_tensor(brz, bih[:, 0:2], bhh[:, 0:2], ALU.add).then_inc(bias_dve, 1)
            dve.wait_ge(bias_dve, 3)
            dve.tensor_scalar(brz, brz, 0.5, None, ALU.mult).then_inc(bias_dve, 1)
            dve.wait_ge(bias_pool, 3)
            dve.wait_ge(bias_act, 2)
            dve.tensor_scalar(hb[:, 2:3], hb[:, 2:3], MAX_NORM, hb[:, 0:1], ALU.min, ALU.mult).then_inc(bias_dve, 1)
            dve.wait_ge(bias_dve, 5)
            dve.tensor_scalar(hbias[:, :], hbias[:, :], hb[:, 2:3], None, ALU.mult).then_inc(bias_dve, 1)

            def sum_slot(c, s, fresh):
                dve.wait_ge(ring_landed[s], 16 * (c + 1))
                lo = ring[:, s, 0:2, :].rearrange("p j i -> p (j i)")
                hi = ring[:, s, 2:4, :].rearrange("p j i -> p (j i)")
                if s == 0:
                    if not fresh:
                        dve.wait_ge(gru_pe, GP(c - 1, "degree"))
                    dve.tensor_tensor(colsum, lo, hi, ALU.add).then_inc(ring_summed, 1)
                else:
                    dve.wait_ge(ring_summed, c * SLOTS + s)
                    dve.tensor_tensor(colsum, colsum, lo, ALU.add).then_inc(half_summed, 1)
                    dve.wait_ge(half_summed, c * (SLOTS - 1) + s)
                    dve.tensor_tensor(colsum, colsum, hi, ALU.add).then_inc(ring_summed, 1)

            def gru_steps(c):
                def degree():
                    dve.wait_ge(gru_pe, GP(c, "degree"))
                    dve.tensor_scalar(deg, bank[:, 7, 0:4], 1.0, None, ALU.add).then_inc(gru_dve, 1)
                    dve.wait_ge(gru_dve, GV(c, "degree"))
                    dve.tensor_scalar(deg_on, deg, 0.0, None, ALU.is_gt).then_inc(gru_dve, 1)

                def gate():
                    dve.wait_ge(gru_pe, GP(c, "n_hid"))
                    dve.tensor_scalar(hn_t, bank[:, 6, :], bhh[:, 2:3], 0.5, ALU.add, ALU.mult).then_inc(gru_dve, 1)
                    dve.wait_ge(gru_dve, GV(c, "hn"))
                    dve.wait_ge(gru_act, GA(c, "r"))
                    dve.scalar_tensor_tensor(hn_t, r_t, 1.0, hn_t, ALU.add, ALU.mult).then_inc(gru_dve, 1)
                    dve.wait_ge(gru_dve, GV(c, "rhn"))
                    dve.tensor_tensor(hn_t, bank[:, 5, :], hn_t, ALU.add).then_inc(gru_dve, 1)

                def blend():
                    dve.wait_ge(gru_act, GA(c, "n"))
                    dve.tensor_tensor(y_t, xt_in, n_t, ALU.subtract).then_inc(gru_dve, 1)
                    dve.wait_ge(gru_dve, GV(c, "diff"))
                    dve.scalar_tensor_tensor(y_t, z_t, 1.0, y_t, ALU.add, ALU.mult).then_inc(gru_dve, 1)
                    dve.wait_ge(gru_dve, GV(c, "zdiff"))
                    dve.scalar_tensor_tensor(y_t, y_t, 0.5, n_t, ALU.mult, ALU.add).then_inc(gru_dve, 1)
                    dve.wait_ge(gru_dve, GV(c, "nz"))
                    dve.tensor_tensor(y_t, y_t, xt_in, ALU.add).then_inc(gru_dve, 1)

                def stats():
                    dve.wait_ge(gru_pe, GP(c, "y_turned"))
                    norm_stats(bank[:, 7, :], gru_dve, GV, c)

                def norm():
                    dve.wait_ge(gru_pool, GG(c, "rstd"))
                    normalise(x_new, bank[:, 7, :]).then_inc(gru_dve, 1)

                def scale():
                    dve.wait_ge(gru_pool, GG(c, "deg_pow"))
                    dcol = dinv[:, bass.ds(c * TPC, TPC)]
                    dve.tensor_tensor(dcol, deg, deg_on, ALU.mult).then_inc(gru_dve, 1)
                    dve.wait_ge(gru_dve, GV(c, "dinv"))
                    dve.wait_ge(gru_pe, GP(c, "support"))
                    dve.tensor_tensor(stat_s[:, bass.ds(c * TPC, TPC), :], tiles(bank[:, 1, :]),
                                      dcol.unsqueeze(2).to_broadcast([P, TPC, P]), ALU.mult).then_inc(gru_dve, 1)

                return {0: [degree], 2: [gate, blend], 4: [stats], 5: [norm], 7: [scale]}

            def sums(c, fresh, steps):
                for s in range(SLOTS):
                    sum_slot(c, s, fresh)
                    for step in steps.get(s, ()):
                        step()

            sums(0, True, {})
            with dve.Fori(1, CHUNKS) as c:
                sums(c, False, gru_steps(c - 1))
            last_steps = gru_steps(CHUNKS - 1)
            for s in sorted(last_steps):
                for step in last_steps[s]:
                    step()

            def gcn(c):
                dve.wait_ge(gcn_pe, CP(c, "turned"))
                dve.tensor_tensor(tiles(y_n), tiles(bank[:, 7, :]), stat_s[:, bass.ds(c * TPC, TPC), :],
                                  ALU.add).then_inc(gcn_dve, 1)
                dve.tensor_copy(deg, dinv[:, bass.ds(c * TPC, TPC)]).then_inc(gcn_dve, 1)
                dve.wait_ge(gcn_dve, CV(c, "dinv"))
                dve.wait_ge(gcn_pool, CG(c, "x1_bias"))
                for t in range(TPC):
                    s_ = slice(t * P, (t + 1) * P)
                    last = dve.scalar_tensor_tensor(y_n[:, s_], y_n[:, s_], deg[:, t:t + 1], res_in[:, s_],
                                                    ALU.mult, ALU.add)
                last.then_inc(gcn_dve, 1)
                dve.wait_ge(gcn_dve, CV(c, "y"))
                norm_stats(y_n, gcn_dve, CV, c)
                dve.wait_ge(gcn_pool, CG(c, "rstd"))
                if not is_zero(c):
                    dve.wait_ge(gcn_x2_out, 16 * c)
                normalise(x2_new, y_n).then_inc(gcn_dve, 1)
                dve.wait_ge(gcn_act, CA(c, "k_hi"))
                dve.scalar_tensor_tensor(k_parts[:, 1, :], bank[:, 4, :], bk, k_parts[:, 0, :].bitcast(F32), ALU.add,
                                         ALU.subtract).then_inc(gcn_dve, 1)
                dve.wait_ge(gcn_act, CA(c, "q_hi"))
                dve.scalar_tensor_tensor(q_parts[:, 1, :], bank[:, 7, :], bq, q_parts[:, 0, :].bitcast(F32), ALU.add,
                                         ALU.subtract).then_inc(gcn_dve, 1)
                dve.wait_ge(gcn_pe, CP(c, "vs"))
                both = bank[:, 5:7, :].rearrange("p b (t k f) -> p (b t) k f", t=2, k=2)
                for k, dst in ((0, stat_x[:, bass.ds(c * TPC, TPC), :]), (1, tiles(root_out))):
                    if k == 1 and not is_zero(c):
                        dve.wait_ge(gcn_root_out, 16 * c)
                    dve.tensor_tensor(dst, both[:, :, k, :], per_tile(bvs[:, k * P:(k + 1) * P]),
                                      ALU.add).then_inc(gcn_dve, 1)

            gcn(0)
            with dve.Fori(1, CHUNKS) as c:
                gcn(c)

            def mask(c, m, h, first):
                t, b = m // BLOCKS, m % BLOCKS
                if h == 0:
                    dve.wait_ge(bias_ready, c * COLS + m + 1)
                    if not (first and m < 4):
                        dve.wait_ge(unit_turned, (c * COLS + m - 3) * UPB)
                dve.wait_ge(scores_ready, (c * COLS + m) * H + h + 1)
                dve.nop(nofuse=True)
                i = b * H + h
                dve.tensor_tensor_reduce(out=cols[:, m % 4, h, :],
                                         in0=bank[:, 2 * (h % 2):2 * (h % 2) + 2, :].rearrange("p b n -> p (b n)"),
                                         in1=maskbias[m % 4], scale=1.0, scalar=LOWEST, op0=ALU.add,
                                         op1=ALU.max, accum_out=blockmax[:, t % 2, i:i + 1]).then_inc(masked_ready, 1)
                if h == H - 1:
                    dve.wait_ge(masked_ready, (c * COLS + m) * H + H)
                    dve.tensor_scalar(shift[:, t % 2, b * H:(b + 1) * H], blockmax[:, t % 2, b * H:(b + 1) * H],
                                      -SCORE_SCALE, None, ALU.mult).then_inc(shift_ready, 1)

            def copy_unit(c, n, u, first):
                k = n * UPB + u
                dve.wait_ge(unit_turned, c * COLS * UPB + k + 1)
                if not (first and k < 4):
                    dve.wait_ge(unit_used, c * COLS * UPB + k - 3)
                dve.tensor_copy(turned[:, k % 4, :], bank[:, TURN_BANKS.bank(("unit", n, u)), :]).then_inc(unit_copied_dve, 1)

            def below_max(c, t):
                g = c * TPC + t
                bm = blockmax[:, t % 2, :].rearrange("p (b h) -> p b h", h=H)
                dve.wait_ge(masked_ready, (g + 1) * BLOCKS * H)
                dve.tensor_reduce(rowmax, bm.rearrange("p b h -> p h b"), AX.X, ALU.max).then_inc(rows_dve, 1)
                dve.wait_ge(rows_dve, TV(g, "rowmax"))
                dve.tensor_tensor(mix.rearrange("p (b h) -> p b h", h=H), bm,
                                  rowmax.unsqueeze(1).to_broadcast([P, BLOCKS, H]), ALU.subtract).then_inc(rows_dve, 1)

            def weigh(c, t, b_):
                g = c * TPC + t
                dve.wait_ge(rows_pool, TG(g, "mix"))
                dve.wait_ge(rows_pe, TP(g, "turned"))
                dve.tensor_tensor(wide.rearrange("p (k f) -> p k f", f=C), bank[:, b_, :].rearrange("p (k f) -> p k f", f=C),
                                  mix.unsqueeze(2).to_broadcast([P, BLOCKS * H, C]), ALU.mult).then_inc(rows_dve, 1)

            def add_blocks(c, t):
                g = c * TPC + t
                dve.wait_ge(rows_dve, TV(g, "wide"))
                dve.tensor_reduce(o_n[:, t * P:(t + 1) * P].rearrange("p (f h) -> p h f", h=H),
                                  wide.rearrange("p (b h f) -> p h f b", b=BLOCKS, h=H), AX.X,
                                  ALU.add).then_inc(rows_dve, 1)

            def post_steps(c):
                def beta_logit():
                    dve.wait_ge(att_pool, AG(c, "z"))
                    dve.tensor_reduce(zz, tiles(y_g), AX.X, ALU.add).then_inc(att_dve, 1)

                def gate():
                    dve.wait_ge(att_act, AA(c, "ez"))
                    dve.tensor_scalar(ez, ez, 1.0, None, ALU.add).then_inc(att_dve, 1)
                    dve.wait_ge(att_dve, AV(c, "one_ez"))
                    dve.reciprocal(beta, ez).then_inc(att_dve, 1)

                def stats():
                    dve.wait_ge(att_pool, AG(c, "y"))
                    row_stats(y_g, att_dve)

                def norm():
                    dve.wait_ge(att_pool, AG(c, "rstd"))
                    normalise(x3_g, y_g).then_inc(att_dve, 1)

                def norm_x3():
                    dve.wait_ge(att_pool, AG(c, "x3sq"))
                    dve.tensor_reduce(xx, tiles(y_g), AX.X, ALU.add).then_inc(att_dve, 1)

                def norm_mx():
                    dve.wait_ge(att_pool, AG(c, "mxsq"))
                    dve.tensor_reduce(mm, tiles(y_g), AX.X, ALU.add).then_inc(att_dve, 1)

                def bias_mx():
                    dve.wait_ge(att_pool, AG(c, "mxhb"))
                    dve.tensor_reduce(mh, tiles(root_g), AX.X, ALU.add).then_inc(att_dve, 1)

                def norm_h():
                    dve.wait_ge(att_pool, AG(c, "hsq"))
                    dve.tensor_reduce(hh, tiles(y_g), AX.X, ALU.add).then_inc(att_dve, 1)

                return {(2, 5): beta_logit, (3, 5): gate, (4, 7): stats,
                        (5, 1): lambda: mean_and_var(att_dve, AV, c), (6, 3): norm, (7, 3): norm_x3,
                        (8, 5): norm_mx, (9, 1): bias_mx, (13, 5): norm_h}

            def attention(c, first, last_chunk):
                post = post_steps(c - 1) if not first else {}
                for n in range(COLS):
                    for u in range(UPB):
                        ahead = head_ahead(c, n, u, MASK_LEAD, last_chunk)
                        if u % 2 == 0 and ahead:
                            mask(*ahead, first and n < COLS - BLOCKS)
                        if u in VECTOR_UNITS:
                            copy_unit(c, n, u, first)
                        if n % BLOCKS == 0 and not (first and n == 0):
                            done = (c, n // BLOCKS - 1) if n > 0 else (c - 1, TPC - 1)
                            if u == 6:
                                weigh(*done, TURN_BANKS.bank(("out", n)))
                        if n % BLOCKS == 1 and u == 1 and not (first and n == 1):
                            done = (c, n // BLOCKS - 1) if n > 1 else (c - 1, TPC - 1)
                            add_blocks(*done)
                        if n % BLOCKS == BLOCKS - 1 and u == 1:
                            below_max(c, n // BLOCKS)
                        if (n, u) in post:
                            post[(n, u)]()

            dve.wait_ge(ring_multiplied, 2 * CHUNKS * SLOTS)
            dve.wait_ge(bias_dve, 6)
            for i in range(MASK_LEAD):
                mask(0, i // H, i % H, True)
            attention(0, True, False)
            with dve.Fori(1, CHUNKS - 1) as c:
                attention(c, False, False)
            attention(CHUNKS - 1, False, True)
            weigh(CHUNKS - 1, TPC - 1, 1)
            add_blocks(CHUNKS - 1, TPC - 1)
            final = post_steps(CHUNKS - 1)
            for place in sorted(final):
                final[place]()

            def hyperbolic(c):
                dve.wait_ge(hyp_pool, HG(c, "fh"))
                dve.tensor_tensor(y_n, msg_t, res_in, ALU.add).then_inc(hyp_dve, 1)
                dve.wait_ge(hyp_dve, HV(c, "y"))
                norm_stats(y_n, hyp_dve, HV, c)
                dve.wait_ge(hyp_pool, HG(c, "rstd"))
                if not is_zero(c):
                    dve.wait_ge(hyp_out, 16 * c)
                normalise(x_new, y_n).then_inc(hyp_dve, 1)

            hyperbolic(0)
            with dve.Fori(1, CHUNKS) as c:
                hyperbolic(c)

        @block.gpsimd
        def _(pool):
            pool.memset(ones, 1.0).then_inc(consts_set, 1)
            pool.memset(minus_half, -0.5).then_inc(consts_set, 1)
            pool.memset(half, 0.5).then_inc(consts_set, 1)
            pool.memset(minus_one, -1.0).then_inc(consts_set, 1)
            pool.memset(ident[:, :], 0.0).then_inc(consts_set, 1)
            pool.wait_ge(consts_set, 5)
            pool.affine_select(out=ident[:, :], in_=ident[:, :], compare_op=ALU.not_equal, fill=1.0, base=0,
                               pattern=[[-1, P]], channel_multiplier=1).then_inc(consts_set, 1)
            pool.wait_ge(bias_act, 1)
            pool.tensor_tensor(hb[:, 1:2], hb[:, 0:1], half[:, 0:1], ALU.pow).then_inc(bias_pool, 1)
            pool.wait_ge(bias_pool, 1)
            pool.tensor_scalar(hb[:, 1:2], hb[:, 1:2], MIN_NORM, None, ALU.max).then_inc(bias_pool, 1)
            pool.wait_ge(bias_pool, 2)
            pool.tensor_tensor(hb[:, 0:1], hb[:, 1:2], minus_one[:, 0:1], ALU.pow).then_inc(bias_pool, 1)

            def stage(sem_, st):
                def step(c, name, ins):
                    ins.then_inc(sem_, 1)
                    pool.wait_ge(sem_, st(c, name))
                    pool.nop(nofuse=True)
                return step

            def rsqrt_var(c, step):
                pool.nop(nofuse=True)
                step(c, "eps", pool.tensor_scalar(rstd, mean_var[:, :, 1], LN_EPS, None, ALU.add))
                step(c, "rstd", pool.tensor_tensor(rstd, rstd, minus_half, ALU.pow))

            def gru(c):
                step = stage(gru_pool, GG)
                pool.wait_ge(gru_dve, GV(c, "deg_on"))
                pool.nop(nofuse=True)
                step(c, "deg_max", pool.tensor_scalar(deg, deg, 1e-30, None, ALU.max))
                step(c, "deg_pow", pool.tensor_tensor(deg, deg, minus_half, ALU.pow))
                pool.wait_ge(gru_dve, GV(c, "bn"))
                rsqrt_var(c, step)

            gru(0)
            with pool.Fori(1, CHUNKS) as c:
                gru(c)

            def gcn(c):
                step = stage(gcn_pool, CG)
                pool.wait_ge(gcn_x1_in, 16 * (c + 1))
                step(c, "x1_bias", pool.tensor_tensor(tiles(res_in), tiles(res_in), per_tile(bgcn[:, :]), ALU.add))
                pool.wait_ge(gcn_dve, CV(c, "bn"))
                rsqrt_var(c, step)

            def load_k4(c):
                pool.wait_ge(gcn_k_out, 64 * (c + 1))
                for g in range(4):
                    pool.dma_start(k4[g * C:(g + 1) * C, :, bass.ds(c * CHUNK, CHUNK)].bitcast(F32),
                                   k4_dram[bass.ds(c, 1), g, :, :, :].rearrange("o h c n -> (o c) h n")
                                   ).then_inc(gcn_k4_in, 16)

            gcn(0)
            with pool.Fori(1, CHUNKS) as c:
                gcn(c)
                load_k4(c - 1)
            load_k4(CHUNKS - 1)

            def mask_bias(c, m, first):
                pool.wait_ge(adj_landed[m % 2], 16 * (c * COLS // 2 + m // 2 + 1))
                if not (first and m < 4):
                    pool.wait_ge(masked_ready, (c * COLS + m - 3) * H)
                pool.nop(nofuse=True)
                pool.tensor_scalar(maskbias[m % 4], adj_in[:, m % 2, :], 0.0, MASKED, ALU.is_equal,
                                   ALU.mult).then_inc(bias_ready, 1)

            def post_steps(c):
                step = stage(att_pool, AG)

                def tt(name, out_, a, b, op):
                    step(c, name, pool.tensor_tensor(out_, a, b, op))

                def ts(name, out_, a, x, op, y=None, op2=None):
                    if op2 is None:
                        step(c, name, pool.tensor_scalar(out_, a, x, None, op))
                    else:
                        step(c, name, pool.tensor_scalar(out_, a, x, y, op, op2))

                def beta_terms():
                    pool.wait_ge(rows_dve, TV(c * TPC + TPC - 1, "out"))
                    pool.wait_ge(att_in, 32 * (c + 1))
                    tt("zo", tiles(y_g), tiles(o_n), per_tile(wbo[:, :]), ALU.mult)
                    tt("zr", tiles(mx_g), tiles(root_g), per_tile(wbr[:, :]), ALU.mult)
                    tt("z", y_g, y_g, mx_g, ALU.add)

                def residual_terms():
                    tt("diff", root_g, root_g, o_n, ALU.subtract)
                    tt("sum", x2_g, x2_g, o_n, ALU.add)

                def blend():
                    pool.wait_ge(att_dve, AV(c, "beta"))
                    tt("root_b", tiles(root_g), tiles(root_g), beta.unsqueeze(2).to_broadcast([P, TPC, P]), ALU.mult)
                    tt("y", y_g, root_g, x2_g, ALU.add)

                def rs():
                    pool.wait_ge(att_dve, AV(c, "bn"))
                    rsqrt_var(c, step)

                def x3sq():
                    pool.wait_ge(att_dve, AV(c, "x3"))
                    tt("x3sq", y_g, x3_g, x3_g, ALU.mult)

                def mx_terms():
                    pool.wait_ge(att_act, AA(c, "mx"))
                    pool.wait_ge(att_dve, AV(c, "xx"))
                    tt("mxsq", y_g, mx_g, mx_g, ALU.mult)
                    tt("mxhb", tiles(root_g), tiles(mx_g), per_tile(hbias[:, :]), ALU.mult)

                def norms():
                    pool.wait_ge(att_dve, AV(c, "mh"))
                    tt("xn", s1, xx, half, ALU.pow)
                    ts("xn_max", s1, s1, MIN_NORM, ALU.max)
                    tt("mn", s2, mm, half, ALU.pow)
                    ts("mn_max", s2, s2, MIN_NORM, ALU.max)
                    ts("xn_min", s3, s1, ARTANH_MAX, ALU.min)

                def argument():
                    pool.wait_ge(att_act, AA(c, "ln_b"))
                    tt("a", t1, t1, t2, ALU.subtract)
                    ts("a_half", t1, t1, 0.5, ALU.mult)
                    tt("xn_inv", s4, s1, minus_one, ALU.pow)
                    tt("arg", s4, s4, s2, ALU.mult)
                    tt("arg2", s4, s4, t1, ALU.mult)

                def coefficients():
                    pool.wait_ge(att_act, AA(c, "tanh"))
                    pool.nop(nofuse=True)
                    ts("g_min", s4, s4, MAX_NORM, ALU.min)
                    tt("mn_inv", s5, s2, minus_one, ALU.pow)
                    tt("g", s4, s4, s5, ALU.mult)
                    tt("g2", s5, s4, s4, ALU.mult)
                    tt("x2", s5, s5, mm, ALU.mult)
                    tt("xy", s6, s4, mh, ALU.mult)
                    ts("xy2", s6, s6, 2.0, ALU.mult, 1.0, ALU.add)
                    ts("x2y2", s7, s5, hb[:, 3:4], ALU.mult)
                    tt("den", s7, s7, s6, ALU.add)
                    ts("den_max", s7, s7, MIN_NORM, ALU.max)
                    tt("den_inv", s3, s7, minus_one, ALU.pow)
                    ts("a_num", s6, s6, hb[:, 3:4], ALU.add)
                    tt("a_g", s6, s6, s4, ALU.mult)
                    tt("A", s6, s6, s3, ALU.mult)
                    ts("b_num", s7, s5, -1.0, ALU.mult, 1.0, ALU.add)
                    tt("B", s7, s7, s3, ALU.mult)

                def mobius_sum():
                    tt("bias_b", tiles(root_g), per_tile(hbias[:, :]), s7.unsqueeze(2).to_broadcast([P, TPC, P]),
                       ALU.mult)
                    tt("mx_a", tiles(mx_g), tiles(mx_g), s6.unsqueeze(2).to_broadcast([P, TPC, P]), ALU.mult)
                    tt("h", mx_g, mx_g, root_g, ALU.add)
                    tt("hsq", y_g, mx_g, mx_g, ALU.mult)

                def norms_h():
                    pool.wait_ge(att_dve, AV(c, "hh"))
                    tt("hn", s1, hh, half, ALU.pow)
                    ts("hn_max", s1, s1, MIN_NORM, ALU.max)
                    ts("pn", s3, s1, MAX_NORM, ALU.min)

                def factor():
                    pool.wait_ge(att_act, AA(c, "ln_d"))
                    tt("fa", t1, t1, t2, ALU.subtract)
                    ts("fa_half", t1, t1, 0.5, ALU.mult)
                    tt("hn_inv", s1, s1, minus_one, ALU.pow)
                    tt("fac", s1, s1, t1, ALU.mult)
                    tt("xt", stat_s[:, bass.ds(c * TPC, TPC), :], tiles(mx_g), s1.unsqueeze(2).to_broadcast([P, TPC, P]),
                       ALU.mult)

                return {3: beta_terms, 5: residual_terms, 8: blend, 10: rs, 13: x3sq, 16: mx_terms, 18: norms,
                        20: argument, 22: coefficients, 24: mobius_sum, 28: norms_h, 31: factor}

            def block_mix(c, t):
                g = c * TPC + t
                step = stage(rows_pool, TG)
                pool.wait_ge(rows_act, TA(g, "weights"))
                pool.wait_ge(exp_ready, (g + 1) * BLOCKS * H)
                step(g, "wsum", pool.tensor_tensor(mix2, mix, blocksum[:, t % 2, :], ALU.mult))
                step(g, "pair", pool.tensor_tensor(mix2[:, 0:2 * H], mix2[:, 0:2 * H], mix2[:, 2 * H:4 * H], ALU.add))
                step(g, "rowsum", pool.tensor_tensor(rowsum, mix2[:, 0:H], mix2[:, H:2 * H], ALU.add))
                step(g, "noedge", pool.tensor_scalar(noedge, rowsum, 0.0, None, ALU.is_equal))
                step(g, "guard", pool.tensor_tensor(rowsum, rowsum, noedge, ALU.add))
                step(g, "recip", pool.tensor_tensor(rrow, rowsum, minus_one, ALU.pow))
                step(g, "mix", pool.tensor_tensor(mix.rearrange("p (b h) -> p b h", h=H),
                                                  mix.rearrange("p (b h) -> p b h", h=H),
                                                  rrow.unsqueeze(1).to_broadcast([P, BLOCKS, H]), ALU.mult))

            pool.wait_ge(bias_dve, 6)
            pool.wait_ge(bias_act, 3)

            def attention(c, first, last_chunk):
                post = post_steps(c - 1) if not first else {}
                for n in range(COLS):
                    for half_ in range(2):
                        if half_ == 1:
                            ahead = n + BIAS_LEAD
                            if ahead < COLS:
                                mask_bias(c, ahead, first)
                            elif not last_chunk:
                                mask_bias(c + 1, ahead - COLS, False)
                        if half_ == 1 and n % BLOCKS == BLOCKS - 1:
                            block_mix(c, n // BLOCKS)
                        if 2 * n + half_ in post:
                            post[2 * n + half_]()

            for m in range(BIAS_LEAD):
                mask_bias(0, m, True)
            attention(0, True, False)
            with pool.Fori(1, CHUNKS - 1) as c:
                attention(c, False, False)
            attention(CHUNKS - 1, False, True)
            final = post_steps(CHUNKS - 1)
            for slot in sorted(final):
                final[slot]()

            def hyperbolic(c):
                step = stage(hyp_pool, HG)
                pool.wait_ge(hyp_act, HA(c, "uu"))
                step(c, "un", pool.tensor_tensor(s2, s1, half, ALU.pow))
                step(c, "un_max", pool.tensor_scalar(s2, s2, MIN_NORM, None, ALU.max))
                pool.wait_ge(hyp_act, HA(c, "tanh"))
                pool.nop(nofuse=True)
                step(c, "p", pool.tensor_scalar(s3, t1, MAX_NORM, None, ALU.min))
                step(c, "un_inv", pool.tensor_tensor(s5, s2, minus_one, ALU.pow))
                pool.wait_ge(hyp_act, HA(c, "ln_b"))
                pool.tensor_tensor(t2, t2, t3, ALU.subtract).then_inc(hyp_sub, 1)
                pool.wait_ge(hyp_sub, 2 * c + 1)
                pool.nop(nofuse=True)
                pool.tensor_scalar(t2, t2, 0.5, None, ALU.mult).then_inc(hyp_sub, 1)
                pool.wait_ge(hyp_sub, 2 * c + 2)
                step(c, "fac", pool.tensor_tensor(s5, s5, t2, ALU.mult))
                pool.wait_ge(hyp_act, HA(c, "ww"))
                step(c, "wn", pool.tensor_tensor(s7, s6, half, ALU.pow))
                step(c, "wn_max", pool.tensor_scalar(s7, s7, MIN_NORM, None, ALU.max))
                pool.wait_ge(hyp_act, HA(c, "tanh2"))
                pool.nop(nofuse=True)
                step(c, "p2", pool.tensor_scalar(t1, t1, MAX_NORM, None, ALU.min))
                step(c, "wn_inv", pool.tensor_tensor(s7, s7, minus_one, ALU.pow))
                step(c, "f2", pool.tensor_tensor(s7, s7, t1, ALU.mult))
                pool.wait_ge(hyp_in, 16 * (c + 1))
                step(c, "fh", pool.tensor_tensor(tiles(msg_t), tiles(msg_t), s7.unsqueeze(2).to_broadcast([P, TPC, P]),
                                                 ALU.mult))
                pool.wait_ge(hyp_dve, HV(c, "bn"))
                rsqrt_var(c, step)

            hyperbolic(0)
            with pool.Fori(1, CHUNKS) as c:
                hyperbolic(c)


def kernel(x, adj, L0_gnn_W_msg, L0_gnn_b_msg, L0_gnn_W_ih, L0_gnn_W_hh, L0_gnn_b_ih, L0_gnn_b_hh,
           L1_gnn_weight, L1_gnn_bias, L2_gnn_Wq, L2_gnn_bq, L2_gnn_Wk, L2_gnn_bk, L2_gnn_Wv, L2_gnn_bv,
           L2_gnn_Ws, L2_gnn_bs, L2_gnn_Wb, L3_gnn_weight, L3_gnn_bias):
    import numpy as np
    import concourse.bacc as bacc
    from concourse.bass_utils import run_bass_kernel_spmd

    def a(v):
        return np.asarray(v)

    arrays = {
        "adj_cols": a(adj).reshape(CHUNKS, CHUNK, SLOTS, JPS, P).transpose(0, 2, 4, 3, 1).reshape(
            CHUNKS, SLOTS, P, JPS * CHUNK),
        "adj": a(adj),
        "x_tiles": a(x).reshape(TILES, P, P).transpose(1, 0, 2).reshape(P, TILES * P),
        "x_t": a(x).T,
        "w_msg": a(L0_gnn_W_msg).T, "b_msg": a(L0_gnn_b_msg).reshape(P, 1),
        "w_ih": a(L0_gnn_W_ih).T, "w_hh": a(L0_gnn_W_hh).T,
        "b_ih": a(L0_gnn_b_ih).reshape(3, P).T, "b_hh": a(L0_gnn_b_hh).reshape(3, P).T,
        "w_gcn": a(L1_gnn_weight), "b_gcn": a(L1_gnn_bias),
        "w_q": a(L2_gnn_Wq), "b_q": a(L2_gnn_bq).reshape(P, 1),
        "w_k": a(L2_gnn_Wk), "b_k": a(L2_gnn_bk).reshape(P, 1),
        "w_vs": np.concatenate([a(L2_gnn_Wv), a(L2_gnn_Ws)], axis=1),
        "b_vs": np.concatenate([a(L2_gnn_bv), a(L2_gnn_bs)]),
        "w_beta": a(L2_gnn_Wb).reshape(3 * P),
        "w_hyp": a(L3_gnn_weight).T, "b_hyp": a(L3_gnn_bias),
    }
    arrays = {name: np.ascontiguousarray(v) for name, v in arrays.items()}
    nc = bacc.Bacc("TRN2", target_bir_lowering=False, num_devices=1)
    args = {name: nc.dram_tensor(name, v.shape, F32, kind="ExternalInput").ap() for name, v in arrays.items()}
    out = nc.dram_tensor("out", (P, TILES * P), F32, kind="ExternalOutput").ap()
    build_program(nc, out=out, **args)
    result = run_bass_kernel_spmd(nc, [arrays], core_ids=[0])
    return result.results[0]["out"].reshape(P, TILES, P).transpose(1, 0, 2).reshape(N, P)
```

```python
from contextlib import ExitStack

import concourse.bass as bass
from concourse import mybir

F32 = mybir.dt.float32
F32R = mybir.dt.float32r
BF16 = mybir.dt.bfloat16
ALU = mybir.AluOpType
ACT = mybir.ActivationFunctionType
AX = mybir.AxisListType

P = 128
N = 4096
CONSTS = 6
WEIGHTS = 19
TILES = N // P
CHUNK = 512
CHUNKS = N // CHUNK
TPC = CHUNK // P
SLOTS = 8
JPS = TILES // SLOTS
H, C = 4, 32
BLOCK = 1024
BLOCKS = N // BLOCK
COLS = TPC * BLOCKS
UPB = BLOCK // P
SCORE_SCALE = 1.0 / float(C) ** 0.5
MASKED = -1.0e30
LOWEST = -1.0e20
LN_EPS = 1e-5
EXP_AND_LN = "natural_log_exp_and_others"
MIN_NORM = 1e-15
MAX_NORM = 1.0 - 0.004
ARTANH_MAX = 1.0 - 1e-7
VECTOR_UNITS = [(n, u) for n in range(COLS) for u in range(0, UPB, 2) if (n % BLOCKS, u) not in ((0, 6), (1, 0))]
SCORE_LEAD = 11
MASK_LEAD = 10
EXP_LEAD = 6
BIAS_LEAD = 6
USE_LAG = 3
MIX_COLUMN = 2
OUT_AT = 5
X3_AT = (6, 5)
MX_AT = (7, 5)


def is_zero(c):
    return isinstance(c, int) and c == 0


def head_ahead(c, n, u, lead, last_chunk):
    i = n * H + u // 2 + lead
    if i < COLS * H:
        return c, i // H, i % H
    return None if last_chunk else (c + 1, i // H - COLS, i % H)


class Steps:

    def __init__(self, *names):
        self.names = names

    def __call__(self, c, name):
        return c * len(self.names) + self.names.index(name) + 1


class TurnBanks:

    BANKS = (4, 5, 6)

    def __init__(self):
        self.uses = []
        for n in range(COLS):
            for u in range(UPB):
                self.uses.append(("unit", n, u))
                if u == OUT_AT and n % BLOCKS == 0:
                    self.uses.append(("out", n))
                if (n, u) == X3_AT:
                    self.uses.append(("x3",))
                if (n, u) == MX_AT:
                    self.uses.append(("mx",))
        while len(self.uses) % len(self.BANKS):
            self.uses.append(None)

    def bank(self, use):
        return self.BANKS[self.uses.index(use) % len(self.BANKS)]

    def before(self, use, first):
        i = self.uses.index(use) - len(self.BANKS)
        while i >= 0:
            if self.uses[i] and not (first and self.uses[i] in (("out", 0), ("x3",), ("mx",))):
                return self.uses[i], 0
            i -= len(self.BANKS)
        if first:
            return None, 0
        i += len(self.uses)
        while not self.uses[i]:
            i -= len(self.BANKS)
        return self.uses[i], 1


TURN_BANKS = TurnBanks()
LAST_BLOCK_CHUNK = CHUNKS - BLOCK // CHUNK
UNITS = [(n, u) for n in range(COLS) for u in range(UPB)]
BY_VECTOR = [n * UPB + u for n, u in UNITS if (n, u) in VECTOR_UNITS]
BY_SCALAR = [n * UPB + u for n, u in UNITS if (n, u) not in VECTOR_UNITS]


def build_program(nc, adj_cols, adj, x_tiles, x_t, w_msg, b_msg, w_ih, w_hh, b_ih, b_hh, w_gcn, b_gcn,
                  w_q, b_q, w_k, b_k, w_vs, b_vs, w_beta, w_hyp, b_hyp, out):
    x1_dram = nc.dram_tensor("x1_dram", [P, TILES * P], F32)
    x2_dram = nc.dram_tensor("x2_dram", [P, TILES * P], F32)
    root_dram = nc.dram_tensor("root_dram", [P, TILES * P], F32)
    x3_dram = nc.dram_tensor("x3_dram", [P, TILES * P], F32)
    q4_dram = nc.dram_tensor("q4_dram", [CHUNKS, 4, H, C, CHUNK], F32)
    k4_dram = nc.dram_tensor("k4_dram", [CHUNKS, 4, H, C, CHUNK], F32)

    with ExitStack() as ctx:
        def sb(name, shape, dt=F32):
            return ctx.enter_context(nc.sbuf_tensor(name, shape, dt))

        def sem(name):
            return ctx.enter_context(nc.semaphore(name))

        k4 = sb("k4", [P, H, N], F32R)
        parts = sb("parts", [P, 2, CHUNK], F32R)
        stat_x = sb("stat_x", [P, TILES, P])
        stat_s = sb("stat_s", [P, TILES, P])
        arena = sb("arena", [P, 25600])
        ident = sb("ident", [P, P])
        early = sb("early", [P, 8 * P])
        wgcn, wq, wk, bgcn = [early[:, i * P:(i + 1) * P] for i in range(4)]
        wvs, bvs = early[:, 4 * P:6 * P], early[:, 6 * P:8 * P]
        whyp = sb("whyp", [P, P])
        wbo = sb("wbo", [P, P])
        wbr = sb("wbr", [P, P])
        hbias = sb("hbias", [P, P])
        small = sb("small", [P, 340])
        taken = [0]

        def cut(n):
            taken[0] += n
            return small[:, taken[0] - n:taken[0]]

        bmsg, bih, bhh, bq, bk = cut(1), cut(3), cut(3), cut(1), cut(1)
        brz = cut(2)
        ones = cut(1)
        minus_half, half, minus_one = cut(4), cut(4), cut(4)
        dinv = cut(TILES)
        deg = cut(4)
        deg_on = cut(4)
        bn6 = cut(24)
        mean_var = cut(8).rearrange("p (t k) -> p t k", k=2)
        rstd = cut(4)
        hb = cut(4)
        blockmax = cut(32).rearrange("p (b k) -> p b k", b=2)
        shift = cut(32).rearrange("p (b k) -> p b k", b=2)
        blocksum = cut(32).rearrange("p (b k) -> p b k", b=2)
        rowmax, rowsum, noedge, rrow = cut(4), cut(4), cut(4), cut(4)
        mix = cut(16)
        mix2 = cut(16)
        zz, ez, beta = cut(4), cut(4), cut(4)
        xx, mm, mh, hh = cut(4), cut(4), cut(4), cut(4)
        s1, s2, s3, s4, s5, s6, s7 = [cut(4) for _ in range(7)]
        t1, t2, t3 = [cut(4) for _ in range(3)]

        RING = SLOTS * JPS * CHUNK
        ring = arena[:, 0:RING].rearrange("p (s j i) -> p s j i", s=SLOTS, j=JPS)
        stages = [arena[:, RING + i * CHUNK:RING + (i + 1) * CHUNK] for i in range(18)]
        agg_t, msg_t, xt_in, r_t, z_t, n_t, hn_t, y_t, x_new, x_new_t = stages[:10]
        colsum = arena[:, RING + 10 * CHUNK:RING + 12 * CHUNK]
        wih = arena[:, RING + 12 * CHUNK:RING + 12 * CHUNK + 384]
        whh = arena[:, RING + 13 * CHUNK:RING + 13 * CHUNK + 384]
        wmsg = arena[:, RING + 14 * CHUNK:RING + 14 * CHUNK + 128]
        res_in, root_out, y_n = stages[15:18]
        agg1_t, x2_new, x2_new_t = stages[10:13]
        k_parts, q_parts = [arena[:, RING + i * CHUNK:RING + (i + 2) * CHUNK].bitcast(F32R).rearrange(
            "p (k n) -> p k n", k=2) for i in (2, 13)]
        wb3, bias_sq = root_out[:, 0:P], root_out[:, P:2 * P]
        spare_slot = stat_x[:, 0:JPS * CHUNK // P, :].rearrange("p (j i) f -> p j (i f)", j=JPS)
        cols = arena[:, 0:4 * H * BLOCK].rearrange("p (s h n) -> p s h n", s=4, h=H)
        at = 4 * H * BLOCK
        turned = arena[:, at:at + 4 * CHUNK].rearrange("p (s n) -> p s n", s=4)
        at += 4 * CHUNK
        adj_in = arena[:, at:at + 2 * BLOCK].rearrange("p (s n) -> p s n", s=2)
        at += 2 * BLOCK
        maskbias = [half_[:, i * BLOCK:(i + 1) * BLOCK] for half_ in
                    (arena[:, at:at + BLOCK].bitcast(BF16), early[:, :].bitcast(BF16)) for i in range(2)]
        at += BLOCK
        o_t, wide, o_n, root_g, x2_g, y_g, x3_g, mx_g = [arena[:, at + i * CHUNK:at + (i + 1) * CHUNK]
                                                        for i in range(8)]
        x3_t = wide
        bank = ctx.enter_context(nc.psum_tensor("bank", [P, 8, CHUNK], F32))

        def tiles(ap):
            return ap.rearrange("p (t f) -> p t f", f=P)

        def per_tile(row, n=TPC):
            return row.unsqueeze(1).to_broadcast([P, n, P])

        x_in = [sem(f"x_in{s}") for s in range(SLOTS)]
        weights_in = sem("weights_in")
        consts_set = sem("consts_set")
        bias_dve = sem("bias_dve")
        bias_act = sem("bias_act")
        bias_pool = sem("bias_pool")
        ring_landed = [sem(f"ring_landed{s}") for s in range(SLOTS)]
        spare_landed = sem("spare_landed")
        ring_multiplied = sem("ring_multiplied")
        ring_summed = sem("ring_summed")
        half_summed = sem("half_summed")
        sums_folded = sem("sums_folded")
        gru_pe, gru_act, gru_dve, gru_pool = [sem(f"gru_{e}") for e in ("pe", "act", "dve", "pool")]
        gru_xt_in, gru_x1_out = sem("gru_xt_in"), sem("gru_x1_out")
        GP = Steps("degree", "msg", "r", "z", "n_in", "n_hid", "y_turned", "x1_turned", "support")
        GA = Steps("agg", "msg", "r", "z", "n", "x1_t")
        GV = Steps("degree", "deg_on", "hn", "rhn", "npre", "diff", "zdiff", "nz", "y", "bn6", "bn", "x1", "dinv", "scaled")
        GG = Steps("deg_max", "deg_pow", "eps", "rstd")
        gcn_pe, gcn_act, gcn_dve, gcn_pool = [sem(f"gcn_{e}") for e in ("pe", "act", "dve", "pool")]
        gcn_x1_in, gcn_x2_out, gcn_root_out = sem("gcn_x1_in"), sem("gcn_x2_out"), sem("gcn_root_out")
        gcn_k_out, gcn_q_out = sem("gcn_k_out"), sem("gcn_q_out")
        gcn_k4_in, gcn_k4_last_in = sem("gcn_k4_in"), sem("gcn_k4_last_in")
        CP = Steps("turned", "x2_turned", "k", "q", "vs")
        CA = Steps("agg", "x2_t", "k_hi", "q_hi")
        CV = Steps("self", "dinv", "y", "bn6", "bn", "x2", "k_lo", "q_lo", "v", "root")
        CG = Steps("x1_bias", "eps", "rstd")
        adj_landed = [sem(f"adj_landed{s}") for s in range(2)]
        q4_landed = [sem(f"q4_landed{s}") for s in range(2)]
        bias_ready = sem("bias_ready")
        scores_ready = sem("scores_ready")
        masked_ready = sem("masked_ready")
        shift_ready = sem("shift_ready")
        exp_ready = sem("exp_ready")
        unit_turned = sem("unit_turned")
        unit_copied_act = sem("unit_copied_act")
        unit_copied_dve = sem("unit_copied_dve")
        unit_used = sem("unit_used")
        rows_pe, rows_act, rows_dve, rows_pool = [sem(f"rows_{e}") for e in ("pe", "act", "dve", "pool")]
        TP = Steps("turned")
        TA = Steps("weights", "copied")
        TV = Steps("rowmax", "below", "wide", "out")
        TG = Steps("wsum", "pair", "rowsum", "noedge", "guard", "recip", "mix")
        att_pe, att_act, att_dve, att_pool = [sem(f"att_{e}") for e in ("pe", "act", "dve", "pool")]
        att_in, att_x3_out = sem("att_in"), sem("att_x3_out")
        AP_ = Steps("x3_turned", "mx")
        AA = Steps("ez", "x3_t", "mx", "ln_a", "ln_b", "tanh", "ln_c", "ln_d")
        AV = Steps("zz", "one_ez", "beta", "bn6", "bn", "x3", "xx", "mm", "mh", "hh")
        AG = Steps("zo", "zr", "z", "diff", "sum", "root_b", "y", "eps", "rstd", "x3sq", "mxsq", "mxhb",
                   "xn", "xn_max", "mn", "mn_max", "xn_min", "xn_inv", "arg", "a", "a_half", "arg2", "mn_inv",
                   "g_min", "g", "g2", "x2", "xy", "xy2", "x2y2", "den", "den_max", "den_inv",
                   "a_num", "a_g", "A", "b_num", "B", "bias_b", "mx_a", "h", "hsq", "hn", "hn_max", "pn", "hn_inv", "fa", "fa_half",
                   "fac", "xt")
        hyp_pe, hyp_act, hyp_dve, hyp_pool = [sem(f"hyp_{e}") for e in ("pe", "act", "dve", "pool")]
        hyp_in, hyp_out, hyp_sub = sem("hyp_in"), sem("hyp_out"), sem("hyp_sub")
        HP = Steps("turned")
        HA = Steps("agg", "uu", "tanh", "ln_a", "ln_b", "w", "ww", "tanh2")
        HV = Steps("y", "bn6", "bn", "out")
        HG = Steps("un", "un_max", "p", "un_inv", "fac", "wn", "wn_max", "wn_inv", "p2", "f2", "fh", "eps", "rstd")

        block = ctx.enter_context(nc.Block())

        @block.sync
        def _(sp):
            def load_ring(layer, c, first, slots=SLOTS):
                for s in range(slots):
                    turn = layer * CHUNKS + c
                    if layer == 0 and first:
                        sp.dma_start(stat_x[:, s * JPS:(s + 1) * JPS, :].rearrange("p t f -> p (t f)"),
                                     x_tiles[:, s * JPS * P:(s + 1) * JPS * P]).then_inc(x_in[s], 16)
                    if first and layer == 2 and s % 2 == 0:
                        sp.wait_ge(unit_turned, (CHUNKS * COLS - 4 + s // 2 + 1) * UPB)
                    if not first:
                        sp.wait_ge(ring_multiplied, (turn - 1) * SLOTS + s + 1)
                        if layer == 0 or is_zero(c):
                            sp.wait_ge(ring_summed, (turn - 1) * SLOTS + s + 1)
                    sp.dma_start(ring[:, s, :, :].rearrange("p j i -> p (j i)"),
                                 adj_cols[bass.ds(c, 1), s, :, :].rearrange("c p n -> (c p) n")
                                 ).then_inc(ring_landed[s], 16)

            load_ring(0, 0, True)
            with sp.Fori(1, CHUNKS) as c:
                load_ring(0, c, False)
            load_ring(1, 0, False)
            with sp.Fori(1, CHUNKS) as c:
                load_ring(1, c, False)

            def load_mask(c, m, fresh):
                t, b = m // BLOCKS, m % BLOCKS
                if not (fresh and m < 2):
                    sp.wait_ge(bias_ready, c * COLS + m - 1)
                sp.dma_start(adj_in[:, m % 2, :],
                             adj[bass.ds((c * TPC + t) * P, P), b * BLOCK:(b + 1) * BLOCK]
                             ).then_inc(adj_landed[m % 2], 16)

            def load_queries(c, t, fresh):
                if not (fresh and t < 2):
                    sp.wait_ge(scores_ready, (c * TPC + t - 1) * BLOCKS * H)
                for g in range(4):
                    sp.dma_start(parts[g * C:(g + 1) * C, t % 2, :].bitcast(F32).rearrange("p (h n) -> p h n", h=H),
                                 q4_dram[bass.ds(c, 1), g, :, :, t * P:(t + 1) * P].rearrange("o h c n -> (o c) h n")
                                 ).then_inc(q4_landed[t % 2], 16)

            def attention_loads(c, first):
                for m in range(COLS):
                    if m % BLOCKS == 0:
                        load_queries(c, m // BLOCKS, first)
                    if not (first and m < 2):
                        load_mask(c, m, first)
                    if m == 8 and not first:
                        load_residuals(c - 1)
                    if m == 15 and not first:
                        store_x3(c - 1)

            def load_residuals(c):
                if not is_zero(c):
                    sp.wait_ge(att_pool, AG(c - 1, "xt"))
                    sp.wait_ge(att_x3_out, 16 * c)
                sp.dma_start(x2_g, x2_dram[:, bass.ds(c * CHUNK, CHUNK)]).then_inc(att_in, 16)
                sp.dma_start(root_g, root_dram[:, bass.ds(c * CHUNK, CHUNK)]).then_inc(att_in, 16)

            def store_x3(c):
                sp.wait_ge(att_dve, AV(c, "x3"))
                sp.dma_start(x3_dram[:, bass.ds(c * CHUNK, CHUNK)], x3_g).then_inc(att_x3_out, 16)

            sp.wait_ge(gru_pe, GP(CHUNKS - 1, "y_turned"))
            load_mask(0, 0, True)
            load_mask(0, 1, True)
            sp.wait_ge(gcn_q_out, 64 * (CHUNKS - 2))
            attention_loads(0, True)
            sp.wait_ge(gcn_dve, CV(CHUNKS - 1, "root"))
            sp.wait_ge(gcn_q_out, 64 * CHUNKS)
            sp.wait_ge(gcn_k_out, 64 * CHUNKS)
            sp.wait_ge(gcn_root_out, 16 * CHUNKS)
            sp.wait_ge(gcn_x2_out, 16 * CHUNKS)
            load_residuals(0)
            for m in range(COLS):
                if m % BLOCKS == 0:
                    load_queries(1, m // BLOCKS, False)
                load_mask(1, m, False)
                if m == 15:
                    store_x3(0)
            with sp.Fori(2, CHUNKS) as c:
                attention_loads(c, False)
            load_ring(2, 0, True)
            load_residuals(CHUNKS - 1)
            load_ring(2, 1, False, SLOTS - 1)
            sp.wait_ge(unit_used, CHUNKS * COLS * UPB)
            sp.dma_start(spare_slot.rearrange("p j i -> p (j i)"), adj_cols[1, SLOTS - 1, :, :]
                         ).then_inc(spare_landed, 16)
            store_x3(CHUNKS - 1)
            with sp.Fori(2, CHUNKS) as c:
                load_ring(2, c, False)
            sp.wait_ge(hyp_out, 16 * CHUNKS)

        @block.tensor
        def _(pe):
            def turn4(dst_bank, src):
                for t in range(4):
                    last = pe.transpose(bank[:, dst_bank, t * P:(t + 1) * P], src[:, t * P:(t + 1) * P], ident[:, :])
                return last

            def product(layer, c, hooks, to=0, slots=range(SLOTS), skipped=0):
                stat = stat_x if layer == 0 else stat_s
                for s in slots:
                    landed = layer * CHUNKS + c + 1 - (skipped if s == SLOTS - 1 else 0)
                    pe.wait_ge(ring_landed[s], 16 * landed)
                    for j in range(JPS):
                        jt = s * JPS + j
                        mm_ = pe.matmul(bank[:, to, :], stat[:, jt, :], ring[:, s, j, :], start=(jt == 0),
                                        stop=(jt == TILES - 1))
                    mm_.then_inc(ring_multiplied, 1)
                    for hook in hooks.get(s, ()):
                        hook()

            def degree(c):
                pe.wait_ge(sums_folded, c + 1)
                for t in range(TPC):
                    last = pe.matmul(bank[:, 7, t:t + 1], colsum[:, t * P:(t + 1) * P], ones, start=True, stop=True)
                last.then_inc(gru_pe, 1)

            def message(c):
                pe.wait_ge(gru_act, GA(c, "agg"))
                pe.matmul(bank[:, 2, :], wmsg, agg_t, start=True, stop=True).then_inc(gru_pe, 1)

            def gates(c):
                pe.wait_ge(gru_act, GA(c, "msg"))
                pe.wait_ge(gru_xt_in, 16 * (c + 1))
                for g in range(2):
                    pe.matmul(bank[:, 3 + g, :], wih[:, g * P:(g + 1) * P], msg_t, start=True, stop=False)
                    pe.matmul(bank[:, 3 + g, :], whh[:, g * P:(g + 1) * P], xt_in, start=False,
                              stop=True).then_inc(gru_pe, 1)
                pe.matmul(bank[:, 5, :], wih[:, 2 * P:3 * P], msg_t, start=True, stop=True).then_inc(gru_pe, 1)
                pe.matmul(bank[:, 6, :], whh[:, 2 * P:3 * P], xt_in, start=True, stop=True).then_inc(gru_pe, 1)

            def turn_y(c):
                pe.wait_ge(gru_dve, GV(c, "y"))
                turn4(7, y_t).then_inc(gru_pe, 1)

            def turn_x1(c):
                pe.wait_ge(gru_dve, GV(c, "x1"))
                turn4(7, x_new).then_inc(gru_pe, 1)

            def support(c):
                pe.wait_ge(gru_act, GA(c, "x1_t"))
                for t in range(TPC):
                    last = pe.matmul(bank[:, 1, t * P:(t + 1) * P], x_new_t[:, t * P:(t + 1) * P], wgcn[:, :],
                                     start=True, stop=True)
                last.then_inc(gru_pe, 1)

            def gru_hooks(c, support_at=SLOTS - 1):
                return {0: [lambda: degree(c), lambda: message(c)], 1: [lambda: gates(c)], 4: [lambda: turn_y(c)],
                        6: [lambda: turn_x1(c)], support_at: [lambda: support(c)]}

            def turn_agg(c):
                pe.wait_ge(gcn_act, CA(c, "agg"))
                turn4(7, agg1_t).then_inc(gcn_pe, 1)

            def turn_x2(c):
                pe.wait_ge(gcn_dve, CV(c, "x2"))
                turn4(7, x2_new).then_inc(gcn_pe, 1)

            def project(c):
                pe.wait_ge(gcn_act, CA(c, "x2_t"))
                pe.matmul(bank[:, 4, :], wk, x2_new_t, start=True, stop=True).then_inc(gcn_pe, 1)
                pe.matmul(bank[:, 7, :], wq, x2_new_t, start=True, stop=True).then_inc(gcn_pe, 1)
                for t in range(TPC):
                    last = pe.matmul(bank[:, 5 + t // 2, (t % 2) * 256:(t % 2) * 256 + 256],
                                     x2_new_t[:, t * P:(t + 1) * P], wvs, start=True, stop=True)
                last.then_inc(gcn_pe, 1)

            def gcn_hooks(c):
                return {1: [lambda: turn_agg(c)], 5: [lambda: turn_x2(c)], 6: [lambda: project(c)],
                        SLOTS - 1: [lambda: pe.wait_ge(gcn_dve, CV(c, "q_lo"))]}

            pe.wait_ge(x_in[0], 16)
            product(0, 0, {s: [lambda s=s: pe.wait_ge(x_in[s + 1], 16)] for s in range(SLOTS - 1)})
            pe.wait_ge(weights_in, 16 * WEIGHTS)
            pe.wait_ge(consts_set, CONSTS)
            with pe.Fori(1, CHUNKS) as c:
                pe.wait_ge(gru_act, GA(c - 1, "agg"))
                product(0, c, gru_hooks(c - 1))
            pe.wait_ge(gru_act, GA(CHUNKS - 1, "agg"))
            pe.wait_ge(gru_dve, GV(CHUNKS - 2, "scaled"))
            hooks = gru_hooks(CHUNKS - 1)
            hooks[5] = hooks.pop(6)
            hooks[6] = hooks.pop(SLOTS - 1) + [lambda: pe.wait_ge(gru_dve, GV(CHUNKS - 1, "scaled"))]
            product(1, 0, hooks)
            with pe.Fori(0, CHUNKS // 2 - 1) as pair:
                for k, to in ((1, 1), (2, 0)):
                    product(1, 2 * pair + k, gcn_hooks(2 * pair + k - 1), to=to)
            product(1, CHUNKS - 1, gcn_hooks(CHUNKS - 2), to=1)

            def scores(c, m, h, fresh):
                t, b = m // BLOCKS, m % BLOCKS
                if fresh and b == BLOCKS - 1 and h == 0:
                    pe.wait_ge(gcn_k4_last_in, 64 * (CHUNKS - LAST_BLOCK_CHUNK))
                if b == 0 and h == 0:
                    pe.wait_ge(q4_landed[t % 2], 64 * (2 * c + t // 2 + 1))
                if not (fresh and m == 0 and h < 2):
                    pe.wait_ge(masked_ready, (c * COLS + m) * H + h - 1)
                u = 2 * (h % 2)
                for i in range(BLOCK // CHUNK):
                    at_ = b * BLOCK + i * CHUNK
                    last = pe.matmul(bank[:, u + i, :], parts[:, t % 2, h * P:(h + 1) * P],
                                     k4[:, h, at_:at_ + CHUNK], start=True, stop=True)
                last.then_inc(scores_ready, 1)

            def turn_bank(c, first, use):
                prev, chunks = TURN_BANKS.before(use, first)
                if prev is None:
                    return
                if prev[0] == "unit":
                    k = prev[1] * UPB + prev[2]
                    if prev[1:] in VECTOR_UNITS:
                        pe.wait_ge(unit_copied_dve, (c - chunks) * len(BY_VECTOR) + BY_VECTOR.index(k) + 1)
                    else:
                        pe.wait_ge(unit_copied_act, (c - chunks) * len(BY_SCALAR) + BY_SCALAR.index(k) + 1)
                elif prev[0] == "out":
                    pe.wait_ge(rows_dve, TV((c - chunks) * TPC + prev[1] // BLOCKS - 1, "wide"))
                else:
                    pe.wait_ge(att_act, AA(c - chunks - 1, {"x3": "x3_t", "mx": "mx"}[prev[0]]))

            def turn_unit(c, n, u, first):
                if u == 0:
                    pe.wait_ge(exp_ready, (c * COLS + n) * H + H)
                turn_bank(c, first, ("unit", n, u))
                b_ = TURN_BANKS.bank(("unit", n, u))
                for h in range(H):
                    last = pe.transpose(bank[:, b_, h * P:(h + 1) * P], cols[:, n % 4, h, u * P:(u + 1) * P],
                                        ident[:, :])
                last.then_inc(unit_turned, 1)

            def attend(c, k, first):
                n, u = k // UPB, k % UPB
                t, b = n // BLOCKS, n % BLOCKS
                if b == 0 and u == 0 and not (first and t == 0):
                    pe.wait_ge(rows_act, TA(c * TPC + t - 1, "copied"))
                if (n, u) in VECTOR_UNITS:
                    pe.wait_ge(unit_copied_dve, c * len(BY_VECTOR) + BY_VECTOR.index(k) + 1)
                else:
                    pe.wait_ge(unit_copied_act, c * len(BY_SCALAR) + BY_SCALAR.index(k) + 1)
                for h in range(H):
                    last = pe.matmul(bank[h * C:(h + 1) * C, 7, b * P:(b + 1) * P],
                                     stat_x[:, b * UPB + u, h * C:(h + 1) * C], turned[:, k % 4, h * P:(h + 1) * P],
                                     start=(u == 0), stop=(u == UPB - 1))
                last.then_inc(unit_used, 1)

            def turn_out(c, t, body_c, first, use):
                pe.wait_ge(rows_act, TA(c * TPC + t, "copied"))
                turn_bank(body_c, first, use)
                turn4(TURN_BANKS.bank(use), o_t).then_inc(rows_pe, 1)

            def turn_x3(c, dst, body_c=None):
                pe.wait_ge(att_dve, AV(c, "x3"))
                if body_c is not None:
                    turn_bank(body_c, False, ("x3",))
                turn4(dst, x3_g).then_inc(att_pe, 1)

            def mobius_product(c, dst, body_c=None):
                pe.wait_ge(att_act, AA(c, "x3_t"))
                if body_c is not None:
                    turn_bank(body_c, False, ("mx",))
                for t in range(TPC):
                    last = pe.matmul(bank[:, dst, t * P:(t + 1) * P], x3_t[:, t * P:(t + 1) * P], whyp[:, :],
                                     start=True, stop=True)
                last.then_inc(att_pe, 1)

            def attention(c, first, last_chunk):
                for n in range(COLS):
                    for u in range(UPB):
                        ahead = head_ahead(c, n, u, SCORE_LEAD, last_chunk)
                        if u % 2 == 0 and ahead:
                            scores(*ahead, first and n == 0)
                        k = n * UPB + u
                        late = n % BLOCKS == 0 and u == USE_LAG
                        if n % BLOCKS == 0 and u == USE_LAG + 1:
                            attend(c, k - USE_LAG - 1, first)
                        turn_unit(c, n, u, first)
                        if k >= USE_LAG and not late:
                            attend(c, k - USE_LAG, first)
                        elif k < USE_LAG and not first:
                            attend(c - 1, COLS * UPB + k - USE_LAG, False)
                        if u == OUT_AT and n % BLOCKS == 0:
                            if n > 0:
                                turn_out(c, n // BLOCKS - 1, c, first, ("out", n))
                            elif not first:
                                turn_out(c - 1, TPC - 1, c, first, ("out", 0))
                        if (n, u) == X3_AT and not first:
                            turn_x3(c - 1, TURN_BANKS.bank(("x3",)), c)
                        if (n, u) == MX_AT and not first:
                            mobius_product(c - 1, TURN_BANKS.bank(("mx",)), c)
                if last_chunk:
                    for k in range(COLS * UPB - USE_LAG, COLS * UPB):
                        attend(c, k, first)

            turn_agg(CHUNKS - 1)
            pe.wait_ge(gcn_k4_in, 64 * LAST_BLOCK_CHUNK)
            for i in range(H):
                scores(0, 0, i, True)
            turn_x2(CHUNKS - 1)
            project(CHUNKS - 1)
            for i in range(H, SCORE_LEAD):
                scores(0, i // H, i % H, True)
            pe.wait_ge(gcn_dve, CV(CHUNKS - 1, "root"))
            attention(0, True, False)
            with pe.Fori(1, CHUNKS - 1) as c:
                attention(c, False, False)
            attention(CHUNKS - 1, False, True)

            def turn_u(c):
                pe.wait_ge(hyp_act, HA(c, "agg"))
                turn4(1, agg_t).then_inc(hyp_pe, 1)

            last = CHUNKS - 1

            pe.wait_ge(att_pool, AG(last - 2, "xt"))

            def final_out():
                pe.wait_ge(rows_act, TA(last * TPC + TPC - 1, "copied"))
                turn4(1, o_t).then_inc(rows_pe, 1)

            product(2, 0, {0: [final_out], 5: [lambda: turn_x3(last, 2), lambda: pe.wait_ge(att_pool, AG(last - 1, "xt"))],
                           6: [lambda: mobius_product(last, 3)]}, slots=range(SLOTS - 1))
            product(2, 1, {}, to=4, slots=range(SLOTS - 1))
            pe.wait_ge(att_pool, AG(last, "xt"))
            product(2, 0, {}, slots=[SLOTS - 1])
            pe.wait_ge(spare_landed, 16)
            for j in range(JPS):
                mm_ = pe.matmul(bank[:, 4, :], stat_s[:, TILES - JPS + j, :], spare_slot[:, j, :], start=False,
                                stop=(j == JPS - 1))
            mm_.then_inc(ring_multiplied, 1)
            turn_u(0)
            def two_chunks(pair, turn_slots):
                for k, to in ((0, 0), (1, 4)):
                    pe.wait_ge(hyp_act, HA(2 * pair + k - 2, "agg"))
                    product(2, 2 * pair + k, {turn_slots[k]: [lambda k=k: turn_u(2 * pair + k - 1)]}, to=to,
                            skipped=1)

            two_chunks(1, (6, 4))
            with pe.Fori(2, CHUNKS // 2) as pair:
                two_chunks(pair, (1, 0))
            turn_u(last)

        @block.scalar
        def _(act):
            act.dma_start(xt_in, x_t[:, 0:CHUNK]).then_inc(gru_xt_in, 16)
            for ap, src in ((wmsg, w_msg), (wih, w_ih), (whh, w_hh), (bmsg, b_msg), (bih, b_ih), (bhh, b_hh),
                            (bq, b_q), (bk, b_k), (wgcn[:, :], w_gcn), (wq[:, :], w_q), (wk[:, :], w_k),
                            (wvs[:, :], w_vs), (whyp[:, :], w_hyp)):
                act.dma_start(ap, src).then_inc(weights_in, 16)
            for ap, src in ((bgcn[:, :], b_gcn), (bvs[:, :], b_vs), (hbias[:, :], b_hyp), (wbo[:, :], w_beta[0:P]),
                            (wbr[:, :], w_beta[P:2 * P]), (wb3, w_beta[2 * P:3 * P])):
                act.dma_start(ap, src.partition_broadcast(P)).then_inc(weights_in, 16)
            act.wait_ge(weights_in, 16 * WEIGHTS)
            act.activation(bias_sq, hbias[:, :], ACT.Square, accum_out=hb[:, 0:1]).then_inc(bias_act, 1)
            act.wait_ge(bias_pool, 2)
            act.activation(hb[:, 2:3], hb[:, 1:2], ACT.Tanh).then_inc(bias_act, 1)
            act.wait_ge(bias_dve, 4)

            def gru(c, first):
                if not first:
                    act.wait_ge(gru_dve, GV(c - 1, "y"))
                    act.wait_ge(gru_x1_out, 16 * c)
                    act.dma_start(xt_in, x_t[:, bass.ds(c * CHUNK, CHUNK)]).then_inc(gru_xt_in, 16)
                act.wait_ge(ring_multiplied, (c + 1) * SLOTS)
                act.activation(agg_t, bank[:, 0, :], ACT.Copy).then_inc(gru_act, 1)
                act.wait_ge(gru_pe, GP(c, "msg"))
                act.activation(msg_t, bank[:, 2, :], ACT.Relu, bias=bmsg).then_inc(gru_act, 1)
                act.wait_ge(gru_pe, GP(c, "r"))
                act.activation(r_t, bank[:, 3, :], ACT.Tanh, bias=brz[:, 0:1], scale=0.5).then_inc(gru_act, 1)
                act.wait_ge(gru_pe, GP(c, "z"))
                act.activation(z_t, bank[:, 4, :], ACT.Tanh, bias=brz[:, 1:2], scale=0.5).then_inc(gru_act, 1)
                act.wait_ge(gru_dve, GV(c, "npre"))
                act.activation(n_t, hn_t, ACT.Tanh, bias=bih[:, 2:3]).then_inc(gru_act, 1)
                act.wait_ge(gru_dve, GV(c, "x1"))
                act.dma_start(x1_dram[:, bass.ds(c * CHUNK, CHUNK)], x_new).then_inc(gru_x1_out, 16)
                act.wait_ge(gru_pe, GP(c, "x1_turned"))
                act.activation(x_new_t, bank[:, 7, :], ACT.Copy).then_inc(gru_act, 1)

            gru(0, True)
            act.wait_ge(bias_dve, 6)
            act.activation(bias_sq, hbias[:, :], ACT.Square, accum_out=hb[:, 3:4]).then_inc(bias_act, 1)
            with act.Fori(1, CHUNKS) as c:
                gru(c, False)

            def gcn(c, first, from_bank):
                if not first:
                    act.wait_ge(gcn_dve, CV(c - 1, "y"))
                else:
                    act.wait_ge(gru_x1_out, 16 * CHUNKS)
                act.dma_start(res_in, x1_dram[:, bass.ds(c * CHUNK, CHUNK)]).then_inc(gcn_x1_in, 16)
                act.wait_ge(ring_multiplied, (CHUNKS + c + 1) * SLOTS)
                act.activation(agg1_t, bank[:, from_bank, :], ACT.Copy).then_inc(gcn_act, 1)
                if not first:
                    store_projections(c - 1)
                    store_root(c - 1)
                act.wait_ge(gcn_dve, CV(c, "x2"))
                act.dma_start(x2_dram[:, bass.ds(c * CHUNK, CHUNK)], x2_new).then_inc(gcn_x2_out, 16)
                act.wait_ge(gcn_pe, CP(c, "x2_turned"))
                act.activation(x2_new_t, bank[:, 7, :], ACT.Copy).then_inc(gcn_act, 1)
                act.wait_ge(gcn_pe, CP(c, "k"))
                if not first:
                    act.wait_ge(gcn_k_out, 64 * c)
                act.activation(k_parts[:, 0, :], bank[:, 4, :], ACT.Identity, bias=bk).then_inc(gcn_act, 1)
                act.wait_ge(gcn_pe, CP(c, "q"))
                if not first:
                    act.wait_ge(gcn_q_out, 64 * c)
                act.activation(q_parts[:, 0, :], bank[:, 7, :], ACT.Identity, bias=bq).then_inc(gcn_act, 1)

            def store_projections(c):
                act.wait_ge(gcn_act, CA(c, "k_hi"))
                act.wait_ge(gcn_dve, CV(c, "k_lo"))
                for g in range(4):
                    act.dma_start(k4_dram[bass.ds(c, 1), g, :, :, :].rearrange("o h c n -> (o h c) n"),
                                  k_parts[:, g % 2, :].bitcast(F32)).then_inc(gcn_k_out, 16)
                act.wait_ge(gcn_act, CA(c, "q_hi"))
                act.wait_ge(gcn_dve, CV(c, "q_lo"))
                for g in range(4):
                    act.dma_start(q4_dram[bass.ds(c, 1), g, :, :, :].rearrange("o h c n -> (o h c) n"),
                                  q_parts[:, g // 2, :].bitcast(F32)).then_inc(gcn_q_out, 16)

            def store_root(c):
                act.wait_ge(gcn_dve, CV(c, "root"))
                act.dma_start(root_dram[:, bass.ds(c * CHUNK, CHUNK)], root_out).then_inc(gcn_root_out, 16)

            gcn(0, True, 0)
            with act.Fori(0, CHUNKS // 2 - 1) as pair:
                for k, from_bank in ((1, 1), (2, 0)):
                    gcn(2 * pair + k, False, from_bank)
            gcn(CHUNKS - 1, False, 1)
            store_projections(CHUNKS - 1)

            def exponent(c, m, h):
                t, b = m // BLOCKS, m % BLOCKS
                if h == 0:
                    act.wait_ge(shift_ready, c * COLS + m + 1)
                piece = cols[:, m % 4, h, :]
                i = b * H + h
                act.activation(piece, piece, ACT.Exp, bias=shift[:, t % 2, i:i + 1], scale=SCORE_SCALE,
                               accum_out=blocksum[:, t % 2, i:i + 1]).then_inc(exp_ready, 1)

            def copy_unit(c, n, u, first):
                k = n * UPB + u
                act.wait_ge(unit_turned, c * COLS * UPB + k + 1)
                if not (first and k < 4):
                    act.wait_ge(unit_used, c * COLS * UPB + k - 3)
                elif k >= 2:
                    act.wait_ge(gcn_k_out, 64 * CHUNKS)
                act.activation(turned[:, k % 4, :], bank[:, TURN_BANKS.bank(("unit", n, u)), :],
                               ACT.Copy).then_inc(unit_copied_act, 1)

            def block_weights(c, t):
                g = c * TPC + t
                act.wait_ge(rows_dve, TV(g, "below"))
                act.activation(mix, mix, ACT.Exp, scale=SCORE_SCALE).then_inc(rows_act, 1)

            def copy_out(c, t):
                g = c * TPC + t
                act.wait_ge(unit_used, (g + 1) * BLOCKS * UPB)
                if not is_zero(g):
                    act.wait_ge(rows_pe, TP(g - 1, "turned"))
                act.activation(o_t, bank[:, 7, :], ACT.Copy).then_inc(rows_act, 1)

            def post_steps(c, x3_bank, mx_bank, wide_free, logs_at=(14, 7)):
                def beta_exp():
                    act.wait_ge(att_dve, AV(c, "zz"))
                    act.activation(ez, zz, ACT.Exp, scale=-1.0).then_inc(att_act, 1)

                def copy_x3():
                    act.wait_ge(att_pe, AP_(c, "x3_turned"))
                    act.wait_ge(rows_dve, TV(wide_free, "out"))
                    act.activation(x3_t, bank[:, x3_bank, :], ACT.Copy).then_inc(att_act, 1)

                def copy_mx():
                    act.wait_ge(att_pe, AP_(c, "mx"))
                    act.activation(mx_g, bank[:, mx_bank, :], ACT.Copy).then_inc(att_act, 1)

                def logs(name):
                    act.wait_ge(att_pool, AG(c, name))
                    act.activation(t1, s3, ACT.Ln, bias=1.0, scale=1.0).then_inc(att_act, 1)
                    act.activation(t2, s3, ACT.Ln, bias=1.0, scale=-1.0).then_inc(att_act, 1)

                def arg_tanh():
                    act.wait_ge(att_pool, AG(c, "arg2"))
                    act.activation(s4, s4, ACT.Tanh).then_inc(att_act, 1)
                    act.preload_act_table_set(EXP_AND_LN)

                return {(3, 3): beta_exp, (6, 6): copy_x3, (7, 6): copy_mx, (9, 7): lambda: logs("xn_min"),
                        (10, 7): arg_tanh, logs_at: lambda: logs("pn")}

            def attention(c, first, last_chunk):
                post = {} if first else post_steps(c - 1, TURN_BANKS.bank(("x3",)), TURN_BANKS.bank(("mx",)), c * TPC,
                                                    (13, 3) if last_chunk else (14, 7))
                for n in range(COLS):
                    for u in range(UPB):
                        if n % BLOCKS == MIX_COLUMN and u == 4:
                            block_weights(c, n // BLOCKS)
                        if n % BLOCKS == 0 and u == 2:
                            if n > 0:
                                copy_out(c, n // BLOCKS - 1)
                            elif not first:
                                copy_out(c - 1, TPC - 1)
                        if (n, u) not in VECTOR_UNITS:
                            copy_unit(c, n, u, first)
                        ahead = head_ahead(c, n, u, EXP_LEAD, last_chunk)
                        if u % 2 == 1 and ahead:
                            exponent(*ahead)
                        if (n, u) in post:
                            post[(n, u)]()

            act.preload_act_table_set(EXP_AND_LN)
            for i in range(H):
                exponent(0, 0, i)
            store_root(CHUNKS - 1)
            for i in range(H, EXP_LEAD):
                exponent(0, i // H, i % H)
            attention(0, True, False)
            with act.Fori(1, CHUNKS - 1) as c:
                attention(c, False, False)
            attention(CHUNKS - 1, False, True)
            copy_out(CHUNKS - 1, TPC - 1)
            final = post_steps(CHUNKS - 1, 2, 3, TILES - 1)
            for place in sorted(final):
                final[place]()
            act.wait_ge(att_pool, AG(CHUNKS - 1, "xt"))

            def hyperbolic(c, from_bank, multiplied):
                if is_zero(c):
                    act.wait_ge(att_x3_out, 16 * CHUNKS)
                else:
                    act.wait_ge(hyp_dve, HV(c - 1, "y"))
                act.dma_start(res_in, x3_dram[:, bass.ds(c * CHUNK, CHUNK)]).then_inc(hyp_in, 16)
                act.wait_ge(ring_multiplied, multiplied)
                act.activation(agg_t, bank[:, from_bank, :], ACT.Copy).then_inc(hyp_act, 1)
                act.wait_ge(hyp_pe, HP(c, "turned"))
                for t in range(TPC):
                    last = act.activation(y_t[:, t * P:(t + 1) * P], bank[:, 1, t * P:(t + 1) * P], ACT.Square,
                                          accum_out=s1[:, t:t + 1])
                last.then_inc(hyp_act, 1)
                act.wait_ge(hyp_pool, HG(c, "un_max"))
                act.activation(t1, s2, ACT.Tanh).then_inc(hyp_act, 1)
                act.wait_ge(hyp_pool, HG(c, "p"))
                act.activation(t2, s3, ACT.Ln, bias=1.0, scale=1.0).then_inc(hyp_act, 1)
                act.activation(t3, s3, ACT.Ln, bias=1.0, scale=-1.0).then_inc(hyp_act, 1)
                act.wait_ge(hyp_pool, HG(c, "fac"))
                for t in range(TPC):
                    last = act.activation(msg_t[:, t * P:(t + 1) * P], bank[:, 1, t * P:(t + 1) * P], ACT.Relu,
                                          scale=s5[:, t:t + 1])
                last.then_inc(hyp_act, 1)
                act.wait_ge(hyp_act, HA(c, "w"))
                for t in range(TPC):
                    last = act.activation(y_t[:, t * P:(t + 1) * P], msg_t[:, t * P:(t + 1) * P], ACT.Square,
                                          accum_out=s6[:, t:t + 1])
                last.then_inc(hyp_act, 1)
                act.wait_ge(hyp_pool, HG(c, "wn_max"))
                act.activation(t1, s7, ACT.Tanh).then_inc(hyp_act, 1)
                act.wait_ge(hyp_dve, HV(c, "out"))
                act.dma_start(out[:, bass.ds(c * CHUNK, CHUNK)], x_new).then_inc(hyp_out, 16)

            hyperbolic(0, 0, (2 * CHUNKS + 2) * SLOTS - 1)
            hyperbolic(1, 4, (2 * CHUNKS + 2) * SLOTS)
            with act.Fori(1, CHUNKS // 2) as pair:
                for k, from_bank in ((0, 0), (1, 4)):
                    hyperbolic(2 * pair + k, from_bank, (2 * CHUNKS + 2 * pair + k + 1) * SLOTS)

        @block.vector
        def _(dve):
            def row_stats(src, sem_):
                for t in range(TPC):
                    last = dve.bn_stats(bn6[:, 6 * t:6 * t + 6], src[:, t * P:(t + 1) * P])
                last.then_inc(sem_, 1)

            def mean_and_var(sem_, st, c):
                dve.wait_ge(sem_, st(c, "bn6"))
                dve.nop(nofuse=True)
                for t in range(TPC):
                    last = dve.bn_aggr(mean_var[:, t, :], bn6[:, 6 * t:6 * t + 6])
                last.then_inc(sem_, 1)

            def norm_stats(src, sem_, st, c):
                row_stats(src, sem_)
                mean_and_var(sem_, st, c)

            def normalise(dst, src):
                for t in range(TPC):
                    last = dve.tensor_scalar(dst[:, t * P:(t + 1) * P], src[:, t * P:(t + 1) * P],
                                             mean_var[:, t, 0:1], rstd[:, t:t + 1], ALU.subtract, ALU.mult)
                return last

            def sum_slot(c, s, fresh):
                dve.wait_ge(ring_landed[s], 16 * (c + 1))
                lo = ring[:, s, 0:2, :].rearrange("p j i -> p (j i)")
                hi = ring[:, s, 2:4, :].rearrange("p j i -> p (j i)")
                if s == 0:
                    if not fresh:
                        dve.wait_ge(gru_pe, GP(c - 1, "degree"))
                    dve.tensor_tensor(colsum, lo, hi, ALU.add).then_inc(ring_summed, 1)
                else:
                    dve.wait_ge(ring_summed, c * SLOTS + s)
                    dve.tensor_tensor(colsum, colsum, lo, ALU.add).then_inc(half_summed, 1)
                    dve.wait_ge(half_summed, c * (SLOTS - 1) + s)
                    dve.tensor_tensor(colsum, colsum, hi, ALU.add).then_inc(ring_summed, 1)

            def gru_steps(c):
                def degree():
                    dve.wait_ge(gru_pe, GP(c, "degree"))
                    dve.tensor_scalar(deg, bank[:, 7, 0:4], 1.0, None, ALU.add).then_inc(gru_dve, 1)
                    dve.wait_ge(gru_dve, GV(c, "degree"))
                    dve.tensor_scalar(deg_on, deg, 0.0, None, ALU.is_gt).then_inc(gru_dve, 1)

                def gate():
                    dve.wait_ge(gru_pe, GP(c, "n_hid"))
                    dve.tensor_scalar(hn_t, bank[:, 6, :], bhh[:, 2:3], 0.5, ALU.add, ALU.mult).then_inc(gru_dve, 1)
                    dve.wait_ge(gru_dve, GV(c, "hn"))
                    dve.wait_ge(gru_act, GA(c, "r"))
                    dve.scalar_tensor_tensor(hn_t, r_t, 1.0, hn_t, ALU.add, ALU.mult).then_inc(gru_dve, 1)
                    dve.wait_ge(gru_dve, GV(c, "rhn"))
                    dve.tensor_tensor(hn_t, bank[:, 5, :], hn_t, ALU.add).then_inc(gru_dve, 1)

                def blend():
                    dve.wait_ge(gru_act, GA(c, "n"))
                    dve.tensor_tensor(y_t, xt_in, n_t, ALU.subtract).then_inc(gru_dve, 1)
                    dve.wait_ge(gru_dve, GV(c, "diff"))
                    dve.scalar_tensor_tensor(y_t, z_t, 1.0, y_t, ALU.add, ALU.mult).then_inc(gru_dve, 1)
                    dve.wait_ge(gru_dve, GV(c, "zdiff"))
                    dve.scalar_tensor_tensor(y_t, y_t, 0.5, n_t, ALU.mult, ALU.add).then_inc(gru_dve, 1)
                    dve.wait_ge(gru_dve, GV(c, "nz"))
                    dve.tensor_tensor(y_t, y_t, xt_in, ALU.add).then_inc(gru_dve, 1)

                def stats():
                    dve.wait_ge(gru_pe, GP(c, "y_turned"))
                    norm_stats(bank[:, 7, :], gru_dve, GV, c)

                def norm():
                    dve.wait_ge(gru_pool, GG(c, "rstd"))
                    normalise(x_new, bank[:, 7, :]).then_inc(gru_dve, 1)

                def scale():
                    dve.wait_ge(gru_pool, GG(c, "deg_pow"))
                    dcol = dinv[:, bass.ds(c * TPC, TPC)]
                    dve.tensor_tensor(dcol, deg, deg_on, ALU.mult).then_inc(gru_dve, 1)
                    dve.wait_ge(gru_dve, GV(c, "dinv"))
                    dve.wait_ge(gru_pe, GP(c, "support"))
                    dve.tensor_tensor(stat_s[:, bass.ds(c * TPC, TPC), :], tiles(bank[:, 1, :]),
                                      dcol.unsqueeze(2).to_broadcast([P, TPC, P]), ALU.mult).then_inc(gru_dve, 1)

                return {0: [degree], 2: [gate, blend], 4: [stats], 5: [norm], 7: [scale]}

            def sums(c, fresh, steps):
                for s in range(SLOTS):
                    sum_slot(c, s, fresh)
                    if s == SLOTS - 1:
                        dve.wait_ge(ring_summed, (c + 1) * SLOTS)
                        dve.tensor_tensor(colsum[:, 0:CHUNK], colsum[:, 0:CHUNK], colsum[:, CHUNK:2 * CHUNK],
                                          ALU.add).then_inc(sums_folded, 1)
                    for step in steps.get(s, ()):
                        step()

            sums(0, True, {})
            dve.wait_ge(weights_in, 16 * WEIGHTS)
            dve.tensor_tensor(wbo[:, :], wbo[:, :], wb3, ALU.add).then_inc(bias_dve, 1)
            dve.tensor_tensor(wbr[:, :], wbr[:, :], wb3, ALU.subtract).then_inc(bias_dve, 1)
            dve.tensor_tensor(brz, bih[:, 0:2], bhh[:, 0:2], ALU.add).then_inc(bias_dve, 1)
            dve.wait_ge(bias_dve, 3)
            dve.tensor_scalar(brz, brz, 0.5, None, ALU.mult).then_inc(bias_dve, 1)
            dve.wait_ge(bias_pool, 3)
            dve.wait_ge(bias_act, 2)
            dve.tensor_scalar(hb[:, 2:3], hb[:, 2:3], MAX_NORM, hb[:, 0:1], ALU.min, ALU.mult).then_inc(bias_dve, 1)
            dve.wait_ge(bias_dve, 5)
            dve.tensor_scalar(hbias[:, :], hbias[:, :], hb[:, 2:3], None, ALU.mult).then_inc(bias_dve, 1)

            with dve.Fori(1, CHUNKS) as c:
                sums(c, False, gru_steps(c - 1))
            last_steps = gru_steps(CHUNKS - 1)
            for s in sorted(last_steps):
                for step in last_steps[s]:
                    step()

            def gcn_sum(c):
                dve.wait_ge(gcn_pe, CP(c, "turned"))
                dve.tensor_tensor(tiles(y_n), tiles(bank[:, 7, :]), stat_s[:, bass.ds(c * TPC, TPC), :],
                                  ALU.add).then_inc(gcn_dve, 1)
                dve.tensor_copy(deg, dinv[:, bass.ds(c * TPC, TPC)]).then_inc(gcn_dve, 1)
                dve.wait_ge(gcn_dve, CV(c, "dinv"))
                dve.wait_ge(gcn_pool, CG(c, "x1_bias"))
                for t in range(TPC):
                    s_ = slice(t * P, (t + 1) * P)
                    last = dve.scalar_tensor_tensor(y_n[:, s_], y_n[:, s_], deg[:, t:t + 1], res_in[:, s_],
                                                    ALU.mult, ALU.add)
                last.then_inc(gcn_dve, 1)
                dve.wait_ge(gcn_dve, CV(c, "y"))
                norm_stats(y_n, gcn_dve, CV, c)

            def gcn_norm(c):
                dve.wait_ge(gcn_pool, CG(c, "rstd"))
                if not is_zero(c):
                    dve.wait_ge(gcn_x2_out, 16 * c)
                normalise(x2_new, y_n).then_inc(gcn_dve, 1)

            def gcn_projections(c):
                dve.wait_ge(gcn_act, CA(c, "k_hi"))
                dve.scalar_tensor_tensor(k_parts[:, 1, :], bank[:, 4, :], bk, k_parts[:, 0, :].bitcast(F32), ALU.add,
                                         ALU.subtract).then_inc(gcn_dve, 1)
                dve.wait_ge(gcn_act, CA(c, "q_hi"))
                dve.scalar_tensor_tensor(q_parts[:, 1, :], bank[:, 7, :], bq, q_parts[:, 0, :].bitcast(F32), ALU.add,
                                         ALU.subtract).then_inc(gcn_dve, 1)
                dve.wait_ge(gcn_pe, CP(c, "vs"))
                both = bank[:, 5:7, :].rearrange("p b (t k f) -> p (b t) k f", t=2, k=2)
                for k, dst in ((0, stat_x[:, bass.ds(c * TPC, TPC), :]), (1, tiles(root_out))):
                    if k == 1 and not is_zero(c):
                        dve.wait_ge(gcn_root_out, 16 * c)
                    dve.tensor_tensor(dst, both[:, :, k, :], per_tile(bvs[:, k * P:(k + 1) * P]),
                                      ALU.add).then_inc(gcn_dve, 1)

            def gcn(c):
                gcn_sum(c)
                gcn_norm(c)
                gcn_projections(c)

            gcn(0)
            with dve.Fori(1, CHUNKS - 1) as c:
                gcn(c)

            def mask(c, m, h, first):
                t, b = m // BLOCKS, m % BLOCKS
                if h == 0:
                    dve.wait_ge(bias_ready, c * COLS + m + 1)
                    if not (first and m < 4):
                        dve.wait_ge(unit_turned, (c * COLS + m - 3) * UPB)
                dve.wait_ge(scores_ready, (c * COLS + m) * H + h + 1)
                dve.nop(nofuse=True)
                i = b * H + h
                dve.tensor_tensor_reduce(out=cols[:, m % 4, h, :],
                                         in0=bank[:, 2 * (h % 2):2 * (h % 2) + 2, :].rearrange("p b n -> p (b n)"),
                                         in1=maskbias[m % 4], scale=1.0, scalar=LOWEST, op0=ALU.add,
                                         op1=ALU.max, accum_out=blockmax[:, t % 2, i:i + 1]).then_inc(masked_ready, 1)
                if h == H - 1:
                    dve.wait_ge(masked_ready, (c * COLS + m) * H + H)
                    dve.tensor_scalar(shift[:, t % 2, b * H:(b + 1) * H], blockmax[:, t % 2, b * H:(b + 1) * H],
                                      -SCORE_SCALE, None, ALU.mult).then_inc(shift_ready, 1)

            def copy_unit(c, n, u, first):
                k = n * UPB + u
                dve.wait_ge(unit_turned, c * COLS * UPB + k + 1)
                if not (first and k < 4):
                    dve.wait_ge(unit_used, c * COLS * UPB + k - 3)
                elif k >= 2:
                    dve.wait_ge(gcn_k_out, 64 * CHUNKS)
                dve.tensor_copy(turned[:, k % 4, :], bank[:, TURN_BANKS.bank(("unit", n, u)), :]).then_inc(unit_copied_dve, 1)

            def below_max(c, t):
                g = c * TPC + t
                bm = blockmax[:, t % 2, :].rearrange("p (b h) -> p b h", h=H)
                dve.wait_ge(masked_ready, (g + 1) * BLOCKS * H)
                dve.tensor_reduce(rowmax, bm.rearrange("p b h -> p h b"), AX.X, ALU.max).then_inc(rows_dve, 1)
                dve.wait_ge(rows_dve, TV(g, "rowmax"))
                dve.tensor_tensor(mix.rearrange("p (b h) -> p b h", h=H), bm,
                                  rowmax.unsqueeze(1).to_broadcast([P, BLOCKS, H]), ALU.subtract).then_inc(rows_dve, 1)

            def weigh(c, t, b_):
                g = c * TPC + t
                dve.wait_ge(rows_pool, TG(g, "mix"))
                dve.wait_ge(rows_pe, TP(g, "turned"))
                dve.tensor_tensor(wide.rearrange("p (k f) -> p k f", f=C), bank[:, b_, :].rearrange("p (k f) -> p k f", f=C),
                                  mix.unsqueeze(2).to_broadcast([P, BLOCKS * H, C]), ALU.mult).then_inc(rows_dve, 1)

            def add_blocks(c, t):
                g = c * TPC + t
                dve.wait_ge(rows_dve, TV(g, "wide"))
                dve.tensor_reduce(o_n[:, t * P:(t + 1) * P].rearrange("p (f h) -> p h f", h=H),
                                  wide.rearrange("p (b h f) -> p h f b", b=BLOCKS, h=H), AX.X,
                                  ALU.add).then_inc(rows_dve, 1)

            def post_steps(c, norm_h_at=(13, 5)):
                def beta_logit():
                    dve.wait_ge(att_pool, AG(c, "z"))
                    dve.tensor_reduce(zz, tiles(y_g), AX.X, ALU.add).then_inc(att_dve, 1)

                def gate():
                    dve.wait_ge(att_act, AA(c, "ez"))
                    dve.tensor_scalar(ez, ez, 1.0, None, ALU.add).then_inc(att_dve, 1)
                    dve.wait_ge(att_dve, AV(c, "one_ez"))
                    dve.reciprocal(beta, ez).then_inc(att_dve, 1)

                def stats():
                    dve.wait_ge(att_pool, AG(c, "y"))
                    row_stats(y_g, att_dve)

                def norm():
                    dve.wait_ge(att_pool, AG(c, "rstd"))
                    normalise(x3_g, y_g).then_inc(att_dve, 1)

                def norm_x3():
                    dve.wait_ge(att_pool, AG(c, "x3sq"))
                    dve.tensor_reduce(xx, tiles(y_g), AX.X, ALU.add).then_inc(att_dve, 1)

                def norm_mx():
                    dve.wait_ge(att_pool, AG(c, "mxsq"))
                    dve.tensor_reduce(mm, tiles(y_g), AX.X, ALU.add).then_inc(att_dve, 1)

                def bias_mx():
                    dve.wait_ge(att_pool, AG(c, "mxhb"))
                    dve.tensor_reduce(mh, tiles(root_g), AX.X, ALU.add).then_inc(att_dve, 1)

                def norm_h():
                    dve.wait_ge(att_pool, AG(c, "hsq"))
                    dve.tensor_reduce(hh, tiles(y_g), AX.X, ALU.add).then_inc(att_dve, 1)

                return {(2, 5): beta_logit, (3, 5): gate, (4, 7): stats,
                        (5, 1): lambda: mean_and_var(att_dve, AV, c), (6, 3): norm, (7, 3): norm_x3,
                        (8, 5): norm_mx, (9, 1): bias_mx, norm_h_at: norm_h}

            def attention(c, first, last_chunk):
                post = post_steps(c - 1, (12, 7) if last_chunk else (13, 5)) if not first else {}
                for n in range(COLS):
                    for u in range(UPB):
                        ahead = head_ahead(c, n, u, MASK_LEAD, last_chunk)
                        if u % 2 == 0 and ahead:
                            mask(*ahead, first and n < COLS - BLOCKS)
                        if (n, u) in VECTOR_UNITS:
                            copy_unit(c, n, u, first)
                        if n % BLOCKS == 0 and not (first and n == 0):
                            done = (c, n // BLOCKS - 1) if n > 0 else (c - 1, TPC - 1)
                            if u == 6:
                                weigh(*done, TURN_BANKS.bank(("out", n)))
                        if n % BLOCKS == 1 and u == 1 and not (first and n == 1):
                            done = (c, n // BLOCKS - 1) if n > 1 else (c - 1, TPC - 1)
                            add_blocks(*done)
                        if n % BLOCKS == MIX_COLUMN and u == 1:
                            below_max(c, n // BLOCKS)
                        if (n, u) in post:
                            post[(n, u)]()

            gcn_sum(CHUNKS - 1)
            dve.wait_ge(ring_multiplied, 2 * CHUNKS * SLOTS)
            dve.wait_ge(bias_dve, 6)
            for i in range(2):
                mask(0, 0, i, True)
            gcn_norm(CHUNKS - 1)
            for i in range(2, H):
                mask(0, 0, i, True)
            gcn_projections(CHUNKS - 1)
            for i in range(H, MASK_LEAD):
                mask(0, i // H, i % H, True)
            dve.wait_ge(gcn_x2_out, 16 * CHUNKS)
            attention(0, True, False)
            with dve.Fori(1, CHUNKS - 1) as c:
                attention(c, False, False)
            attention(CHUNKS - 1, False, True)
            weigh(CHUNKS - 1, TPC - 1, 1)
            add_blocks(CHUNKS - 1, TPC - 1)
            final = post_steps(CHUNKS - 1)
            for place in sorted(final):
                final[place]()

            def hyperbolic(c):
                dve.wait_ge(hyp_pool, HG(c, "fh"))
                dve.tensor_tensor(y_n, msg_t, res_in, ALU.add).then_inc(hyp_dve, 1)
                dve.wait_ge(hyp_dve, HV(c, "y"))
                norm_stats(y_n, hyp_dve, HV, c)
                dve.wait_ge(hyp_pool, HG(c, "rstd"))
                if not is_zero(c):
                    dve.wait_ge(hyp_out, 16 * c)
                normalise(x_new, y_n).then_inc(hyp_dve, 1)

            hyperbolic(0)
            with dve.Fori(1, CHUNKS) as c:
                hyperbolic(c)

        @block.gpsimd
        def _(pool):
            pool.memset(ones, 1.0).then_inc(consts_set, 1)
            pool.memset(minus_half, -0.5).then_inc(consts_set, 1)
            pool.memset(half, 0.5).then_inc(consts_set, 1)
            pool.memset(minus_one, -1.0).then_inc(consts_set, 1)
            pool.memset(ident[:, :], 0.0).then_inc(consts_set, 1)
            pool.wait_ge(consts_set, 5)
            pool.affine_select(out=ident[:, :], in_=ident[:, :], compare_op=ALU.not_equal, fill=1.0, base=0,
                               pattern=[[-1, P]], channel_multiplier=1).then_inc(consts_set, 1)
            pool.wait_ge(bias_act, 1)
            pool.tensor_tensor(hb[:, 1:2], hb[:, 0:1], half[:, 0:1], ALU.pow).then_inc(bias_pool, 1)
            pool.wait_ge(bias_pool, 1)
            pool.tensor_scalar(hb[:, 1:2], hb[:, 1:2], MIN_NORM, None, ALU.max).then_inc(bias_pool, 1)
            pool.wait_ge(bias_pool, 2)
            pool.tensor_tensor(hb[:, 0:1], hb[:, 1:2], minus_one[:, 0:1], ALU.pow).then_inc(bias_pool, 1)

            def stage(sem_, st):
                def step(c, name, ins):
                    ins.then_inc(sem_, 1)
                    pool.wait_ge(sem_, st(c, name))
                    pool.nop(nofuse=True)
                return step

            def rsqrt_var(c, step):
                pool.nop(nofuse=True)
                step(c, "eps", pool.tensor_scalar(rstd, mean_var[:, :, 1], LN_EPS, None, ALU.add))
                step(c, "rstd", pool.tensor_tensor(rstd, rstd, minus_half, ALU.pow))

            def gru(c):
                step = stage(gru_pool, GG)
                pool.wait_ge(gru_dve, GV(c, "deg_on"))
                pool.nop(nofuse=True)
                step(c, "deg_max", pool.tensor_scalar(deg, deg, 1e-30, None, ALU.max))
                step(c, "deg_pow", pool.tensor_tensor(deg, deg, minus_half, ALU.pow))
                pool.wait_ge(gru_dve, GV(c, "bn"))
                rsqrt_var(c, step)

            gru(0)
            with pool.Fori(1, CHUNKS) as c:
                gru(c)

            def add_bias(c):
                step = stage(gcn_pool, CG)
                pool.wait_ge(gcn_x1_in, 16 * (c + 1))
                step(c, "x1_bias", pool.tensor_tensor(tiles(res_in), tiles(res_in), per_tile(bgcn), ALU.add))

            def gcn_rsqrt(c):
                pool.wait_ge(gcn_dve, CV(c, "bn"))
                rsqrt_var(c, stage(gcn_pool, CG))

            def load_k4(c, landed):
                pool.wait_ge(gcn_k_out, 64 * (c + 1))
                for g in range(4):
                    pool.dma_start(k4[g * C:(g + 1) * C, :, bass.ds(c * CHUNK, CHUNK)].bitcast(F32),
                                   k4_dram[bass.ds(c, 1), g, :, :, :].rearrange("o h c n -> (o c) h n")
                                   ).then_inc(landed, 16)

            add_bias(0)
            gcn_rsqrt(0)
            with pool.Fori(1, CHUNKS - 1) as c:
                add_bias(c)
                gcn_rsqrt(c)
                load_k4(c - 1, gcn_k4_in)

            def mask_bias(c, m, first):
                pool.wait_ge(adj_landed[m % 2], 16 * (c * COLS // 2 + m // 2 + 1))
                if not (first and m < 4):
                    pool.wait_ge(masked_ready, (c * COLS + m - 3) * H)
                pool.nop(nofuse=True)
                pool.tensor_scalar(maskbias[m % 4], adj_in[:, m % 2, :], 0.0, MASKED, ALU.is_equal,
                                   ALU.mult).then_inc(bias_ready, 1)

            def post_steps(c, factor_at=31):
                step = stage(att_pool, AG)

                def tt(name, out_, a, b, op):
                    step(c, name, pool.tensor_tensor(out_, a, b, op))

                def ts(name, out_, a, x, op, y=None, op2=None):
                    if op2 is None:
                        step(c, name, pool.tensor_scalar(out_, a, x, None, op))
                    else:
                        step(c, name, pool.tensor_scalar(out_, a, x, y, op, op2))

                def beta_terms():
                    pool.wait_ge(rows_dve, TV(c * TPC + TPC - 1, "out"))
                    pool.wait_ge(att_in, 32 * (c + 1))
                    tt("zo", tiles(y_g), tiles(o_n), per_tile(wbo[:, :]), ALU.mult)
                    tt("zr", tiles(mx_g), tiles(root_g), per_tile(wbr[:, :]), ALU.mult)
                    tt("z", y_g, y_g, mx_g, ALU.add)

                def residual_terms():
                    tt("diff", root_g, root_g, o_n, ALU.subtract)
                    tt("sum", x2_g, x2_g, o_n, ALU.add)

                def blend():
                    pool.wait_ge(att_dve, AV(c, "beta"))
                    tt("root_b", tiles(root_g), tiles(root_g), beta.unsqueeze(2).to_broadcast([P, TPC, P]), ALU.mult)
                    tt("y", y_g, root_g, x2_g, ALU.add)

                def rs():
                    pool.wait_ge(att_dve, AV(c, "bn"))
                    rsqrt_var(c, step)

                def x3sq():
                    pool.wait_ge(att_dve, AV(c, "x3"))
                    tt("x3sq", y_g, x3_g, x3_g, ALU.mult)

                def mx_terms():
                    pool.wait_ge(att_act, AA(c, "mx"))
                    pool.wait_ge(att_dve, AV(c, "xx"))
                    tt("mxsq", y_g, mx_g, mx_g, ALU.mult)
                    tt("mxhb", tiles(root_g), tiles(mx_g), per_tile(hbias[:, :]), ALU.mult)

                def norms():
                    pool.wait_ge(att_dve, AV(c, "mh"))
                    tt("xn", s1, xx, half, ALU.pow)
                    ts("xn_max", s1, s1, MIN_NORM, ALU.max)
                    tt("mn", s2, mm, half, ALU.pow)
                    ts("mn_max", s2, s2, MIN_NORM, ALU.max)
                    ts("xn_min", s3, s1, ARTANH_MAX, ALU.min)
                    tt("xn_inv", s4, s1, minus_one, ALU.pow)
                    tt("arg", s4, s4, s2, ALU.mult)

                def argument():
                    pool.wait_ge(att_act, AA(c, "ln_b"))
                    tt("a", t1, t1, t2, ALU.subtract)
                    ts("a_half", t1, t1, 0.5, ALU.mult)
                    tt("arg2", s4, s4, t1, ALU.mult)
                    tt("mn_inv", s5, s2, minus_one, ALU.pow)

                def coefficients():
                    pool.wait_ge(att_act, AA(c, "tanh"))
                    pool.nop(nofuse=True)
                    ts("g_min", s4, s4, MAX_NORM, ALU.min)
                    tt("g", s4, s4, s5, ALU.mult)
                    tt("g2", s5, s4, s4, ALU.mult)
                    tt("x2", s5, s5, mm, ALU.mult)
                    tt("xy", s6, s4, mh, ALU.mult)
                    ts("xy2", s6, s6, 2.0, ALU.mult, 1.0, ALU.add)
                    ts("x2y2", s7, s5, hb[:, 3:4], ALU.mult)
                    tt("den", s7, s7, s6, ALU.add)
                    ts("den_max", s7, s7, MIN_NORM, ALU.max)
                    tt("den_inv", s3, s7, minus_one, ALU.pow)
                    ts("a_num", s6, s6, hb[:, 3:4], ALU.add)
                    tt("a_g", s6, s6, s4, ALU.mult)
                    tt("A", s6, s6, s3, ALU.mult)
                    ts("b_num", s7, s5, -1.0, ALU.mult, 1.0, ALU.add)
                    tt("B", s7, s7, s3, ALU.mult)

                def mobius_sum():
                    tt("bias_b", tiles(root_g), per_tile(hbias[:, :]), s7.unsqueeze(2).to_broadcast([P, TPC, P]),
                       ALU.mult)
                    tt("mx_a", tiles(mx_g), tiles(mx_g), s6.unsqueeze(2).to_broadcast([P, TPC, P]), ALU.mult)
                    tt("h", mx_g, mx_g, root_g, ALU.add)
                    tt("hsq", y_g, mx_g, mx_g, ALU.mult)

                def norms_h():
                    pool.wait_ge(att_dve, AV(c, "hh"))
                    tt("hn", s1, hh, half, ALU.pow)
                    ts("hn_max", s1, s1, MIN_NORM, ALU.max)
                    ts("pn", s3, s1, MAX_NORM, ALU.min)
                    tt("hn_inv", s1, s1, minus_one, ALU.pow)

                def factor():
                    pool.wait_ge(att_act, AA(c, "ln_d"))
                    tt("fa", t1, t1, t2, ALU.subtract)
                    ts("fa_half", t1, t1, 0.5, ALU.mult)
                    tt("fac", s1, s1, t1, ALU.mult)
                    tt("xt", stat_s[:, bass.ds(c * TPC, TPC), :], tiles(mx_g), s1.unsqueeze(2).to_broadcast([P, TPC, P]),
                       ALU.mult)

                return {3: beta_terms, 5: residual_terms, 8: blend, 10: rs, 13: x3sq, 16: mx_terms, 18: norms,
                        20: argument, 22: coefficients, 24: mobius_sum, 28: norms_h, factor_at: factor}

            def block_mix(c, t):
                g = c * TPC + t
                step = stage(rows_pool, TG)
                pool.wait_ge(rows_act, TA(g, "weights"))
                pool.wait_ge(exp_ready, (g + 1) * BLOCKS * H)
                step(g, "wsum", pool.tensor_tensor(mix2, mix, blocksum[:, t % 2, :], ALU.mult))
                step(g, "pair", pool.tensor_tensor(mix2[:, 0:2 * H], mix2[:, 0:2 * H], mix2[:, 2 * H:4 * H], ALU.add))
                step(g, "rowsum", pool.tensor_tensor(rowsum, mix2[:, 0:H], mix2[:, H:2 * H], ALU.add))
                step(g, "noedge", pool.tensor_scalar(noedge, rowsum, 0.0, None, ALU.is_equal))
                step(g, "guard", pool.tensor_tensor(rowsum, rowsum, noedge, ALU.add))
                step(g, "recip", pool.tensor_tensor(rrow, rowsum, minus_one, ALU.pow))
                step(g, "mix", pool.tensor_tensor(mix.rearrange("p (b h) -> p b h", h=H),
                                                  mix.rearrange("p (b h) -> p b h", h=H),
                                                  rrow.unsqueeze(1).to_broadcast([P, BLOCKS, H]), ALU.mult))

            pool.wait_ge(bias_dve, 6)
            pool.wait_ge(bias_act, 3)

            def attention(c, first, last_chunk):
                post = post_steps(c - 1, 30 if last_chunk else 31) if not first else {}
                for n in range(COLS):
                    for half_ in range(2):
                        if half_ == 1:
                            ahead = n + BIAS_LEAD
                            if ahead < COLS:
                                mask_bias(c, ahead, first)
                            elif not last_chunk:
                                mask_bias(c + 1, ahead - COLS, False)
                        if half_ == 1 and n % BLOCKS == MIX_COLUMN:
                            block_mix(c, n // BLOCKS)
                        if 2 * n + half_ in post:
                            post[2 * n + half_]()

            mask_bias(0, 0, True)
            add_bias(CHUNKS - 1)
            gcn_rsqrt(CHUNKS - 1)
            mask_bias(0, 1, True)
            load_k4(CHUNKS - 2, gcn_k4_last_in)
            pool.wait_ge(gcn_dve, CV(CHUNKS - 1, "root"))
            mask_bias(0, 2, True)
            load_k4(CHUNKS - 1, gcn_k4_last_in)
            for m in range(3, BIAS_LEAD):
                mask_bias(0, m, True)
            attention(0, True, False)
            with pool.Fori(1, CHUNKS - 1) as c:
                attention(c, False, False)
            attention(CHUNKS - 1, False, True)
            final = post_steps(CHUNKS - 1)
            for slot in sorted(final):
                final[slot]()

            def hyperbolic(c):
                step = stage(hyp_pool, HG)
                pool.wait_ge(hyp_act, HA(c, "uu"))
                step(c, "un", pool.tensor_tensor(s2, s1, half, ALU.pow))
                step(c, "un_max", pool.tensor_scalar(s2, s2, MIN_NORM, None, ALU.max))
                pool.wait_ge(hyp_act, HA(c, "tanh"))
                pool.nop(nofuse=True)
                step(c, "p", pool.tensor_scalar(s3, t1, MAX_NORM, None, ALU.min))
                step(c, "un_inv", pool.tensor_tensor(s5, s2, minus_one, ALU.pow))
                pool.wait_ge(hyp_act, HA(c, "ln_b"))
                pool.tensor_tensor(t2, t2, t3, ALU.subtract).then_inc(hyp_sub, 1)
                pool.wait_ge(hyp_sub, 2 * c + 1)
                pool.nop(nofuse=True)
                pool.tensor_scalar(t2, t2, 0.5, None, ALU.mult).then_inc(hyp_sub, 1)
                pool.wait_ge(hyp_sub, 2 * c + 2)
                step(c, "fac", pool.tensor_tensor(s5, s5, t2, ALU.mult))
                pool.wait_ge(hyp_act, HA(c, "ww"))
                step(c, "wn", pool.tensor_tensor(s7, s6, half, ALU.pow))
                step(c, "wn_max", pool.tensor_scalar(s7, s7, MIN_NORM, None, ALU.max))
                step(c, "wn_inv", pool.tensor_tensor(s6, s7, minus_one, ALU.pow))
                pool.wait_ge(hyp_act, HA(c, "tanh2"))
                pool.nop(nofuse=True)
                step(c, "p2", pool.tensor_scalar(t1, t1, MAX_NORM, None, ALU.min))
                step(c, "f2", pool.tensor_tensor(s7, s6, t1, ALU.mult))
                pool.wait_ge(hyp_in, 16 * (c + 1))
                step(c, "fh", pool.tensor_tensor(tiles(msg_t), tiles(msg_t), s7.unsqueeze(2).to_broadcast([P, TPC, P]),
                                                 ALU.mult))
                pool.wait_ge(hyp_dve, HV(c, "bn"))
                rsqrt_var(c, step)

            hyperbolic(0)
            with pool.Fori(1, CHUNKS) as c:
                hyperbolic(c)


def kernel(x, adj, L0_gnn_W_msg, L0_gnn_b_msg, L0_gnn_W_ih, L0_gnn_W_hh, L0_gnn_b_ih, L0_gnn_b_hh,
           L1_gnn_weight, L1_gnn_bias, L2_gnn_Wq, L2_gnn_bq, L2_gnn_Wk, L2_gnn_bk, L2_gnn_Wv, L2_gnn_bv,
           L2_gnn_Ws, L2_gnn_bs, L2_gnn_Wb, L3_gnn_weight, L3_gnn_bias):
    import numpy as np
    import concourse.bacc as bacc
    from concourse.bass_utils import run_bass_kernel_spmd

    def a(v):
        return np.asarray(v)

    arrays = {
        "adj_cols": a(adj).reshape(CHUNKS, CHUNK, SLOTS, JPS, P).transpose(0, 2, 4, 3, 1).reshape(
            CHUNKS, SLOTS, P, JPS * CHUNK),
        "adj": a(adj),
        "x_tiles": a(x).reshape(TILES, P, P).transpose(1, 0, 2).reshape(P, TILES * P),
        "x_t": a(x).T,
        "w_msg": a(L0_gnn_W_msg).T, "b_msg": a(L0_gnn_b_msg).reshape(P, 1),
        "w_ih": a(L0_gnn_W_ih).T, "w_hh": a(L0_gnn_W_hh).T,
        "b_ih": a(L0_gnn_b_ih).reshape(3, P).T, "b_hh": a(L0_gnn_b_hh).reshape(3, P).T,
        "w_gcn": a(L1_gnn_weight), "b_gcn": a(L1_gnn_bias),
        "w_q": a(L2_gnn_Wq), "b_q": a(L2_gnn_bq).reshape(P, 1),
        "w_k": a(L2_gnn_Wk), "b_k": a(L2_gnn_bk).reshape(P, 1),
        "w_vs": np.concatenate([a(L2_gnn_Wv), a(L2_gnn_Ws)], axis=1),
        "b_vs": np.concatenate([a(L2_gnn_bv), a(L2_gnn_bs)]),
        "w_beta": a(L2_gnn_Wb).reshape(3 * P),
        "w_hyp": a(L3_gnn_weight).T, "b_hyp": a(L3_gnn_bias),
    }
    arrays = {name: np.ascontiguousarray(v) for name, v in arrays.items()}
    nc = bacc.Bacc("TRN2", target_bir_lowering=False, num_devices=1)
    args = {name: nc.dram_tensor(name, v.shape, F32, kind="ExternalInput").ap() for name, v in arrays.items()}
    out = nc.dram_tensor("out", (P, TILES * P), F32, kind="ExternalOutput").ap()
    build_program(nc, out=out, **args)
    result = run_bass_kernel_spmd(nc, [arrays], core_ids=[0])
    return result.results[0]["out"].reshape(P, TILES, P).transpose(1, 0, 2).reshape(N, P)
```
